# Optimizing a Trainium2 kernel written in Bass

```python
import numpy as np
import jax
import jax.numpy as jnp

def _softmax(x, axis=-1):
    return jax.nn.softmax(x, axis=axis)

def _gelu(x):
    return jax.nn.gelu(x, approximate=True)

def _silu(x):
    return jax.nn.silu(x)

def _sigmoid(x):
    return jax.nn.sigmoid(x)

def _layernorm(x, axis=-1, eps=1e-05):
    m = jnp.mean(x, axis=axis, keepdims=True)
    v = jnp.var(x, axis=axis, keepdims=True)
    return (x - m) / jnp.sqrt(v + eps)

def _scatter_add(tgt, idx, src, axis=0):
    return tgt.at[idx].add(src)

def _segment_sum(src, seg, n):
    return jax.ops.segment_sum(src, seg, n)
kernel_name = 'mk_conv_attn_hybrid_d4_conv_nhwc384_r4_58aba1'

def setup_inputs(seed: int=0):
    np.random.seed(seed)
    _w = jnp.asarray

    def _rec_inputs():
        import jax
        import jax.numpy as jnp
        _gk = jax.random.key(seed)
        x = -0.0004039 + 1 * jax.random.normal(jax.random.fold_in(_gk, 1), (8, 16, 16, 96), jnp.float32)
        return x
    x = _rec_inputs()

    def _L0_conv_setup():
        import jax, jax.numpy as jnp
        import numpy as np
        DIM = 96
        H = 16
        W = 16
        NB = 8
        BS = DIM // NB
        WF = W // 2 + 1
        EPS = 1e-05

        def _layernorm(x, g, b):
            mu = jnp.mean(x, axis=-1, keepdims=True)
            var = jnp.mean(jnp.square(x - mu), axis=-1, keepdims=True)
            return (x - mu) * jax.lax.rsqrt(var + EPS) * g + b
        key = jax.random.key(seed)
        ks = jax.random.split(key, 8)
        scale = 0.02
        x = jax.random.normal(ks[0], (8, H, W, DIM), dtype=jnp.float32)
        w1 = scale * jax.random.normal(ks[1], (H, WF, NB, BS, BS, 2), dtype=jnp.float32)
        b1 = scale * jax.random.normal(ks[2], (H, WF, NB, BS, 2), dtype=jnp.float32)
        norm1_w = jnp.ones((DIM,), jnp.float32)
        norm1_b = jnp.zeros((DIM,), jnp.float32)
        norm2_w = jnp.ones((DIM,), jnp.float32)
        norm2_b = jnp.zeros((DIM,), jnp.float32)
        lim1 = 1.0 / np.sqrt(DIM)
        lim2 = 1.0 / np.sqrt(4 * DIM)
        mlp_w1 = jax.random.uniform(ks[3], (DIM, 4 * DIM), jnp.float32, -lim1, lim1)
        mlp_b1 = jax.random.uniform(ks[4], (4 * DIM,), jnp.float32, -lim1, lim1)
        mlp_w2 = jax.random.uniform(ks[5], (4 * DIM, DIM), jnp.float32, -lim2, lim2)
        mlp_b2 = jax.random.uniform(ks[6], (DIM,), jnp.float32, -lim2, lim2)
        return {'x': x, 'w1': w1, 'b1': b1, 'norm1_w': norm1_w, 'norm1_b': norm1_b, 'norm2_w': norm2_w, 'norm2_b': norm2_b, 'mlp_w1': mlp_w1, 'mlp_b1': mlp_b1, 'mlp_w2': mlp_w2, 'mlp_b2': mlp_b2}
    _L0_conv_all = _L0_conv_setup()
    _L0_conv_in = {k: v for k, v in _L0_conv_all.items() if k in ('w1', 'b1', 'norm1_w', 'norm1_b', 'norm2_w', 'norm2_b', 'mlp_w1', 'mlp_b1', 'mlp_w2', 'mlp_b2')}
    del _L0_conv_all

    def _L1_conv_setup():
        import jax, jax.numpy as jnp
        import numpy as np
        DECAY = 0.6
        GAIN = 0.4

        def _layernorm(x, g, b, eps=1e-05):
            m = x.mean(-1, keepdims=True)
            v = x.var(-1, keepdims=True)
            return (x - m) * jax.lax.rsqrt(v + eps) * g + b

        def _ema_scan(x, axis, reverse=False):
            a = jnp.full_like(x, DECAY)
            b = GAIN * x

            def comb(c1, c2):
                a1, b1 = c1
                a2, b2 = c2
                return (a1 * a2, a2 * b1 + b2)
            _, y = jax.lax.associative_scan(comb, (a, b), axis=axis, reverse=reverse)
            return y
        key = jax.random.key(seed)
        B, H, W, D = (16, 16, 16, 96)
        inner = 2 * D
        hidden = 4 * D
        ks = jax.random.split(key, 12)
        s = 0.02
        return {'x': jax.random.normal(ks[0], (B, H, W, D), jnp.float32), 'n1_g': jnp.ones((D,), jnp.float32), 'n1_b': jnp.zeros((D,), jnp.float32), 'w_in': s * jax.random.normal(ks[1], (D, inner), jnp.float32), 'b_in': jnp.zeros((inner,), jnp.float32), 'k_conv': s * jax.random.normal(ks[2], (3, 3, 1, inner), jnp.float32), 'on_g': jnp.ones((inner,), jnp.float32), 'on_b': jnp.zeros((inner,), jnp.float32), 'w_out': s * jax.random.normal(ks[3], (inner, D), jnp.float32), 'b_out': jnp.zeros((D,), jnp.float32), 'n2_g': jnp.ones((D,), jnp.float32), 'n2_b': jnp.zeros((D,), jnp.float32), 'w1': s * jax.random.normal(ks[4], (D, hidden), jnp.float32), 'b1': jnp.zeros((hidden,), jnp.float32), 'w2': s * jax.random.normal(ks[5], (hidden, D), jnp.float32), 'b2': jnp.zeros((D,), jnp.float32)}
    _L1_conv_all = _L1_conv_setup()
    _L1_conv_in = {k: v for k, v in _L1_conv_all.items() if k in ('n1_g', 'n1_b', 'w_in', 'b_in', 'k_conv', 'on_g', 'on_b', 'w_out', 'b_out', 'n2_g', 'n2_b', 'w1', 'b1', 'w2', 'b2')}
    del _L1_conv_all

    def _L2_attn_setup():
        import jax, jax.numpy as jnp
        import numpy as np
        import math
        B, T, N_EMBD, N_HEAD = (4, 1024, 96, 6)
        HEAD_DIM = N_EMBD // N_HEAD
        key = jax.random.key(seed)
        k1, k2, k3 = jax.random.split(key, 3)
        x = jax.random.normal(k1, (B, T, N_EMBD), dtype=jnp.float32)
        w_attn = jax.random.normal(k2, (N_EMBD, 3 * N_EMBD), dtype=jnp.float32) * 0.02
        w_proj = jax.random.normal(k3, (N_EMBD, N_EMBD), dtype=jnp.float32) * 0.02
        return {'x': x, 'w_attn': w_attn, 'w_proj': w_proj}
    _L2_attn_all = _L2_attn_setup()
    _L2_attn_in = {k: v for k, v in _L2_attn_all.items() if k in ('w_attn', 'w_proj')}
    del _L2_attn_all

    def _L2_ffn_setup():
        import jax, jax.numpy as jnp
        import numpy as np
        NUM_GROUPS = 5
        EPS = 1e-05
        QB = 128.0

        def _binarize_weights_groupwise(W):
            n_out = W.shape[0]
            gs = n_out // NUM_GROUPS
            Wb = jnp.zeros_like(W)
            for g in range(NUM_GROUPS):
                wg = W[g * gs:(g + 1) * gs]
                z = wg - wg.mean()
                ste = z + jax.lax.stop_gradient(jnp.sign(z) - z)
                Wb = Wb.at[g * gs:(g + 1) * gs].set(ste)
            return Wb

        def _quantize_activations_groupwise(x):
            n = x.shape[0]
            gs = n // NUM_GROUPS
            xq = jnp.zeros_like(x)
            for g in range(NUM_GROUPS):
                ag = x[g * gs:(g + 1) * gs]
                gamma = jnp.max(jnp.abs(ag))
                xq = xq.at[g * gs:(g + 1) * gs].set(jnp.clip(ag * QB / (gamma + EPS), -QB + EPS, QB - EPS))
            return xq

        def _bitlinear(x, W, b):
            Wb = _binarize_weights_groupwise(W)
            y = jnp.einsum('btc,oc->bto', x, Wb) + b
            return _quantize_activations_groupwise(y)
        key = jax.random.key(seed)
        k1, k2, k3, k4, k5 = jax.random.split(key, 5)
        B, T, C = (10, 512, 96)
        H = 4 * C
        lim1 = 1.0 / np.sqrt(C)
        lim2 = 1.0 / np.sqrt(H)
        x = jax.random.normal(k1, (B, T, C), dtype=jnp.float32)
        W1 = jax.random.uniform(k2, (H, C), minval=-lim1, maxval=lim1, dtype=jnp.float32)
        b1 = jax.random.uniform(k3, (H,), minval=-lim1, maxval=lim1, dtype=jnp.float32)
        W2 = jax.random.uniform(k4, (C, H), minval=-lim2, maxval=lim2, dtype=jnp.float32)
        b2 = jax.random.uniform(k5, (C,), minval=-lim2, maxval=lim2, dtype=jnp.float32)
        return {'x': x, 'W1': W1, 'b1': b1, 'W2': W2, 'b2': b2}
    _L2_ffn_all = _L2_ffn_setup()
    _L2_ffn_in = {k: v for k, v in _L2_ffn_all.items() if k in ('W1', 'b1', 'W2', 'b2')}
    del _L2_ffn_all

    def _L3_attn_setup():
        import jax, jax.numpy as jnp
        import numpy as np
        NUM_HEADS = 6
        HEAD_SIZE = 16
        N_EMBD = 96
        key = jax.random.key(seed)
        k1, k2, k3 = jax.random.split(key, 3)
        B, T, C = (64, 64, N_EMBD)
        x = jax.random.normal(k1, (B, T, C), dtype=jnp.float32)
        W_qkv = jax.random.normal(k2, (C, 3 * C), dtype=jnp.float32) * (1.0 / np.sqrt(C))
        W_proj = jax.random.normal(k3, (C, C), dtype=jnp.float32) * (1.0 / np.sqrt(C))
        b_proj = jnp.zeros((C,), dtype=jnp.float32)
        return {'x': x, 'W_qkv': W_qkv, 'W_proj': W_proj, 'b_proj': b_proj}
    _L3_attn_all = _L3_attn_setup()
    _L3_attn_in = {k: v for k, v in _L3_attn_all.items() if k in ('W_qkv', 'W_proj', 'b_proj')}
    del _L3_attn_all

    def _L3_ffn_setup():
        import jax, jax.numpy as jnp
        import numpy as np
        NUM_EXPERTS = 4
        TOP_K = 2
        DIM = 96
        HID = 4 * DIM
        key = jax.random.key(seed)
        ks = jax.random.split(key, 5)
        B, S = (16, 512)
        scale_in = 1.0 / np.sqrt(DIM)
        scale_hid = 1.0 / np.sqrt(HID)
        return {'x': jax.random.normal(ks[0], (B, S, DIM), dtype=jnp.float32), 'gate_w': jax.random.normal(ks[1], (DIM, NUM_EXPERTS), dtype=jnp.float32) * scale_in, 'gate_b': jnp.zeros((NUM_EXPERTS,), dtype=jnp.float32), 'w1': jax.random.normal(ks[2], (NUM_EXPERTS, DIM, HID), dtype=jnp.float32) * scale_in, 'b1': jnp.zeros((NUM_EXPERTS, HID), dtype=jnp.float32), 'w2': jax.random.normal(ks[3], (NUM_EXPERTS, HID, DIM), dtype=jnp.float32) * scale_hid, 'b2': jnp.zeros((NUM_EXPERTS, DIM), dtype=jnp.float32)}
    _L3_ffn_all = _L3_ffn_setup()
    _L3_ffn_in = {k: v for k, v in _L3_ffn_all.items() if k in ('gate_w', 'gate_b', 'w1', 'b1', 'w2', 'b2')}
    del _L3_ffn_all
    return {'x': x, 'L0_conv_w1': _L0_conv_in['w1'], 'L0_conv_b1': _L0_conv_in['b1'], 'L0_conv_norm1_w': _L0_conv_in['norm1_w'], 'L0_conv_norm1_b': _L0_conv_in['norm1_b'], 'L0_conv_norm2_w': _L0_conv_in['norm2_w'], 'L0_conv_norm2_b': _L0_conv_in['norm2_b'], 'L0_conv_mlp_w1': _L0_conv_in['mlp_w1'], 'L0_conv_mlp_b1': _L0_conv_in['mlp_b1'], 'L0_conv_mlp_w2': _L0_conv_in['mlp_w2'], 'L0_conv_mlp_b2': _L0_conv_in['mlp_b2'], 'L1_conv_n1_g': _L1_conv_in['n1_g'], 'L1_conv_n1_b': _L1_conv_in['n1_b'], 'L1_conv_w_in': _L1_conv_in['w_in'], 'L1_conv_b_in': _L1_conv_in['b_in'], 'L1_conv_k_conv': _L1_conv_in['k_conv'], 'L1_conv_on_g': _L1_conv_in['on_g'], 'L1_conv_on_b': _L1_conv_in['on_b'], 'L1_conv_w_out': _L1_conv_in['w_out'], 'L1_conv_b_out': _L1_conv_in['b_out'], 'L1_conv_n2_g': _L1_conv_in['n2_g'], 'L1_conv_n2_b': _L1_conv_in['n2_b'], 'L1_conv_w1': _L1_conv_in['w1'], 'L1_conv_b1': _L1_conv_in['b1'], 'L1_conv_w2': _L1_conv_in['w2'], 'L1_conv_b2': _L1_conv_in['b2'], 'L2_attn_w_attn': _L2_attn_in['w_attn'], 'L2_attn_w_proj': _L2_attn_in['w_proj'], 'L2_ffn_W1': _L2_ffn_in['W1'], 'L2_ffn_b1': _L2_ffn_in['b1'], 'L2_ffn_W2': _L2_ffn_in['W2'], 'L2_ffn_b2': _L2_ffn_in['b2'], 'L3_attn_W_qkv': _L3_attn_in['W_qkv'], 'L3_attn_W_proj': _L3_attn_in['W_proj'], 'L3_attn_b_proj': _L3_attn_in['b_proj'], 'L3_ffn_gate_w': _L3_ffn_in['gate_w'], 'L3_ffn_gate_b': _L3_ffn_in['gate_b'], 'L3_ffn_w1': _L3_ffn_in['w1'], 'L3_ffn_b1': _L3_ffn_in['b1'], 'L3_ffn_w2': _L3_ffn_in['w2'], 'L3_ffn_b2': _L3_ffn_in['b2']}

def reference(x, L0_conv_w1, L0_conv_b1, L0_conv_norm1_w, L0_conv_norm1_b, L0_conv_norm2_w, L0_conv_norm2_b, L0_conv_mlp_w1, L0_conv_mlp_b1, L0_conv_mlp_w2, L0_conv_mlp_b2, L1_conv_n1_g, L1_conv_n1_b, L1_conv_w_in, L1_conv_b_in, L1_conv_k_conv, L1_conv_on_g, L1_conv_on_b, L1_conv_w_out, L1_conv_b_out, L1_conv_n2_g, L1_conv_n2_b, L1_conv_w1, L1_conv_b1, L1_conv_w2, L1_conv_b2, L2_attn_w_attn, L2_attn_w_proj, L2_ffn_W1, L2_ffn_b1, L2_ffn_W2, L2_ffn_b2, L3_attn_W_qkv, L3_attn_W_proj, L3_attn_b_proj, L3_ffn_gate_w, L3_ffn_gate_b, L3_ffn_w1, L3_ffn_b1, L3_ffn_w2, L3_ffn_b2):
    import jax
    import jax.numpy as jnp

    def _L0_conv_ref(x, w1, b1, norm1_w, norm1_b, norm2_w, norm2_b, mlp_w1, mlp_b1, mlp_w2, mlp_b2):
        import jax, jax.numpy as jnp
        import numpy as np
        DIM = 96
        H = 16
        W = 16
        NB = 8
        BS = DIM // NB
        WF = W // 2 + 1
        EPS = 1e-05

        def _layernorm(x, g, b):
            mu = jnp.mean(x, axis=-1, keepdims=True)
            var = jnp.mean(jnp.square(x - mu), axis=-1, keepdims=True)
            return (x - mu) * jax.lax.rsqrt(var + EPS) * g + b
        B, h, w, C = x.shape
        residual = x
        xn = _layernorm(x, norm1_w, norm1_b)
        xf = jnp.fft.rfft2(xn.astype(jnp.float32), axes=(1, 2), norm='ortho')
        xf = xf.reshape(B, h, w // 2 + 1, NB, BS)
        w1c = jax.lax.complex(w1[..., 0], w1[..., 1])
        b1c = jax.lax.complex(b1[..., 0], b1[..., 1])
        o1 = jnp.einsum('bhwni,hwnio->bhwno', xf, w1c) + b1c
        o1 = jax.lax.complex(jax.nn.relu(o1.real), jax.nn.relu(o1.imag))
        o1 = o1.reshape(B, h, w // 2 + 1, C)
        xs = jnp.fft.irfft2(o1, s=(h, w), axes=(1, 2), norm='ortho')
        xm = _layernorm(xs, norm2_w, norm2_b)
        hdn = jax.nn.gelu(xm @ mlp_w1 + mlp_b1, approximate=False)
        mlp_out = hdn @ mlp_w2 + mlp_b2
        return xs + residual + mlp_out

    def _L1_conv_ref(x, n1_g, n1_b, w_in, b_in, k_conv, on_g, on_b, w_out, b_out, n2_g, n2_b, w1, b1, w2, b2):
        import jax, jax.numpy as jnp
        import numpy as np
        DECAY = 0.6
        GAIN = 0.4

        def _layernorm(x, g, b, eps=1e-05):
            m = x.mean(-1, keepdims=True)
            v = x.var(-1, keepdims=True)
            return (x - m) * jax.lax.rsqrt(v + eps) * g + b

        def _ema_scan(x, axis, reverse=False):
            a = jnp.full_like(x, DECAY)
            b = GAIN * x

            def comb(c1, c2):
                a1, b1 = c1
                a2, b2 = c2
                return (a1 * a2, a2 * b1 + b2)
            _, y = jax.lax.associative_scan(comb, (a, b), axis=axis, reverse=reverse)
            return y
        inner = w_in.shape[1]
        h = _layernorm(x, n1_g, n1_b)
        p = h @ w_in + b_in
        local = jax.lax.conv_general_dilated(p, k_conv, window_strides=(1, 1), padding='SAME', dimension_numbers=('NHWC', 'HWIO', 'NHWC'), feature_group_count=inner)
        lr = _ema_scan(local, axis=2)
        rl = _ema_scan(local, axis=2, reverse=True)
        tb = _ema_scan(local, axis=1)
        bt = _ema_scan(local, axis=1, reverse=True)
        mixed = 0.25 * (lr + rl + tb + bt) + local
        mixed = _layernorm(mixed, on_g, on_b)
        x = x + (mixed @ w_out + b_out)
        h2 = _layernorm(x, n2_g, n2_b)
        m = jax.nn.gelu(h2 @ w1 + b1, approximate=False) @ w2 + b2
        return x + m

    def _L2_attn_ref(x, w_attn, w_proj):
        import jax, jax.numpy as jnp
        import numpy as np
        import math
        B, T, N_EMBD, N_HEAD = (4, 1024, 96, 6)
        HEAD_DIM = N_EMBD // N_HEAD
        b, t, c = x.shape
        qkv = x @ w_attn
        q, k, v = jnp.split(qkv, 3, axis=-1)
        q = q.reshape(b, t, N_HEAD, HEAD_DIM)
        k = k.reshape(b, t, N_HEAD, HEAD_DIM)
        v = v.reshape(b, t, N_HEAD, HEAD_DIM)
        scale = 1.0 / math.sqrt(HEAD_DIM)
        att = jnp.einsum('bqhd,bkhd->bhqk', q, k) * scale
        causal = jnp.tril(jnp.ones((t, t), dtype=bool))
        att = jnp.where(causal[None, None], att, jnp.finfo(att.dtype).min)
        att = jax.nn.softmax(att, axis=-1)
        out = jnp.einsum('bhqk,bkhd->bqhd', att, v).reshape(b, t, c)
        return out @ w_proj

    def _L2_ffn_ref(x, W1, b1, W2, b2):
        import jax, jax.numpy as jnp
        import numpy as np
        NUM_GROUPS = 5
        EPS = 1e-05
        QB = 128.0

        def _binarize_weights_groupwise(W):
            n_out = W.shape[0]
            gs = n_out // NUM_GROUPS
            Wb = jnp.zeros_like(W)
            for g in range(NUM_GROUPS):
                wg = W[g * gs:(g + 1) * gs]
                z = wg - wg.mean()
                ste = z + jax.lax.stop_gradient(jnp.sign(z) - z)
                Wb = Wb.at[g * gs:(g + 1) * gs].set(ste)
            return Wb

        def _quantize_activations_groupwise(x):
            n = x.shape[0]
            gs = n // NUM_GROUPS
            xq = jnp.zeros_like(x)
            for g in range(NUM_GROUPS):
                ag = x[g * gs:(g + 1) * gs]
                gamma = jnp.max(jnp.abs(ag))
                xq = xq.at[g * gs:(g + 1) * gs].set(jnp.clip(ag * QB / (gamma + EPS), -QB + EPS, QB - EPS))
            return xq

        def _bitlinear(x, W, b):
            Wb = _binarize_weights_groupwise(W)
            y = jnp.einsum('btc,oc->bto', x, Wb) + b
            return _quantize_activations_groupwise(y)
        h = _bitlinear(x, W1, b1)
        h = jax.nn.gelu(h, approximate=False)
        out = _bitlinear(h, W2, b2)
        return out

    def _L3_attn_ref(x, W_qkv, W_proj, b_proj):
        import jax, jax.numpy as jnp
        import numpy as np
        NUM_HEADS = 6
        HEAD_SIZE = 16
        N_EMBD = 96
        B, T, C = x.shape
        H, D = (NUM_HEADS, HEAD_SIZE)
        qkv = x @ W_qkv
        q, k, v = jnp.split(qkv, 3, axis=-1)
        q = q.reshape(B, T, H, D).transpose(0, 2, 1, 3)
        k = k.reshape(B, T, H, D).transpose(0, 2, 1, 3)
        v = v.reshape(B, T, H, D).transpose(0, 2, 1, 3)
        att = jnp.einsum('bhtd,bhsd->bhts', q, k) / np.sqrt(D).astype(jnp.float32)
        causal = jnp.tril(jnp.ones((T, T), dtype=bool))
        att = jnp.where(causal[None, None], att, -jnp.inf)
        att = jax.nn.softmax(att, axis=-1)
        out = jnp.einsum('bhts,bhsd->bhtd', att, v)
        out = out.transpose(0, 2, 1, 3).reshape(B, T, C)
        return out @ W_proj.T @ jnp.eye(C, dtype=out.dtype) if False else out @ W_proj + b_proj

    def _L3_ffn_ref(x, gate_w, gate_b, w1, b1, w2, b2):
        import jax, jax.numpy as jnp
        import numpy as np
        NUM_EXPERTS = 4
        TOP_K = 2
        DIM = 96
        HID = 4 * DIM
        scores = jnp.einsum('bsd,de->bse', x, gate_w) + gate_b
        probs = jax.nn.softmax(scores, axis=-1)
        topk_vals, topk_idx = jax.lax.top_k(probs, TOP_K)
        mask = jnp.sum(jax.nn.one_hot(topk_idx, NUM_EXPERTS, dtype=probs.dtype), axis=-2)
        masked = probs * mask
        masked = masked / (jnp.sum(masked, axis=-1, keepdims=True) + 1e-09)
        h = jax.nn.gelu(jnp.einsum('bsd,edh->ebsh', x, w1) + b1[:, None, None, :], approximate=False)
        y = jnp.einsum('ebsh,ehd->ebsd', h, w2) + b2[:, None, None, :]
        out = jnp.einsum('bse,ebsd->bsd', masked, y)
        return out

    def _gn(v, G=32, eps=1e-05):
        B_, H_, W_, C_ = v.shape
        g = v.reshape(B_, H_, W_, G, C_ // G)
        m = jnp.mean(g, axis=(1, 2, 4), keepdims=True)
        s = jnp.var(g, axis=(1, 2, 4), keepdims=True)
        return ((g - m) / jnp.sqrt(s + eps)).reshape(v.shape)

    def _ln_c(v, eps=1e-06):
        m = jnp.mean(v, axis=-1, keepdims=True)
        s = jnp.var(v, axis=-1, keepdims=True)
        return (v - m) / jnp.sqrt(s + eps)

    def _ln_t(v, eps=1e-05):
        m = jnp.mean(v, axis=-1, keepdims=True)
        s = jnp.var(v, axis=-1, keepdims=True)
        return (v - m) / jnp.sqrt(s + eps)

    def _to_tokens(v):
        B_, H_, W_, C_ = v.shape
        return v.reshape(B_, H_ * W_, C_)

    def _from_tokens(t, like):
        return t.reshape(like.shape)
    x = _L0_conv_ref(x, L0_conv_w1, L0_conv_b1, L0_conv_norm1_w, L0_conv_norm1_b, L0_conv_norm2_w, L0_conv_norm2_b, L0_conv_mlp_w1, L0_conv_mlp_b1, L0_conv_mlp_w2, L0_conv_mlp_b2)
    x = _L1_conv_ref(x, L1_conv_n1_g, L1_conv_n1_b, L1_conv_w_in, L1_conv_b_in, L1_conv_k_conv, L1_conv_on_g, L1_conv_on_b, L1_conv_w_out, L1_conv_b_out, L1_conv_n2_g, L1_conv_n2_b, L1_conv_w1, L1_conv_b1, L1_conv_w2, L1_conv_b2)
    t = _to_tokens(x)
    t = t + _L2_attn_ref(_ln_t(t), L2_attn_w_attn, L2_attn_w_proj)
    t = t + _L2_ffn_ref(_ln_t(t), L2_ffn_W1, L2_ffn_b1, L2_ffn_W2, L2_ffn_b2)
    t = t + _L3_attn_ref(_ln_t(t), L3_attn_W_qkv, L3_attn_W_proj, L3_attn_b_proj)
    t = t + _L3_ffn_ref(_ln_t(t), L3_ffn_gate_w, L3_ffn_gate_b, L3_ffn_w1, L3_ffn_b1, L3_ffn_w2, L3_ffn_b2)
    x = _from_tokens(t, x)
    return x

_drawn_inputs = setup_inputs


def setup_inputs(seed=0):
    import zlib

    import numpy as np

    out = dict(_drawn_inputs(seed))
    spreads = {'L0_conv_norm1_w': (1.0, 0.2),
     'L0_conv_norm1_b': (0.0, 0.51),
     'L0_conv_norm2_w': (1.0, 0.2),
     'L0_conv_norm2_b': (0.0, 0.387),
     'L1_conv_n1_g': (1.0, 0.2),
     'L1_conv_n1_b': (0.0, 0.301),
     'L1_conv_b_in': (0.0, 0.1),
     'L1_conv_on_g': (1.0, 0.2),
     'L1_conv_on_b': (0.0, 0.346),
     'L1_conv_b_out': (0.0, 0.1),
     'L1_conv_n2_g': (1.0, 0.6),
     'L1_conv_n2_b': (0.0, 0.8),
     'L1_conv_b1': (0.0, 0.449),
     'L1_conv_b2': (0.0, 0.1),
     'L3_attn_b_proj': (0.0, 0.8),
     'L3_ffn_gate_b': (0.0, 0.8),
     'L3_ffn_b1': (0.0, 0.8),
     'L3_ffn_b2': (0.0, 2.0)}
    factors = {'L0_conv_mlp_b1': 2.96,
     'L2_attn_w_attn': 5.475,
     'L2_attn_w_proj': 5.833,
     'L2_ffn_b1': 8.0,
     'L2_ffn_b2': 200.0,
     'L3_ffn_gate_w': 3.168,
     'L3_ffn_w1': 3.162,
     'L3_ffn_w2': 2.73}
    for name, (base, spread) in spreads.items():
        noise = np.random.default_rng([zlib.crc32(name.encode()), seed]).standard_normal(out[name].shape)
        drawn = base * np.exp(spread * noise) if base else spread * noise
        out[name] = jnp.asarray(drawn.astype(out[name].dtype))
    for name, factor in factors.items():
        out[name] = (out[name] * factor).astype(out[name].dtype)
    return out
```

```python
from contextlib import ExitStack

import numpy as np

import concourse.bass as bass
from concourse import mybir

F32 = mybir.dt.float32
BF16 = mybir.dt.bfloat16
ALU = mybir.AluOpType
ACT = mybir.ActivationFunctionType
AX = mybir.AxisListType

B, HH, WW, C = 8, 16, 16, 96
P = 128
TOK = HH * WW
HALVES = TOK // P
TILES = B * HALVES
IMGS = 2
CT = IMGS * HALVES
CN = IMGS * TOK
CHUNKS = B // IMGS
HID = 4 * C
HT = HID // P
WF = WW // 2 + 1
POS = HH * WF
NB, BS = 8, C // 8
GB = NB // 2
GR = GB * BS
BINS = 2 * BS
PPB = 512 // BINS
SBANKS = -(-POS // PPB)
KT = 3
KP = POS // KT
KROWS = 2 * KP
OH = BS // 2
INNER = 2 * C
IN2 = INNER - P
PW = WW + 1
IMG = PW * (HH + 1)
LEAD = PW + 1
TAPS = [(dy, dx) for dy in (-1, 0, 1) for dx in (-1, 0, 1)]
PE_TAPS = 4
UNITS = ["m0", "m1", "s0", "m2", "m3", "s1"]
NH, HD = 6, 16
HEAD_GROUPS = ((0, 1, 2, 3), (4, 5))
ITEMS = [(im, h) for heads in HEAD_GROUPS for im in range(IMGS) for h in heads]
NI = len(ITEMS)
NEG = -1e30
QG = 5
G1, G2 = HID // QG, C // QG
QB, QEPS = 128.0, 1e-5
QIMGS = QG * (B // QG)
NE = 4
LN_EPS = 1e-5
L0A, L0B, L1A, L1M, L1B, A2, F2, A3, MO = range(9)
X_OF = {L1A: 0, L1B: 1, A2: 2, F2: 3, A3: 4, MO: 5}

CONST_A = {"ident": 128, "nmask": 4, "delta": GB * B, "dft": HALVES * 2 * POS}
CONST_B = {"mask": 384, "sumsel": 128, "rank": 32, "idft": KT * TOK, "mix": HALVES * TOK}


def spots(widths):
    at, out = 0, {}
    for name, w in widths.items():
        out[name] = (at, at + w)
        at += w
    return out, at


def chunks_of(l):
    if l == F2:
        return [(c, min(CT, HALVES * QIMGS - CT * c)) for c in range(CHUNKS) if CT * c < HALVES * QIMGS]
    return [(c, CT) for c in range(CHUNKS)]


LN_SEQ = [(l, c) for l in (L0A, L0B, L1A) for c in range(CHUNKS)]
LN_SEQ += [(l, c) for pair in ((0, 1), (2, 3)) for l in (L1M, L1B) for c in pair]
LN_SEQ += [(l, c) for l in (A2, F2, A3, MO) for c, _ in chunks_of(l)]
LN_NO = {k: n + 1 for n, k in enumerate(LN_SEQ)}
T_SEQ = [k for k in LN_SEQ if k[0] not in (L0A, L1M)]


def attention_steps():
    hooks = {}
    for c in range(CHUNKS):
        if c:
            hooks.setdefault(NI * c - 6, []).append(("qkv", c))
        hooks.setdefault(NI * c + 11, []).append(("sum0", c))
        hooks.setdefault(NI * c + 15, []).append(("sum1", c))
        hooks.setdefault(NI * c + 16, []).append(("proj", c))
        hooks.setdefault(NI * c + 17, []).append(("back", c))
        hooks.setdefault(NI * c + 19, []).append(("turn", c))
    return [(s, hooks.get(s, [])) for s in range(NI * CHUNKS + 8)]


def plan_banks():
    seq = []

    def use(bank, *key):
        seq.append((key, bank))

    def turn(l, c):
        use(c % 2, "turn", l, c)

    def mlp(m, l, nxt):
        for s in range(CHUNKS + 3):
            if s < CHUNKS:
                for k in range(HT):
                    use(2 + k, "up", m, s, k)
            if 1 <= s <= CHUNKS:
                use(5, "down", m, s - 1)
            if 2 <= s <= CHUNKS + 1:
                use(6, "back", l, s - 2)
            if s >= 3:
                turn(nxt, s - 3)

    for b in range(B):
        use(b, "dft", b)
    for k in range(SBANKS):
        use(k, "spec", k)
    for k in range(KT):
        for j in range(2):
            use((7, 0, 1, 2, 3, 4)[2 * k + j], "spec_t", k, j)
    for k in range(HALVES * 2):
        use((5, 6, 7, 0)[k], "inv", k)
    use(1, "signprep", 0)
    use(2, "signprep", 1)
    for c in range(CHUNKS):
        turn(L0B, c)
    use(3, "signprep", 2)
    use(4, "signprep", 3)
    mlp(0, L0B, L1A)
    def win(c):
        use(2 + c % 2, "win", c, 0)
        use(4 + c % 2, "win", c, 1)

    def taps(u):
        for im in range(IMGS):
            use(6 + im, "taps", u, im)

    for w in conv_order():
        if w[0] == "win":
            win(w[1])
        elif w[0] == "taps":
            taps(w[1])
        elif w[0] == "loc":
            use(1, "loc", w[1])
        elif w[0] == "mix":
            for ho in range(HALVES):
                use(2 + ho, "mix", w[1], ho)
        elif w[0] == "turn_m":
            use(4, "turn_m", w[1], 0)
            use(5, "turn_m", w[1], 1)
        elif w[0] == "wout":
            use(0, "wout", w[1])
        elif w[0] == "back":
            use(1, "back", L1A, w[1])
        elif w[0] == "turn":
            use(0, "turn", L1B, w[1])
    mlp(1, L1B, A2)

    def attention(a, l, nxt):
        def qkv(c):
            for k in range(3):
                use(7, "qk", a, c, k)
            use(7, "v", a, c)
        qkv(0)
        for s, hooks in attention_steps():
            if s < NI * CHUNKS:
                use(s % 3, "s", a, s)
            if 0 <= s - 2 < NI * CHUNKS:
                use(3 + s % 2, "pt", a, s - 2)
            i = s - 3
            if 0 <= i < NI * CHUNKS:
                if i % NI == 0:
                    use(5, "o", a, i // NI, 0)
                if i % NI == IMGS * len(HEAD_GROUPS[0]):
                    use(6, "o", a, i // NI, 1)
            for what, c in hooks:
                if what == "qkv":
                    qkv(c)
                if what in ("sum0", "sum1"):
                    use(7, "sum", a, c, int(what[-1]))
                if what == "proj":
                    use(7, "proj", a, c)
                if what == "back":
                    use(7, "back", l, c)
                if what == "turn" and (nxt, c) in T_SEQ:
                    use(7, "turn", nxt, c)

    attention(0, A2, F2)
    for c, _ in chunks_of(F2):
        for k in range(HT):
            use(k + 3 * (c % 2), "qup", c, k)
    for k in range(2):
        use(6 + k, "gamma", 0, k)
    for c, _ in chunks_of(F2):
        use(c, "qdown", c)
    for k in range(2):
        use(6 + k, "gamma", 1, k)
    for c, _ in chunks_of(F2):
        use(3 + c, "back", F2, c)
    for c in range(CHUNKS):
        use(6 + c % 2, "turn", A3, c)
    attention(1, A3, MO)
    for s in range(NE * CHUNKS + 2):
        if s < NE * CHUNKS:
            for k in range(HT):
                use(k, "eup", s, k)
        if s == 0:
            use(6, "gate")
        if 0 <= s - 1 < NE * CHUNKS:
            use(3 + (s - 1) % 2, "edown", s - 1)
        if s >= 2:
            use(5 + 2 * (s % 2), "eback", s - 2)
    out, count = {}, [0] * 8
    for key, bank in seq:
        assert key not in out, key
        out[key] = (bank, count[bank])
        count[bank] += 1
    return out


def conv_order():
    return [("win", 0), ("win", 1), ("taps", "m0"), ("taps", "m1"), ("loc", "m0"), ("win", 2), ("taps", "s0"),
            ("loc", "m1"), ("win", 3), ("taps", "m2"), ("loc", "s0"), ("mix", 0), ("taps", "m3"), ("mix", 1),
            ("turn_m", 0), ("taps", "s1"), ("wout", 0), ("turn_m", 1), ("loc", "m2"), ("back", 0), ("wout", 1),
            ("loc", "m3"), ("back", 1), ("turn", 0), ("loc", "s1"), ("mix", 2), ("turn", 1), ("mix", 3),
            ("turn_m", 2), ("wout", 2), ("turn_m", 3), ("back", 2), ("wout", 3), ("turn", 2), ("back", 3),
            ("turn", 3)]


def hybrid_kernel(nc, a, out):
    uses = plan_banks()
    ctx = ExitStack()
    with ctx:
        def sb(name, shape, dt=F32):
            return ctx.enter_context(nc.sbuf_tensor(name, shape, dt))

        def sem(name):
            return ctx.enter_context(nc.semaphore(name))

        bank = [ctx.enter_context(nc.psum_tensor(f"bank{i}", [P, 512], F32)) for i in range(8)]

        at_a, wa = spots(CONST_A)
        at_b, wb = spots(CONST_B)
        const_a, const_b = sb("const_a", [P, wa]), sb("const_b", [P, wb])
        ca = lambda n: const_a[:, at_a[n][0]:at_a[n][1]]
        cb = lambda n: const_b[:, at_b[n][0]:at_b[n][1]]
        ident = ca("ident")
        nmask, delta = ca("nmask"), ca("delta")
        dft = ca("dft").rearrange("p (h n) -> p h n", h=HALVES)
        sumsel = cb("sumsel")
        idft = cb("idft").rearrange("p (k t) -> p k t", k=KT)
        mix = cb("mix").rearrange("p (h t) -> p h t", h=HALVES)
        ident_b, mask_b = sb("ident_b", [P, P], BF16), sb("mask_b", [P, 384], BF16)
        ones = sb("ones", [P, P])

        n1g, n1b, n1b16 = sb("n1g", [P, 1]), sb("n1b", [P, 1]), sb("n1b16", [P, 1])
        affine = {l: (sb(f"g{l}", [C, 1]), sb(f"b{l}", [C, 1])) for l in (L0B, L1A, L1B)}
        mlp_w1 = [sb(f"mlp_w1_{m}", [C, HID]) for m in range(2)]
        mlp_b1 = [sb(f"mlp_b1_{m}", [P, HT]) for m in range(2)]
        mlp_w2 = [sb(f"mlp_w2_{m}", [P, HT, C]) for m in range(2)]
        mlp_b2 = [sb(f"mlp_b2_{m}", [C, 1]) for m in range(2)]
        w_in = sb("w_in", [C, INNER])
        b_in = [sb("b_in0", [P, 1]), sb("b_in1", [IN2, 1])]
        kcol = [sb("kcol0", [P, 9]), sb("kcol1", [P, 9])]
        on_g = [sb("on_g0", [P, 1]), sb("on_g1", [IN2, 1])]
        on_b = [sb("on_b0", [P, 1]), sb("on_b1", [IN2, 1])]
        w_out = [sb("w_out0", [P, C]), sb("w_out1", [IN2, C])]
        b_out = sb("b_out", [C, 1])
        tap_diag = sb("tap_diag", [P, 2, PE_TAPS, P])
        w_qkv = [sb(f"w_qkv{i}", [C, 3 * C]) for i in range(2)]
        w_heads = [sb(f"w_heads{i}", [C, 3, P]) for i in range(2)]
        w_proj = [[sb(f"w_proj{i}{g}", [32 * len(h), C]) for g, h in enumerate(HEAD_GROUPS)] for i in range(2)]
        b_proj = sb("b_proj", [C, 1])
        qw1, qw2 = sb("qw1", [P, HT, C]), sb("qw2", [C, HID])
        qb1, qb2 = sb("qb1", [P, HT]), sb("qb2", [C, 1])
        qw1_t, qw2_t = sb("qw1_t", [C, HID]), sb("qw2_t", [P, HT, C])
        sign1, sign2 = sb("sign1", [C, HID]), sb("sign2", [P, HT, C])
        qsum, qmean = sb("qsum", [P, 2, QG]), sb("qmean", [P, 2, QG])
        gate_w, gate_b = sb("gate_w", [C, NE]), sb("gate_b", [P, NE])
        e_w1, e_w2 = sb("e_w1", [C, NE, HID]), sb("e_w2", [P, NE, HT, C])
        e_b1, e_b2 = sb("e_b1", [P, NE, HT]), sb("e_b2", [C, NE])

        X = sb("X", [P, TILES, C])
        stats, moments = sb("stats", [P, 9, TILES, 6]), sb("moments", [P, 9, TILES, 2])
        rstd, exponent = sb("rstd", [P, 9, TILES]), sb("exponent", [P, CT])
        normed = [sb(f"normed{i}", [P, TILES, C]) for i in range(2)]
        normed_t = [sb(f"normed_t{i}", [C, B * TOK]) for i in range(2)]
        y_t = sb("y_t", [C, 2, CN])
        hidden = sb("hidden", [P, 2, HT, CN])
        normed_s = hidden[:, :, :, :].rearrange("p a k n -> p (a k n)")[:, 0:TILES * P].rearrange(
            "p (t c) -> p t c", c=P)
        arena = sb("arena", [P, 24600])

        class Arena:
            def __init__(self):
                self.at = 0

            def __call__(self, shape, rows=P):
                n = int(np.prod(shape))
                assert self.at + n <= 24600, self.at + n
                v = arena[0:rows, self.at:self.at + n]
                self.at += n
                if len(shape) == 1:
                    return v
                names = "abcdef"[:len(shape)]
                return v.rearrange(f"p ({' '.join(names)}) -> p {' '.join(names)}",
                                   **{x: s for x, s in zip(names, shape)})

        ar = Arena()
        spec_w = [ar([POS, BINS]) for _ in range(2)]
        spec_x = [ar([POS, GB, B]) for _ in range(2)]
        spec_f = ar([B, 2, POS])
        spec_o = ar([BS, POS, 2], 2 * 32)
        spec_ot = ar([KT, BS, 2 * 32], KROWS)
        xs = normed[0][:, :, :]
        ar = Arena()
        pad = [ar([LEAD + B * IMG + 1]), ar([LEAD + B // 2 * IMG + 1])]
        conv = [ar([B, TOK]), ar([B // 2, TOK])]
        loc = ar([HALVES, B, INNER])
        mixed = ar([TILES, INNER])
        mixed_t = [ar([B * TOK]), ar([B * TOK])]
        conv_end = ar.at
        ar = Arena()
        q_t = [ar([B * TOK]), ar([B * TOK])]
        k_t = [ar([B * TOK]), ar([B * TOK])]
        probs, probs_t = ar([3, 384]), ar([3, 384])
        o_raw, o_div = ar([2, 2, CN]), ar([2, 2, CN])
        ar.at = conv_end
        v_sb = ar([TILES, NH, 32])
        ar = Arena()
        NQ = QIMGS * TOK
        qy1, qh = ar([HT, NQ]), ar([HT, NQ])
        qy2, qc2 = ar([NQ], C), ar([NQ], C)
        nmax = sb("nmax", [P, 3, 2])
        qmax, qmax1, qrec, qdiag, qscale = (sb("qmax", [P, 2, QG]), sb("qmax1", [QG, 2]), sb("qrec", [QG, 2]),
                                            sb("qdiag", [QG, 2, QG]), sb("qscale", [P, 2, QG]))
        ar = Arena()
        score, gate1 = ar([TILES, NE]), ar([TILES])
        cmp_a, cmp_b = ar([TILES, NE * NE]), ar([TILES, NE * NE])
        gates = sb("gates", [P, TILES, NE])

        bank_filled = [sem(f"bank{i}_filled") for i in range(8)]
        bank_drained = [sem(f"bank{i}_drained") for i in range(8)]
        x_loaded = [sem(f"x_loaded{c}") for c in range(CHUNKS)]
        const_a_loaded, const_b_loaded = sem("const_a_loaded"), sem("const_b_loaded")
        spec_w_loaded, n1_loaded = sem("spec_w_loaded"), sem("n1_loaded")
        l0_loaded, l1_loaded, l2_loaded, l3_loaded = (sem(f"l{i}_loaded") for i in range(4))
        q_loaded, proj_w_loaded, stored = sem("q_loaded"), sem("proj_w_loaded"), sem("stored")
        stats_ready, moments_ready = sem("stats_ready"), sem("moments_ready")
        eps_added, o_scaled = sem("eps_added"), sem("o_scaled")
        rstd_ready, normed_ready = sem("rstd_ready"), sem("normed_ready")
        spec_zero, n1_zero, gap_zero = sem("spec_zero"), sem("n1_zero"), sem("gap_zero")
        spec_x_rows, spec_w_rows = sem("spec_x_rows"), sem("spec_w_rows")
        dc_ready, spec_x_dve, spec_x_act = sem("dc_ready"), sem("spec_x_dve"), sem("spec_x_act")
        x_plus_xs = sem("x_plus_xs")
        ones_ready, bf_ready = sem("ones_ready"), sem("bf_ready")
        sign_copied, sign_centred, sign_ready = sem("sign_copied"), sem("sign_centred"), sem("sign_ready")
        diag_ready, pad_zero, conv_step = sem("diag_ready"), sem("pad_zero"), sem("conv_step")
        heads_w_zero, heads_w_ready = sem("heads_w_zero"), sem("heads_w_ready")
        proj_w_zero, v_zero, v_pad_ready = sem("proj_w_zero"), sem("v_zero"), sem("v_pad_ready")
        nmax_ready = sem("nmax_ready")
        qmax_ready, qchain, qclip, qh_ready, qclip2 = (sem("qmax_ready"), sem("qchain"), sem("qclip"),
                                                       sem("qh_ready"), sem("qclip2"))
        gate_step, gate_exp_ready = sem("gate_step"), sem("gate_exp_ready")

        def pe_bank(pe, *key):
            k, n = uses[key]
            if n:
                pe.wait_ge(bank_drained[k], n)
            return bank[k], bank_filled[k]

        def read_bank(eng, *key):
            k, n = uses[key]
            eng.wait_ge(bank_filled[k], n + 1)
            return bank[k], bank_drained[k]

        def landed(eng, *key):
            k, n = uses[key]
            eng.wait_ge(bank_drained[k], n + 1)

        tok = lambda t, n=P: slice(P * t, P * t + n)
        ctok = lambda c, n=CN: slice(CN * c, CN * c + n)
        SPEC_ALL = [(g, ri, n) for g in range(2) for ri in range(2) for n in range(GB)]
        SPEC_DVE, SPEC_ACT = SPEC_ALL[:11], SPEC_ALL[11:]
        CONV_STEPS = IMGS * (len(TAPS) - PE_TAPS - 1)
        HALF = POS // 2

        def unit_chunks(u):
            return (int(u[1]),) if u[0] == "m" else (2 * int(u[1]), 2 * int(u[1]) + 1)

        def window(k, image, dy, dx):
            at = LEAD + IMG * image + dy * PW + dx
            return pad[k][:, at:at + HH * PW].rearrange("p (y x) -> p y x", x=PW)[:, :, 0:WW]

        def spec_copy(g, ri, n, ph):
            rows = slice(64 * g, 64 * g + GR)
            pos = slice(HALF * ph, HALF * ph + HALF)
            return (spec_x[g][64 * ri:64 * ri + GR, pos, n, :],
                    spec_f[rows, :, ri, pos].rearrange("p b q -> p q b"), nmask[rows, n:n + 1])

        def relu_spec(n):
            q = min(PPB, POS - PPB * n)
            return (spec_o[0:64, :, PPB * n:PPB * n + q, :].rearrange("p o q r -> p q o r"),
                    bank[n][0:64, 0:q * BINS].rearrange("p (q o r) -> p q o r", q=q, o=BS))

        def inv_out(h, j):
            return xs.rearrange("p (b h) (n o) -> p h o n b", h=HALVES, o=BS)[:, h, OH * j:OH * j + OH]

        SPEC_W_DMAS, L0_DMAS, L1_DMAS, L2_DMAS, Q_DMAS, L3_DMAS, PROJ_DMAS = 4, 6, 21, 3, 4, 12, 12
        col = lambda v: v.rearrange("(p o) -> p o", o=1)

        ctx.enter_context(nc.allow_non_contiguous_dma(reason="biases and scales, a channel a partition"))
        block = ctx.enter_context(nc.Block())

        @block.sync
        def _(sp):
            x_d = a["x"].rearrange("b h w c -> (b h w) c").rearrange("(t p) c -> p t c", p=P)
            o_d = out.rearrange("b h w c -> (b h w) c").rearrange("(t p) c -> p t c", p=P)
            for c in range(CHUNKS):
                sp.dma_start(X[:, CT * c:CT * c + CT, :], x_d[:, CT * c:CT * c + CT, :]).then_inc(x_loaded[c], 16)
                if c == 0:
                    sp.dma_start(const_a[:, :], a["const_a"]).then_inc(const_a_loaded, 16)
                    sp.wait_ge(n1_zero, 2)
                    for v, t in ((a["L0_conv_norm1_w"], n1g), (a["L0_conv_norm1_b"], n1b)):
                        for g in range(2):
                            sp.dma_start(t[64 * g:64 * g + GR, :], col(v[GR * g:GR * g + GR])).then_inc(n1_loaded, 16)
            w_d = a["L0_conv_w1"].rearrange("h w n i o r -> (n i) (h w) (o r)")
            b_d = a["L0_conv_b1"].rearrange("h w n o r -> n (h w) (o r)")
            sp.wait_ge(spec_zero, 2)
            for g in range(2):
                sp.dma_start(spec_w[g][0:GR], w_d[GR * g:GR * g + GR]).then_inc(spec_w_loaded, 16)
                sp.dma_start(spec_w[g][GR:GR + GB], b_d[GB * g:GB * g + GB]).then_inc(spec_w_loaded, 16)
            sp.dma_start(qw1[:, :, :], a["L2_ffn_W1"].rearrange("(k p) c -> p k c", p=P)).then_inc(q_loaded, 16)
            sp.dma_start(qw2[:, :], a["L2_ffn_W2"]).then_inc(q_loaded, 16)
            sp.dma_start(qb1[:, :], a["L2_ffn_b1"].rearrange("(k p) -> p k", p=P)).then_inc(q_loaded, 16)
            sp.dma_start(qb2[:, :], col(a["L2_ffn_b2"])).then_inc(q_loaded, 16)
            sp.dma_start(const_b[:, :], a["const_b"]).then_inc(const_b_loaded, 16)
            sp.dma_start(mlp_w1[0][:, :], a["L0_conv_mlp_w1"]).then_inc(l0_loaded, 16)
            sp.dma_start(mlp_b1[0][:, :], a["L0_conv_mlp_b1"].rearrange("(k p) -> p k", p=P)).then_inc(l0_loaded, 16)
            sp.dma_start(mlp_w2[0][:, :, :], a["L0_conv_mlp_w2"].rearrange("(k p) c -> p k c", p=P)).then_inc(l0_loaded, 16)
            sp.dma_start(mlp_b2[0][:, :], col(a["L0_conv_mlp_b2"])).then_inc(l0_loaded, 16)
            sp.dma_start(affine[L0B][0][:, :], col(a["L0_conv_norm2_w"])).then_inc(l0_loaded, 16)
            sp.dma_start(affine[L0B][1][:, :], col(a["L0_conv_norm2_b"])).then_inc(l0_loaded, 16)
            l1 = [(affine[L1A][0][:, :], col(a["L1_conv_n1_g"])), (affine[L1A][1][:, :], col(a["L1_conv_n1_b"])),
                  (affine[L1B][0][:, :], col(a["L1_conv_n2_g"])), (affine[L1B][1][:, :], col(a["L1_conv_n2_b"])),
                  (w_in[:, :], a["L1_conv_w_in"]),
                  (b_in[0][:, :], col(a["L1_conv_b_in"][0:P])), (b_in[1][:, :], col(a["L1_conv_b_in"][P:INNER])),
                  (on_g[0][:, :], col(a["L1_conv_on_g"][0:P])), (on_g[1][:, :], col(a["L1_conv_on_g"][P:INNER])),
                  (on_b[0][:, :], col(a["L1_conv_on_b"][0:P])), (on_b[1][:, :], col(a["L1_conv_on_b"][P:INNER])),
                  (w_out[0][:, :], a["L1_conv_w_out"][0:P, :]), (w_out[1][:, :], a["L1_conv_w_out"][P:INNER, :]),
                  (b_out[:, :], col(a["L1_conv_b_out"])),
                  (mlp_w1[1][:, :], a["L1_conv_w1"]),
                  (mlp_b1[1][:, :], a["L1_conv_b1"].rearrange("(k p) -> p k", p=P)),
                  (mlp_w2[1][:, :, :], a["L1_conv_w2"].rearrange("(k p) c -> p k c", p=P)),
                  (mlp_b2[1][:, :], col(a["L1_conv_b2"]))]
            k_d = a["L1_conv_k_conv"].rearrange("y x o c -> c (y x o)")
            l1 += [(kcol[0][:, :], k_d[0:P]), (kcol[1][0:IN2, :], k_d[P:INNER]), (kcol[1][IN2:P, :], k_d[P:INNER])]
            for dst, src in l1:
                sp.dma_start(dst, src).then_inc(l1_loaded, 16)
            for i, name in enumerate(("L2_attn_w_attn", "L3_attn_W_qkv")):
                sp.dma_start(w_qkv[i][:, :], a[name]).then_inc(l2_loaded, 16)
            sp.dma_start(b_proj[:, :], col(a["L3_attn_b_proj"])).then_inc(l2_loaded, 16)
            sp.wait_ge(proj_w_zero, 4)
            for i, name in enumerate(("L2_attn_w_proj", "L3_attn_W_proj")):
                for g, heads in enumerate(HEAD_GROUPS):
                    for j, h in enumerate(heads):
                        sp.dma_start(w_proj[i][g][32 * j:32 * j + HD, :],
                                     a[name][HD * h:HD * h + HD, :]).then_inc(proj_w_loaded, 16)
            sp.dma_start(gate_w[:, :], a["L3_ffn_gate_w"]).then_inc(l3_loaded, 16)
            sp.dma_start(gate_b[:, :], a["L3_ffn_gate_b"].rearrange("(o e) -> o e", o=1).broadcast_to([P, NE])
                         ).then_inc(l3_loaded, 16)
            for e in range(NE):
                sp.dma_start(e_w1[:, e, :], a["L3_ffn_w1"][e]).then_inc(l3_loaded, 16)
                sp.dma_start(e_w2[:, e], a["L3_ffn_w2"][e].rearrange("(k p) c -> p k c", p=P)).then_inc(l3_loaded, 16)
            sp.dma_start(e_b1[:, :, :], a["L3_ffn_b1"].rearrange("e (k p) -> p e k", p=P)).then_inc(l3_loaded, 16)
            sp.dma_start(e_b2[:, :], a["L3_ffn_b2"].rearrange("e c -> c e")).then_inc(l3_loaded, 16)
            for c in range(CHUNKS):
                landed(sp, "eback", NE * c + NE - 1)
                sp.dma_start(o_d[:, CT * c:CT * c + CT, :], X[:, CT * c:CT * c + CT, :]).then_inc(stored, 16)
            sp.wait_ge(stored, 16 * CHUNKS)

        @block.tensor
        def _(pe):
            def turn(l, c, src, width=CT):
                pe.wait_ge(normed_ready, LN_NO[l, c])
                ps, filled = pe_bank(pe, "turn", l, c)
                for t in range(width):
                    mm = nc.tensor.transpose(ps[0:C, tok(t)], src[:, CT * c + t, :], ident)
                mm.then_inc(filled, 1)

            def back(l, c, src, width=CT):
                ps, filled = pe_bank(pe, "back", l, c)
                for t in range(width):
                    mm = nc.tensor.transpose(ps[:, C * t:C * t + C], src[:, tok(t)], ident[0:C, 0:C])
                mm.then_inc(filled, 1)

            def mlp(m, l, nxt):
                for s in range(CHUNKS + 3):
                    if s < CHUNKS:
                        landed(pe, "turn", l, s)
                        for k in range(HT):
                            ps, filled = pe_bank(pe, "up", m, s, k)
                            nc.tensor.matmul(ps[:, :], mlp_w1[m][:, tok(k)], normed_t[l % 2][:, ctok(s)],
                                             start=True, stop=True).then_inc(filled, 1)
                    if 1 <= s <= CHUNKS:
                        c = s - 1
                        ps, filled = pe_bank(pe, "down", m, c)
                        for k in range(HT):
                            landed(pe, "up", m, c, k)
                            mm = nc.tensor.matmul(ps[0:C, :], mlp_w2[m][:, k, :], hidden[:, c % 2, k, :],
                                                  start=(k == 0), stop=(k == HT - 1))
                        mm.then_inc(filled, 1)
                    if 2 <= s <= CHUNKS + 1:
                        landed(pe, "down", m, s - 2)
                        back(l, s - 2, y_t[:, s % 2, :])
                    if s >= 3:
                        turn(nxt, s - 3, normed[nxt % 2])

            pe.wait_ge(const_a_loaded, 16)
            pe.wait_ge(gap_zero, 1)
            for b in range(B):
                pe.wait_ge(normed_ready, LN_NO[L0A, b // IMGS])
                ps, filled = pe_bank(pe, "dft", b)
                for h in range(HALVES):
                    mm = nc.tensor.matmul(ps[0:64 + GR, 0:2 * POS], normed_s[:, HALVES * b + h, 0:64 + GR],
                                          dft[:, h, :], start=(h == 0), stop=(h == HALVES - 1))
                mm.then_inc(filled, 1)
            pe.wait_ge(spec_w_loaded, 16 * SPEC_W_DMAS)
            pe.wait_ge(spec_w_rows, 4)
            for p in range(POS):
                if p % (POS // 2) == 0:
                    pe.wait_ge(spec_x_dve, len(SPEC_DVE) * (1 + p // (POS // 2)))
                    pe.wait_ge(spec_x_act, len(SPEC_ACT) * (1 + p // (POS // 2)))
                if p % PPB == 0:
                    ps, filled = pe_bank(pe, "spec", p // PPB)
                for g in range(2):
                    mm = nc.tensor.matmul(ps[32 * g:32 * g + 32, BINS * (p % PPB):BINS * (p % PPB) + BINS],
                                          spec_x[g][0:64 + GR, p, :, :].rearrange("p n b -> p (n b)"),
                                          spec_w[g][0:64 + GR, p, :], start=True, stop=True)
                if p % PPB == PPB - 1 or p == POS - 1:
                    mm.then_inc(filled, 1)
            for k in range(KT):
                for n in range((KP * (k + 1) - 1) // PPB + 1):
                    landed(pe, "spec", n)
                for j in range(2):
                    ps, filled = pe_bank(pe, "spec_t", k, j)
                    for o in range(OH):
                        oo = OH * j + o
                        mm = nc.tensor.transpose(ps[0:KROWS, 64 * o:64 * o + 64],
                                                 spec_o[:, oo, KP * k:KP * k + KP, :].rearrange("p q r -> p (q r)"),
                                                 ident[0:64, 0:64])
                    mm.then_inc(filled, 1)
            pe.wait_ge(const_b_loaded, 16)
            for h in range(HALVES):
                for j in range(2):
                    ps, filled = pe_bank(pe, "inv", 2 * h + j)
                    for k in range(KT):
                        landed(pe, "spec_t", k, j)
                        mm = nc.tensor.matmul(ps[:, 0:64 * OH], idft[0:KROWS, k, tok(h)],
                                              spec_ot[:, k, OH * j:OH * j + OH, :].rearrange("p o m -> p (o m)"),
                                              start=(k == 0), stop=(k == KT - 1))
                    mm.then_inc(filled, 1)
            pe.wait_ge(q_loaded, 16 * Q_DMAS)
            ps, filled = pe_bank(pe, "signprep", 0)
            for k in range(HT):
                mm = nc.tensor.transpose(ps[0:C, tok(k)], qw1[:, k, :], ident)
            mm.then_inc(filled, 1)
            ps, filled = pe_bank(pe, "signprep", 1)
            for k in range(HT):
                mm = nc.tensor.transpose(ps[:, C * k:C * k + C], qw2[:, tok(k)], ident[0:C, 0:C])
            mm.then_inc(filled, 1)
            for c in range(CHUNKS):
                turn(L0B, c, normed[L0B % 2])
            pe.wait_ge(ones_ready, 1)
            landed(pe, "signprep", 0)
            landed(pe, "signprep", 1)
            ps, filled = pe_bank(pe, "signprep", 2)
            nc.tensor.matmul(ps[:, 0:QG], ones[0:C, :], qsum[0:C, 0, :], start=True, stop=True).then_inc(filled, 1)
            ps, filled = pe_bank(pe, "signprep", 3)
            nc.tensor.matmul(ps[:, 0:QG], ones[:, :], qsum[:, 1, :], start=True, stop=True).then_inc(filled, 1)
            pe.wait_ge(l0_loaded, 16 * L0_DMAS)
            mlp(0, L0B, L1A)

            pe.wait_ge(l1_loaded, 16 * L1_DMAS)
            for what, x in conv_order():
                if what == "win":
                    landed(pe, "turn", L1A, x)
                    for k, (lo, n) in enumerate(((0, P), (P, IN2))):
                        ps, filled = pe_bank(pe, "win", x, k)
                        nc.tensor.matmul(ps[0:n, :], w_in[:, lo:lo + n], normed_t[L1A % 2][:, ctok(x)],
                                         start=True, stop=True).then_inc(filled, 1)
                elif what == "taps":
                    k, first = int(x[0] == "s"), IMGS * int(x[1])
                    pe.wait_ge(diag_ready, 2 * PE_TAPS)
                    pe.wait_ge(pad_zero, 2)
                    for c in unit_chunks(x):
                        landed(pe, "win", c, k)
                    for im in range(IMGS):
                        ps, filled = pe_bank(pe, "taps", x, im)
                        for n in range(PE_TAPS):
                            dy, dx = TAPS[n]
                            mm = nc.tensor.matmul(ps[:, 0:TOK], tap_diag[:, k, n, :], window(k, first + im, dy, dx),
                                                  start=(n == 0), stop=(n == PE_TAPS - 1))
                        mm.then_inc(filled, 1)
                elif what == "loc":
                    k, first = int(x[0] == "s"), IMGS * int(x[1])
                    pe.wait_ge(conv_step, CONV_STEPS * (UNITS.index(x) + 1))
                    ps, filled = pe_bank(pe, "loc", x)
                    for im in range(IMGS):
                        for h in range(HALVES):
                            mm = nc.tensor.transpose(ps[:, tok(HALVES * im + h)], conv[k][:, first + im, tok(h)],
                                                     ident)
                    mm.then_inc(filled, 1)
                elif what == "mix":
                    landed(pe, "loc", f"m{x}")
                    landed(pe, "loc", f"s{x // 2}")
                    for ho in range(HALVES):
                        ps, filled = pe_bank(pe, "mix", x, ho)
                        for hi in range(HALVES):
                            mm = nc.tensor.matmul(
                                ps[:, 0:IMGS * INNER], mix[:, hi, tok(ho)],
                                loc[:, hi, IMGS * x:IMGS * x + IMGS, :].rearrange("p b c -> p (b c)"),
                                start=(hi == 0), stop=(hi == HALVES - 1))
                        mm.then_inc(filled, 1)
                elif what == "turn_m":
                    pe.wait_ge(normed_ready, LN_NO[L1M, x])
                    for k, (lo, n) in enumerate(((0, P), (P, IN2))):
                        ps, filled = pe_bank(pe, "turn_m", x, k)
                        for t in range(CT):
                            mm = nc.tensor.transpose(ps[0:n, tok(t)], mixed[:, CT * x + t, lo:lo + n], ident)
                        mm.then_inc(filled, 1)
                elif what == "wout":
                    landed(pe, "turn_m", x, 0)
                    landed(pe, "turn_m", x, 1)
                    ps, filled = pe_bank(pe, "wout", x)
                    nc.tensor.matmul(ps[0:C, :], w_out[0][:, :], mixed_t[0][:, ctok(x)], start=True, stop=False)
                    nc.tensor.matmul(ps[0:C, :], w_out[1][:, :], mixed_t[1][0:IN2, ctok(x)],
                                     start=False, stop=True).then_inc(filled, 1)
                elif what == "back":
                    landed(pe, "wout", x)
                    back(L1A, x, y_t[:, x % 2, :])
                elif what == "turn":
                    turn(L1B, x, normed[L1B % 2])
            mlp(1, L1B, A2)

            def attention(a, l, nxt):
                def qkv(c):
                    if c == 0 and a == 0:
                        pe.wait_ge(heads_w_ready, 8)
                    landed(pe, "turn", l, c)
                    for k in range(3):
                        ps, filled = pe_bank(pe, "qk", a, c, k)
                        nc.tensor.matmul(ps[:, :], w_heads[a][:, k, :], normed_t[l % 2][:, ctok(c)],
                                         start=True, stop=True).then_inc(filled, 1)
                    ps, filled = pe_bank(pe, "v", a, c)
                    for t in range(CT):
                        mm = nc.tensor.matmul(ps[:, C * t:C * t + C], normed_t[l % 2][:, tok(CT * c + t)],
                                              w_qkv[a][:, 2 * C:3 * C], start=True, stop=True)
                    mm.then_inc(filled, 1)

                def where(i):
                    c, (im, h) = i // NI, ITEMS[i % NI]
                    return c, im, h, int(h >= 4), 32 * (h % 4)

                qkv(0)
                for s, hooks in attention_steps():
                    if s < NI * CHUNKS:
                        c, im, h, g, r = where(s)
                        if s % NI == 0:
                            for k in range(3):
                                landed(pe, "qk", a, c, k)
                        t0 = CN * c + TOK * im
                        ps, filled = pe_bank(pe, "s", a, s)
                        for lo, hi, q0, keys in ((0, P, t0, P), (P, 384, t0 + P, TOK)):
                            nc.tensor.matmul(ps[:, lo:hi], ident_b[:, :], mask_b[:, lo:hi], start=True, stop=False)
                            mm = nc.tensor.matmul(ps[:, lo:hi], q_t[g][r:r + HD, q0:q0 + P],
                                                  k_t[g][r:r + HD, t0:t0 + keys], start=False, stop=True)
                        mm.then_inc(filled, 1)
                    i = s - 2
                    if 0 <= i < NI * CHUNKS:
                        landed(pe, "s", a, i)
                        ps, filled = pe_bank(pe, "pt", a, i)
                        for k in range(3):
                            mm = nc.tensor.transpose(ps[:, tok(k)], probs[:, i % 3, tok(k)], ident)
                        mm.then_inc(filled, 1)
                    i = s - 3
                    if 0 <= i < NI * CHUNKS:
                        c, im, h, g, r = where(i)
                        if i % NI in (0, IMGS * len(HEAD_GROUPS[0])):
                            o_bank = pe_bank(pe, "o", a, c, g)
                        if i % NI == 0:
                            landed(pe, "v", a, c)
                        ps, filled = o_bank
                        landed(pe, "pt", a, i)
                        t0 = CT * c + HALVES * im
                        nc.tensor.matmul(ps[r:r + 32, TOK * im:TOK * im + TOK], v_sb[:, t0, h, :],
                                         probs_t[:, i % 3, 0:TOK], start=True, stop=False)
                        mm = nc.tensor.matmul(ps[r:r + 32, TOK * im + P:TOK * im + TOK], v_sb[:, t0 + 1, h, :],
                                              probs_t[:, i % 3, TOK:384], start=False, stop=True)
                        if i % NI in (IMGS * len(HEAD_GROUPS[0]) - 1, NI - 1):
                            mm.then_inc(filled, 1)
                    for what, c in hooks:
                        if what == "qkv":
                            qkv(c)
                        if what in ("sum0", "sum1"):
                            g = int(what[-1])
                            rows = 32 * len(HEAD_GROUPS[g])
                            landed(pe, "o", a, c, g)
                            ps, filled = pe_bank(pe, "sum", a, c, g)
                            nc.tensor.matmul(ps[0:rows, :], sumsel[0:rows, 0:rows], o_raw[0:rows, c % 2, g, :],
                                             start=True, stop=True).then_inc(filled, 1)
                        if what == "proj":
                            pe.wait_ge(proj_w_loaded, 16 * PROJ_DMAS)
                            pe.wait_ge(o_scaled, 2 * (CHUNKS * a + c) + 2)
                            ps, filled = pe_bank(pe, "proj", a, c)
                            nc.tensor.matmul(ps[0:C, :], w_proj[a][0][:, :], o_div[:, c % 2, 0, :],
                                             start=True, stop=False)
                            nc.tensor.matmul(ps[0:C, :], w_proj[a][1][:, :], o_div[0:64, c % 2, 1, :],
                                             start=False, stop=True).then_inc(filled, 1)
                        if what == "back":
                            landed(pe, "proj", a, c)
                            back(l, c, y_t[:, c % 2, :])
                        if what == "turn" and (nxt, c) in T_SEQ:
                            turn(nxt, c, normed[nxt % 2], dict(chunks_of(nxt))[c])

            attention(0, A2, F2)

            pe.wait_ge(sign_ready, 4)
            for c, w in chunks_of(F2):
                landed(pe, "turn", F2, c)
                for k in range(HT):
                    ps, filled = pe_bank(pe, "qup", c, k)
                    nc.tensor.matmul(ps[:, 0:P * w], sign1[:, tok(k)], normed_t[F2 % 2][:, ctok(c, P * w)],
                                     start=True, stop=True).then_inc(filled, 1)

            def gamma(n, rows):
                pe.wait_ge(qmax_ready, QG * (n + 1))
                ps, filled = pe_bank(pe, "gamma", n, 0)
                nc.tensor.transpose(ps[0:QG, 0:rows], qmax[0:rows, n, :], ident[0:rows, 0:rows]).then_inc(filled, 1)
                pe.wait_ge(qchain, 3 * n + 3)
                ps, filled = pe_bank(pe, "gamma", n, 1)
                nc.tensor.matmul(ps[:, 0:QG], ones[0:QG, :], qdiag[:, n, :], start=True, stop=True).then_inc(filled, 1)

            gamma(0, P)
            for c, w in chunks_of(F2):
                pe.wait_ge(qh_ready, min(IMGS * c + IMGS, QG))
                ps, filled = pe_bank(pe, "qdown", c)
                for k in range(HT):
                    mm = nc.tensor.matmul(ps[0:C, 0:P * w], sign2[:, k, :], qh[:, k, ctok(c, P * w)],
                                          start=(k == 0), stop=(k == HT - 1))
                mm.then_inc(filled, 1)
            gamma(1, C)
            for c, w in chunks_of(F2):
                pe.wait_ge(qclip2, 2 * min(IMGS * c + IMGS, QG))
                back(F2, c, qc2[:, ctok(c, P * w)], w)
            for c in range(CHUNKS):
                turn(A3, c, normed[A3 % 2])

            attention(1, A3, MO)

            pe.wait_ge(l3_loaded, 16 * L3_DMAS)
            for s in range(NE * CHUNKS + 2):
                if s < NE * CHUNKS:
                    c, e = s // NE, s % NE
                    landed(pe, "turn", MO, c)
                    for k in range(HT):
                        ps, filled = pe_bank(pe, "eup", s, k)
                        nc.tensor.matmul(ps[:, :], e_w1[:, e, tok(k)], normed_t[MO % 2][:, ctok(c)],
                                         start=True, stop=True).then_inc(filled, 1)
                if s == 0:
                    for c in range(CHUNKS):
                        landed(pe, "turn", MO, c)
                    ps, filled = pe_bank(pe, "gate")
                    for t in range(TILES):
                        mm = nc.tensor.matmul(ps[:, NE * t:NE * t + NE], normed_t[MO % 2][:, tok(t)], gate_w[:, :],
                                              start=True, stop=True)
                    mm.then_inc(filled, 1)
                if 0 <= s - 1 < NE * CHUNKS:
                    i = s - 1
                    ps, filled = pe_bank(pe, "edown", i)
                    for k in range(HT):
                        landed(pe, "eup", i, k)
                        mm = nc.tensor.matmul(ps[0:C, :], e_w2[:, i % NE, k, :], hidden[:, i % 2, k, :],
                                              start=(k == 0), stop=(k == HT - 1))
                    mm.then_inc(filled, 1)
                if s >= 2:
                    i = s - 2
                    landed(pe, "edown", i)
                    ps, filled = pe_bank(pe, "eback", i)
                    for t in range(CT):
                        mm = nc.tensor.transpose(ps[:, C * t:C * t + C], y_t[:, i % 2, tok(t)], ident[0:C, 0:C])
                    mm.then_inc(filled, 1)


        @block.scalar
        def _(act):
            def turned(l, c, width=CT):
                ps, drained = read_bank(act, "turn", l, c)
                dst = normed_t[l % 2][:, ctok(c, P * width)]
                if l in affine:
                    g, b = affine[l]
                    nc.scalar.activation(dst, ps[0:C, 0:P * width], ACT.Identity, bias=b[:, :],
                                         scale=g[:, :]).then_inc(drained, 1)
                else:
                    nc.scalar.activation(dst, ps[0:C, 0:P * width], ACT.Copy).then_inc(drained, 1)

            def mlp(m, l, nxt):
                for s in range(CHUNKS + 3):
                    if s < CHUNKS:
                        for k in range(HT):
                            ps, drained = read_bank(act, "up", m, s, k)
                            nc.scalar.activation(hidden[:, s % 2, k, :], ps[:, :], ACT.Gelu,
                                                 bias=mlp_b1[m][:, k:k + 1]).then_inc(drained, 1)
                    if s >= 3:
                        turned(nxt, s - 3)

            act.wait_ge(const_a_loaded, 16)
            nc.scalar.activation(spec_x[0][32:64].rearrange("p q n b -> p q (n b)"),
                                 delta[32:64, :].unsqueeze(1).broadcast_to([32, POS, GB * B]),
                                 ACT.Copy).then_inc(spec_x_rows, 1)
            act.wait_ge(n1_loaded, 16 * 4)
            for b in range(B):
                ps, drained = read_bank(act, "dft", b)
                nc.scalar.activation(spec_f[0:64 + GR, b].rearrange("p r q -> p (r q)"), ps[0:64 + GR, 0:2 * POS],
                                     ACT.Identity, scale=n1g[0:64 + GR, :]).then_inc(drained, 1)
            act.wait_ge(spec_w_loaded, 16 * SPEC_W_DMAS)
            for g in range(2):
                nc.scalar.activation(spec_w[g][64:64 + GR, :, 0:BINS:2], spec_w[g][0:GR, :, 1:BINS:2], ACT.Copy,
                                     scale=-1.0).then_inc(spec_w_rows, 1)
                nc.scalar.activation(spec_w[g][64:64 + GR, :, 1:BINS:2], spec_w[g][0:GR, :, 0:BINS:2],
                                     ACT.Copy).then_inc(spec_w_rows, 1)
            act.wait_ge(dc_ready, 2)
            act.wait_ge(spec_x_rows, 2)
            for ph in range(2):
                for g, ri, n in SPEC_ACT:
                    dst, src, mask = spec_copy(g, ri, n, ph)
                    nc.scalar.activation(dst, src, ACT.Copy, scale=mask).then_inc(spec_x_act, 1)
            for n in range(0, SBANKS, 2):
                ps, drained = read_bank(act, "spec", n)
                dst, src = relu_spec(n)
                nc.scalar.activation(dst, src, ACT.Relu).then_inc(drained, 1)
            for k in range(KT):
                ps, drained = read_bank(act, "spec_t", k, 0)
                nc.scalar.activation(spec_ot[:, k, 0:OH, :].rearrange("p o m -> p (o m)"),
                                     ps[0:KROWS, 0:64 * OH], ACT.Copy).then_inc(drained, 1)
            for h in range(HALVES):
                ps, drained = read_bank(act, "inv", 2 * h)
                nc.scalar.activation(inv_out(h, 0), ps[:, 0:64 * OH].rearrange("p (o n b) -> p o n b", o=OH, b=B),
                                     ACT.Copy).then_inc(drained, 1)
            act.wait_ge(l0_loaded, 16 * L0_DMAS)
            for c in range(CHUNKS):
                turned(L0B, c)
            act.wait_ge(sign_centred, 2)
            nc.scalar.activation(sign1[:, 0:QG * G1], qw1_t[:, 0:QG * G1], ACT.Sign).then_inc(sign_ready, 1)
            nc.scalar.activation(sign2[:, :, 0:QG * G2], qw2_t[:, :, 0:QG * G2], ACT.Sign).then_inc(sign_ready, 1)
            act.wait_ge(l1_loaded, 16 * L1_DMAS)
            mlp(0, L0B, L1A)

            act.wait_ge(pad_zero, 2)
            for what, x in conv_order():
                if what == "win":
                    lo = LEAD + IMG * IMGS * x
                    ps, drained = read_bank(act, "win", x, 0)
                    dst = pad[0][:, lo:lo + IMGS * IMG].rearrange("p (b y x) -> p b y x", b=IMGS, x=PW)
                    nc.scalar.activation(dst[:, :, 0:HH, 0:WW],
                                         ps[:, :].rearrange("p (b y x) -> p b y x", b=IMGS, x=WW),
                                         ACT.Identity, bias=b_in[0][:, :]).then_inc(drained, 1)
                    r, lo = 64 * (x % 2), LEAD + IMG * IMGS * (x // 2)
                    ps, drained = read_bank(act, "win", x, 1)
                    dst = pad[1][r:r + IN2, lo:lo + IMGS * IMG].rearrange("p (b y x) -> p b y x", b=IMGS, x=PW)
                    nc.scalar.activation(dst[:, :, 0:HH, 0:WW],
                                         ps[0:IN2, :].rearrange("p (b y x) -> p b y x", b=IMGS, x=WW),
                                         ACT.Identity, bias=b_in[1][:, :]).then_inc(drained, 1)
                elif what == "loc":
                    ps, drained = read_bank(act, "loc", x)
                    n = int(x[1])
                    for im in range(IMGS):
                        if x[0] == "m":
                            src = ps[:, tok(HALVES * im, HALVES * P)].rearrange("p (h c) -> p h c", h=HALVES)
                            last = nc.scalar.activation(loc[:, :, IMGS * n + im, 0:P], src, ACT.Copy)
                        else:
                            src = ps[:, tok(HALVES * im, HALVES * P)].rearrange("p (h k c) -> p h k c",
                                                                               h=HALVES, k=2)
                            b = 2 * IMGS * n + im
                            last = nc.scalar.activation(loc[:, :, b:b + IMGS + 1:IMGS, P:INNER], src, ACT.Copy)
                    last.then_inc(drained, 1)
                elif what == "turn_m":
                    for k, n in enumerate((P, IN2)):
                        ps, drained = read_bank(act, "turn_m", x, k)
                        nc.scalar.activation(mixed_t[k][0:n, ctok(x)], ps[0:n, :], ACT.Identity,
                                             bias=on_b[k][:, :], scale=on_g[k][:, :]).then_inc(drained, 1)
                elif what == "wout":
                    ps, drained = read_bank(act, "wout", x)
                    nc.scalar.activation(y_t[:, x % 2, :], ps[0:C, :], ACT.Identity,
                                         bias=b_out[:, :]).then_inc(drained, 1)
                elif what == "turn":
                    turned(L1B, x)
            mlp(1, L1B, A2)

            def attention(a, l, nxt):
                def qkv(c):
                    ps, drained = read_bank(act, "qk", a, c, 0)
                    nc.scalar.activation(q_t[0][:, ctok(c)], ps[:, :], ACT.Copy).then_inc(drained, 1)
                    ps, drained = read_bank(act, "qk", a, c, 2)
                    nc.scalar.activation(q_t[1][0:64, ctok(c)], ps[0:64, :], ACT.Copy)
                    nc.scalar.activation(k_t[1][0:64, ctok(c)], ps[64:P, :], ACT.Copy).then_inc(drained, 1)

                qkv(0)
                for s, hooks in attention_steps():
                    i = s - 2
                    if 0 <= i < NI * CHUNKS and i % 2:
                        ps, drained = read_bank(act, "pt", a, i)
                        nc.scalar.activation(probs_t[:, i % 3, :], ps[:, 0:384], ACT.Copy).then_inc(drained, 1)
                    if s < NI * CHUNKS:
                        ps, drained = read_bank(act, "s", a, s)
                        act.wait_ge(nmax_ready, NI * CHUNKS * a + s + 1)
                        nc.scalar.activation(probs[:, s % 3, 0:P], ps[:, 0:P], ACT.Exp, bias=nmax[:, s % 3, 0:1])
                        nc.scalar.activation(probs[:, s % 3, P:384], ps[:, P:384], ACT.Exp,
                                             bias=nmax[:, s % 3, 1:2]).then_inc(drained, 1)
                    for what, c in hooks:
                        if what == "qkv":
                            qkv(c)
                        if what in ("sum0", "sum1"):
                            g = int(what[-1])
                            rows = 32 * len(HEAD_GROUPS[g])
                            ps, drained = read_bank(act, "o", a, c, g)
                            nc.scalar.activation(o_raw[0:rows, c % 2, g, :], ps[0:rows, :],
                                                 ACT.Copy).then_inc(drained, 1)
                        if what == "proj":
                            ps, drained = read_bank(act, "proj", a, c)
                            if a == 0:
                                nc.scalar.activation(y_t[:, c % 2, :], ps[0:C, :], ACT.Copy).then_inc(drained, 1)
                            else:
                                nc.scalar.activation(y_t[:, c % 2, :], ps[0:C, :], ACT.Identity,
                                                     bias=b_proj[:, :]).then_inc(drained, 1)
                        if what == "turn" and (nxt, c) in T_SEQ:
                            turned(nxt, c, dict(chunks_of(nxt))[c])

            act.wait_ge(l2_loaded, 16 * L2_DMAS)
            attention(0, A2, F2)

            for c, w in chunks_of(F2):
                for k in range(HT):
                    ps, drained = read_bank(act, "qup", c, k)
                    nc.scalar.activation(qy1[:, k, ctok(c, P * w)], ps[:, 0:P * w], ACT.Identity,
                                         bias=qb1[:, k:k + 1]).then_inc(drained, 1)
            for b in range(QIMGS):
                act.wait_ge(qclip, 2 * b + 2)
                nc.scalar.activation(qh[:, :, TOK * b:TOK * b + TOK], qy1[:, :, TOK * b:TOK * b + TOK],
                                     ACT.Gelu).then_inc(qh_ready, 1)
            for c in range(CHUNKS):
                turned(A3, c)
            attention(1, A3, MO)

            act.wait_ge(l3_loaded, 16 * L3_DMAS)
            for i in range(NE * CHUNKS):
                for k in range(HT):
                    ps, drained = read_bank(act, "eup", i, k)
                    nc.scalar.activation(hidden[:, i % 2, k, :], ps[:, :], ACT.Gelu,
                                         bias=e_b1[:, i % NE, k:k + 1]).then_inc(drained, 1)
                if i == 0:
                    act.wait_ge(gate_step, 2)
                    nc.scalar.activation(score[:, :, :], score[:, :, :], ACT.Exp).then_inc(gate_exp_ready, 1)

        @block.vector
        def _(dve):
            def norm(l, c, src, width=CT):
                no = LN_NO[l, c]
                t0 = CT * c
                for t in range(width):
                    ins = nc.vector.bn_stats(stats[:, l, t0 + t, :], src(t))
                ins.then_inc(stats_ready, 1)
                dve.wait_ge(stats_ready, no)
                for t in range(width):
                    ins = nc.vector.bn_aggr(moments[:, l, t0 + t, :], stats[:, l, t0 + t, :])
                ins.then_inc(moments_ready, 1)
                dve.wait_ge(rstd_ready, no)
                for t in range(width):
                    if l == L0A:
                        dst = normed_s[:, t0 + t, :].rearrange("p (g c) -> p g c", g=2)[:, :, 0:GR]
                        v = src(t).rearrange("p (g c) -> p g c", g=2)
                    else:
                        dst = mixed[:, t0 + t, :] if l == L1M else normed[l % 2][:, t0 + t, :]
                        v = src(t)
                    ins = nc.vector.tensor_scalar(dst, v, moments[:, l, t0 + t, 0:1], rstd[:, l, t0 + t:t0 + t + 1],
                                                  ALU.subtract, ALU.mult)
                return ins.then_inc(normed_ready, 1)

            def x_tile(c):
                return lambda t: X[:, CT * c + t, :]

            def update(l, c, width=CT):
                ps, drained = read_bank(dve, "back", l, c)
                v = X[:, CT * c:CT * c + width, :]
                nc.vector.tensor_tensor(v, ps[:, 0:C * width].rearrange("p (t c) -> p t c", c=C), v,
                                        ALU.add).then_inc(drained, 1)
                landed(dve, "back", l, c)

            def mlp(m, l, nxt):
                for s in range(CHUNKS + 3):
                    if 1 <= s <= CHUNKS:
                        ps, drained = read_bank(dve, "down", m, s - 1)
                        nc.vector.tensor_scalar(y_t[:, (s - 1) % 2, :], ps[0:C, :], mlp_b2[m][:, :], None,
                                                ALU.add).then_inc(drained, 1)
                    if 2 <= s <= CHUNKS + 1:
                        update(l, s - 2)
                        norm(nxt, s - 2, x_tile(s - 2))

            nc.vector.memset(spec_w[0][32:64].rearrange("p q m -> p (q m)"), 0.0).then_inc(spec_zero, 1)
            for c in range(CHUNKS):
                dve.wait_ge(x_loaded[c], 16)
                norm(L0A, c, x_tile(c))
            dve.wait_ge(const_a_loaded, 16)
            nc.vector.tensor_copy(spec_x[1][32:64].rearrange("p q n b -> p q (n b)"),
                                  delta[32:64, :].unsqueeze(1).broadcast_to([32, POS, GB * B])
                                  ).then_inc(spec_x_rows, 1)
            dve.wait_ge(n1_loaded, 16 * 4)
            nc.vector.tensor_scalar(n1b16[0:64 + GR, :], n1b[0:64 + GR, :], float(TOK) ** 0.5, None,
                                    ALU.mult).then_inc(dc_ready, 1)
            for b in range(B):
                landed(dve, "dft", b)
            dve.wait_ge(dc_ready, 1)
            dc = spec_f[0:64 + GR, :, 0, 0]
            nc.vector.tensor_scalar(dc, dc, n1b16[0:64 + GR, :], None, ALU.add).then_inc(dc_ready, 1)
            dve.wait_ge(dc_ready, 2)
            dve.wait_ge(spec_x_rows, 2)
            for ph in range(2):
                for g, ri, n in SPEC_DVE:
                    dst, src, mask = spec_copy(g, ri, n, ph)
                    nc.vector.tensor_scalar(dst, src, mask, None, ALU.mult).then_inc(spec_x_dve, 1)
            for n in range(1, SBANKS, 2):
                ps, drained = read_bank(dve, "spec", n)
                dst, src = relu_spec(n)
                nc.vector.tensor_scalar(dst, src, 0.0, None, ALU.max).then_inc(drained, 1)
            for k in range(KT):
                ps, drained = read_bank(dve, "spec_t", k, 1)
                nc.vector.tensor_copy(spec_ot[:, k, OH:BS, :].rearrange("p o m -> p (o m)"),
                                      ps[0:KROWS, 0:64 * OH]).then_inc(drained, 1)
            for h in range(HALVES):
                ps, drained = read_bank(dve, "inv", 2 * h + 1)
                nc.vector.tensor_copy(inv_out(h, 1),
                                      ps[:, 0:64 * OH].rearrange("p (o n b) -> p o n b", o=OH, b=B)
                                      ).then_inc(drained, 1)
            for k in range(2 * HALVES):
                landed(dve, "inv", k)
            for c in range(CHUNKS):
                norm(L0B, c, lambda t, c=c: xs[:, CT * c + t, :])
            ps, drained = read_bank(dve, "signprep", 0)
            nc.vector.tensor_copy(qw1_t[:, :], ps[0:C, 0:HID]).then_inc(sign_copied, 1)
            nc.vector.tensor_reduce(qsum[0:C, 0, :], ps[0:C, 0:QG * G1].rearrange("p (g m) -> p g m", g=QG),
                                    AX.X, ALU.add).then_inc(drained, 1)
            ps, drained = read_bank(dve, "signprep", 1)
            nc.vector.tensor_copy(qw2_t[:, :, :].rearrange("p k c -> p (k c)"), ps[:, 0:HT * C]
                                  ).then_inc(sign_copied, 1)
            nc.vector.tensor_reduce(
                qsum[:, 1, :],
                ps[:, 0:HT * C].rearrange("p (k c) -> p k c", k=HT)[:, :, 0:QG * G2].rearrange(
                    "p k (g m) -> p g k m", g=QG), AX.XY, ALU.add).then_inc(drained, 1)
            for n, size in enumerate((G1 * C, G2 * HID)):
                ps, drained = read_bank(dve, "signprep", 2 + n)
                nc.vector.tensor_scalar(qmean[:, n, :], ps[:, 0:QG], 1.0 / size, None, ALU.mult).then_inc(drained, 1)
            dve.wait_ge(sign_copied, 2)
            landed(dve, "signprep", 2)
            landed(dve, "signprep", 3)
            v = qw1_t[:, 0:QG * G1].rearrange("p (g m) -> p g m", g=QG)
            nc.vector.tensor_tensor(v, v, qmean[0:C, 0, :].unsqueeze(2).broadcast_to([C, QG, G1]),
                                    ALU.subtract).then_inc(sign_centred, 1)
            for k in range(HT):
                v = qw2_t[:, k, 0:QG * G2].rearrange("p (g m) -> p g m", g=QG)
                ins = nc.vector.tensor_tensor(v, v, qmean[:, 1, :].unsqueeze(2).broadcast_to([P, QG, G2]),
                                              ALU.subtract)
            ins.then_inc(sign_centred, 1)
            dve.wait_ge(l0_loaded, 16 * L0_DMAS)
            dve.wait_ge(x_plus_xs, 1)
            mlp(0, L0B, L1A)

            dve.wait_ge(l1_loaded, 16 * L1_DMAS)

            def conv_unit(u):
                k, first = int(u[0] == "s"), IMGS * int(u[1])
                base = CONV_STEPS * UNITS.index(u)
                for n in range(PE_TAPS, len(TAPS)):
                    dy, dx = TAPS[n]
                    for im in range(IMGS):
                        dst = conv[k][:, first + im, :].rearrange("p (y x) -> p y x", x=WW)
                        src = window(k, first + im, dy, dx)
                        if n == PE_TAPS:
                            ps, drained = read_bank(dve, "taps", u, im)
                            nc.vector.scalar_tensor_tensor(dst, src, kcol[k][:, n:n + 1], ps[:, 0:TOK].rearrange("p (y x) -> p y x", x=WW),
                                                           ALU.mult, ALU.add).then_inc(drained, 1)
                            continue
                        if n == PE_TAPS + 1:
                            landed(dve, "taps", u, im)
                        else:
                            dve.wait_ge(conv_step, base + IMGS * (n - PE_TAPS - 2) + im + 1)
                        nc.vector.scalar_tensor_tensor(dst, src, kcol[k][:, n:n + 1], dst,
                                                       ALU.mult, ALU.add).then_inc(conv_step, 1)

            def norm_mixed(c):
                banks = [read_bank(dve, "mix", c, ho) for ho in range(HALVES)]
                norm(L1M, c, lambda t: banks[t % HALVES][0][:, INNER * (t // HALVES):INNER * (t // HALVES) + INNER])
                for _, drained in banks:
                    dve.wait_ge(normed_ready, LN_NO[L1M, c])
                    dve.sem_inc(drained, 1)

            for u in ("m0", "m1", "s0", "m2"):
                conv_unit(u)
            norm_mixed(0)
            conv_unit("m3")
            norm_mixed(1)
            conv_unit("s1")
            for c in (0, 1):
                update(L1A, c)
                norm(L1B, c, x_tile(c))
            norm_mixed(2)
            norm_mixed(3)
            for c in (2, 3):
                update(L1A, c)
                norm(L1B, c, x_tile(c))
            mlp(1, L1B, A2)

            def attention(a, l, nxt):
                def qkv(c):
                    ps, drained = read_bank(dve, "qk", a, c, 1)
                    nc.vector.tensor_copy(k_t[0][:, ctok(c)], ps[:, :]).then_inc(drained, 1)
                    ps, drained = read_bank(dve, "v", a, c)
                    dst = v_sb[:, CT * c:CT * c + CT].rearrange("p t h d -> p (t h) d")[:, :, 0:HD]
                    nc.vector.tensor_copy(dst, ps[:, 0:CT * C].rearrange("p (n d) -> p n d", d=HD)
                                          ).then_inc(drained, 1)

                qkv(0)
                for s, hooks in attention_steps():
                    if s < NI * CHUNKS:
                        k, n = uses["s", a, s]
                        dve.wait_ge(bank_filled[k], n + 1)
                        nc.vector.tensor_reduce(nmax[:, s % 3, 0:1], bank[k][:, 0:P], AX.X, ALU.max, negate=True)
                        nc.vector.tensor_reduce(nmax[:, s % 3, 1:2], bank[k][:, P:384], AX.X, ALU.max,
                                                negate=True).then_inc(nmax_ready, 1)
                    i = s - 2
                    if 0 <= i < NI * CHUNKS and i % 2 == 0:
                        ps, drained = read_bank(dve, "pt", a, i)
                        nc.vector.tensor_copy(probs_t[:, i % 3, :], ps[:, 0:384]).then_inc(drained, 1)
                    for what, c in hooks:
                        if what == "qkv":
                            qkv(c)
                        if what in ("sum0", "sum1"):
                            g = int(what[-1])
                            rows = 32 * len(HEAD_GROUPS[g])
                            ps, drained = read_bank(dve, "sum", a, c, g)
                            dst = o_div[0:rows, c % 2, g, :]
                            nc.vector.reciprocal(dst, ps[0:rows, :]).then_inc(drained, 1)
                            landed(dve, "sum", a, c, g)
                            nc.vector.tensor_tensor(dst, o_raw[0:rows, c % 2, g, :], dst,
                                                    ALU.mult).then_inc(o_scaled, 1)
                        if what == "back":
                            update(l, c)
                            if (nxt, c) in LN_NO:
                                norm(nxt, c, x_tile(c), dict(chunks_of(nxt))[c])

            dve.wait_ge(v_pad_ready, 1)
            attention(0, A2, F2)

            CLIP = QB - QEPS

            def scale_of(n, rows):
                ps, drained = read_bank(dve, "gamma", n, 0)
                nc.vector.tensor_reduce(qmax1[:, n:n + 1], ps[0:QG, 0:rows], AX.X, ALU.max).then_inc(drained, 1)
                landed(dve, "gamma", n, 0)
                nc.vector.tensor_scalar(qmax1[:, n:n + 1], qmax1[:, n:n + 1], QEPS, None,
                                        ALU.add).then_inc(qchain, 1)
                dve.wait_ge(qchain, 3 * n + 1)
                nc.vector.reciprocal(qrec[:, n:n + 1], qmax1[:, n:n + 1]).then_inc(qchain, 1)
                dve.wait_ge(qchain, 3 * n + 2)
                nc.vector.tensor_scalar(qdiag[:, n, :], ident[0:QG, 0:QG], qrec[:, n:n + 1], QB,
                                        ALU.mult, ALU.mult).then_inc(qchain, 1)
                ps, drained = read_bank(dve, "gamma", n, 1)
                nc.vector.tensor_copy(qscale[:, n, :], ps[:, 0:QG]).then_inc(drained, 1)
                landed(dve, "gamma", n, 1)

            for c, w in chunks_of(F2):
                for k in range(HT):
                    landed(dve, "qup", c, k)
                for b in range(IMGS * c, IMGS * c + w // HALVES):
                    nc.vector.tensor_reduce(qmax[:, 0, b:b + 1], qy1[:, :, TOK * b:TOK * b + TOK], AX.XY, ALU.max,
                                            apply_absolute_value=True).then_inc(qmax_ready, 1)
            scale_of(0, P)
            for b in range(QIMGS):
                v = qy1[:, :, TOK * b:TOK * b + TOK]
                nc.vector.tensor_scalar(v, v, qscale[:, 0, b:b + 1], CLIP, ALU.mult, ALU.min).then_inc(qclip, 1)
                dve.wait_ge(qclip, 2 * b + 1)
                nc.vector.tensor_scalar(v, v, -CLIP, None, ALU.max).then_inc(qclip, 1)
            for c, w in chunks_of(F2):
                ps, drained = read_bank(dve, "qdown", c)
                nc.vector.tensor_scalar(qy2[:, ctok(c, P * w)], ps[0:C, 0:P * w], qb2[:, :], None,
                                        ALU.add).then_inc(drained, 1)
                landed(dve, "qdown", c)
                for b in range(IMGS * c, IMGS * c + w // HALVES):
                    nc.vector.tensor_reduce(qmax[0:C, 1, b:b + 1], qy2[:, TOK * b:TOK * b + TOK], AX.X, ALU.max,
                                            apply_absolute_value=True).then_inc(qmax_ready, 1)
            scale_of(1, C)
            for b in range(QIMGS):
                v = qc2[:, TOK * b:TOK * b + TOK]
                nc.vector.tensor_scalar(v, qy2[:, TOK * b:TOK * b + TOK], qscale[0:C, 1, b:b + 1], CLIP,
                                        ALU.mult, ALU.min).then_inc(qclip2, 1)
                dve.wait_ge(qclip2, 2 * b + 1)
                nc.vector.tensor_scalar(v, v, -CLIP, None, ALU.max).then_inc(qclip2, 1)
            for c in range(CHUNKS):
                if (F2, c) in LN_NO:
                    update(F2, c, dict(chunks_of(F2))[c])
                norm(A3, c, x_tile(c))

            attention(1, A3, MO)

            step = [0]

            def then(ins):
                step[0] += 1
                ins.then_inc(gate_step, 1)
                dve.wait_ge(gate_step, step[0])

            spread = lambda v: v[:, :].unsqueeze(2).broadcast_to([P, TILES, NE])
            pairs = lambda v: v[:, :, :].rearrange("p t (i j) -> p t i j", i=NE)
            rank = lambda k: cb("rank")[:, NE * NE * k:NE * NE * (k + 1)].unsqueeze(1).broadcast_to(
                [P, TILES, NE * NE])
            dve.wait_ge(l3_loaded, 16 * L3_DMAS)
            ps, drained = read_bank(dve, "gate")
            nc.vector.tensor_tensor(score[:, :, :], ps[:, 0:NE * TILES].rearrange("p (t e) -> p t e", e=NE),
                                    gate_b[:, :].unsqueeze(1).broadcast_to([P, TILES, NE]),
                                    ALU.add).then_inc(drained, 1)
            landed(dve, "gate")
            then(nc.vector.tensor_reduce(gate1[:, :], score[:, :, :], AX.X, ALU.max))
            then(nc.vector.tensor_tensor(score[:, :, :], score[:, :, :], spread(gate1), ALU.subtract))
            dve.wait_ge(gate_exp_ready, 1)
            then(nc.vector.tensor_reduce(gate1[:, :], score[:, :, :], AX.X, ALU.add))
            then(nc.vector.reciprocal(gate1[:, :], gate1[:, :]))
            then(nc.vector.tensor_tensor(score[:, :, :], score[:, :, :], spread(gate1), ALU.mult))
            of_j = score[:, :, :].unsqueeze(2).broadcast_to([P, TILES, NE, NE])
            of_i = score[:, :, :].unsqueeze(3).broadcast_to([P, TILES, NE, NE])
            nc.vector.tensor_tensor(pairs(cmp_a), of_j, of_i, ALU.is_ge)
            then(nc.vector.tensor_tensor(pairs(cmp_b), of_j, of_i, ALU.is_gt))
            nc.vector.tensor_tensor(cmp_a[:, :, :], cmp_a[:, :, :], rank(0), ALU.mult)
            then(nc.vector.tensor_tensor(cmp_b[:, :, :], cmp_b[:, :, :], rank(1), ALU.mult))
            then(nc.vector.tensor_tensor(cmp_a[:, :, :], cmp_a[:, :, :], cmp_b[:, :, :], ALU.add))
            then(nc.vector.tensor_reduce(gates[:, :, :], pairs(cmp_a), AX.X, ALU.add))
            then(nc.vector.tensor_scalar(gates[:, :, :], gates[:, :, :], 1.5, None, ALU.is_lt))
            then(nc.vector.tensor_tensor(gates[:, :, :], gates[:, :, :], score[:, :, :], ALU.mult))
            then(nc.vector.tensor_reduce(gate1[:, :], gates[:, :, :], AX.X, ALU.add))
            then(nc.vector.tensor_scalar(gate1[:, :], gate1[:, :], 1e-9, None, ALU.add))
            then(nc.vector.reciprocal(gate1[:, :], gate1[:, :]))
            then(nc.vector.tensor_tensor(gates[:, :, :], gates[:, :, :], spread(gate1), ALU.mult))
            for s in range(1, NE * CHUNKS + 2):
                if s - 1 < NE * CHUNKS:
                    i = s - 1
                    ps, drained = read_bank(dve, "edown", i)
                    nc.vector.tensor_scalar(y_t[:, i % 2, :], ps[0:C, :], e_b2[:, i % NE:i % NE + 1], None,
                                            ALU.add).then_inc(drained, 1)
                if s >= 2:
                    i = s - 2
                    c, e = i // NE, i % NE
                    ps, drained = read_bank(dve, "eback", i)
                    if e:
                        landed(dve, "eback", i - 1)
                    for t in range(CT):
                        n = CT * c + t
                        ins = nc.vector.scalar_tensor_tensor(X[:, n, :], ps[:, C * t:C * t + C],
                                                             gates[:, n, e:e + 1], X[:, n, :], ALU.mult, ALU.add)
                    ins.then_inc(drained, 1)

        @block.gpsimd
        def _(pool):
            def rstds(*norms):
                for l, c in [k for k in LN_SEQ if k[0] in norms]:
                    w = dict(chunks_of(l))[c]
                    pool.wait_ge(moments_ready, LN_NO[l, c])
                    t = slice(CT * c, CT * c + w)
                    nc.gpsimd.tensor_scalar(moments[:, l, t, 1], moments[:, l, t, 1], LN_EPS, None,
                                            ALU.add).then_inc(eps_added, 1)
                    pool.wait_ge(eps_added, LN_NO[l, c])
                    nc.gpsimd.tensor_tensor(rstd[:, l, t], moments[:, l, t, 1], exponent[:, 0:w],
                                            ALU.pow).then_inc(rstd_ready, 1)

            nc.gpsimd.memset(exponent[:, :], -0.5)
            nc.gpsimd.memset(n1g[:, :], 0.0).then_inc(n1_zero, 1)
            nc.gpsimd.memset(n1b[:, :], 0.0).then_inc(n1_zero, 1)
            nc.gpsimd.memset(normed_s[:, :, GR:64], 0.0).then_inc(gap_zero, 1)
            pool.wait_ge(gap_zero, 1)
            nc.gpsimd.memset(spec_w[1][32:64].rearrange("p q m -> p (q m)"), 0.0).then_inc(spec_zero, 1)
            pool.wait_ge(spec_zero, 2)
            rstds(L0A)
            nc.gpsimd.memset(ones[:, :], 1.0).then_inc(ones_ready, 1)
            for i in range(2):
                for g in range(2):
                    nc.gpsimd.memset(w_proj[i][g][:, :], 0.0).then_inc(proj_w_zero, 1)
                nc.gpsimd.memset(w_heads[i][:, :, :], 0.0).then_inc(heads_w_zero, 1)
            nc.gpsimd.memset(sign1[:, QG * G1:HID], 0.0).then_inc(sign_ready, 1)
            nc.gpsimd.memset(sign2[:, :, QG * G2:C], 0.0).then_inc(sign_ready, 1)
            pool.wait_ge(const_b_loaded, 16)
            nc.gpsimd.tensor_copy(ident_b[:, :], ident).then_inc(bf_ready, 1)
            nc.gpsimd.tensor_copy(mask_b[:, :], cb("mask")).then_inc(bf_ready, 1)
            rstds(L0B)
            for k in range(2 * HALVES):
                landed(pool, "inv", k)
            nc.gpsimd.tensor_tensor(X[:, :, :], X[:, :, :], xs, ALU.add).then_inc(x_plus_xs, 1)
            for v in pad:
                nc.gpsimd.memset(v, 0.0).then_inc(pad_zero, 1)
            pool.wait_ge(l1_loaded, 16 * L1_DMAS)
            for k in range(2):
                for n in range(PE_TAPS):
                    nc.gpsimd.tensor_scalar(tap_diag[:, k, n, :], ident, kcol[k][:, n:n + 1], None,
                                            ALU.mult).then_inc(diag_ready, 1)
            rstds(L1A)
            pool.wait_ge(l2_loaded, 16 * L2_DMAS)
            pool.wait_ge(heads_w_zero, 2)
            for i in range(2):
                for which, lo, heads in ((0, 0, HEAD_GROUPS[0]), (1, 0, HEAD_GROUPS[0]),
                                         (0, 0, HEAD_GROUPS[1]), (1, 64, HEAD_GROUPS[1])):
                    k = which if len(heads) == 4 else 2
                    dst = w_heads[i][:, k, lo:lo + 32 * len(heads)].rearrange("p (h d) -> p h d", d=32)[:, :, 0:HD]
                    src = w_qkv[i][:, C * which + HD * heads[0]:C * which + HD * (heads[-1] + 1)].rearrange(
                        "p (h d) -> p h d", d=HD)
                    nc.gpsimd.tensor_scalar(dst, src, HD ** -0.5 if which == 0 else 1.0, None,
                                            ALU.mult).then_inc(heads_w_ready, 1)
            nc.gpsimd.memset(v_sb, 0.0).then_inc(v_zero, 1)
            pool.wait_ge(v_zero, 1)
            nc.gpsimd.memset(v_sb[:, :, :, HD:HD + 1], 1.0).then_inc(v_pad_ready, 1)
            rstds(L1M, L1B, A2, F2, A3, MO)


def constants():
    f = np.float64
    at_a, wa = spots(CONST_A)
    at_b, wb = spots(CONST_B)
    ca, cb = np.zeros((P, wa), f), np.zeros((P, wb), f)
    y, x = np.divmod(np.arange(TOK), WW)
    kh, kw = np.divmod(np.arange(POS), WF)
    angle = 2 * np.pi * (np.outer(y, kh) / HH + np.outer(x, kw) / WW)
    norm = TOK ** -0.5
    dft = np.concatenate([np.cos(angle), -np.sin(angle)], 1) * norm
    twice = np.where((kw == 0) | (kw == WW // 2), 1.0, 2.0)
    idft = np.stack([np.cos(angle) * twice * norm, -np.sin(angle) * twice * norm], 2).reshape(TOK, 2 * POS).T
    near = lambda d: 0.25 * 0.4 * 0.6 ** np.abs(d) * np.where(d == 0, 2.0, 1.0)
    dy, dx = y[:, None] - y[None, :], x[:, None] - x[None, :]
    mixer = np.eye(TOK) + near(dx) * (dy == 0) + near(dy) * (dx == 0)
    cut = lambda m, at, n: m[:, at[n][0]:at[n][1]]
    cut(ca, at_a, "ident")[:] = np.eye(P)
    for g in range(2):
        for n in range(GB):
            cut(ca, at_a, "nmask")[64 * g + BS * n:64 * g + BS * n + BS, n] = 1
    for n in range(GB):
        cut(ca, at_a, "delta")[GR + n, B * n:B * n + B] = 1
    cut(ca, at_a, "dft")[:] = dft.reshape(HALVES, P, 2 * POS).transpose(1, 0, 2).reshape(P, -1)
    above = np.where(np.arange(P)[None, :] > np.arange(P)[:, None], NEG, 0.0)
    cut(cb, at_b, "mask")[:] = np.concatenate([above, np.zeros((P, P)), above], 1)
    for m in range(P):
        cut(cb, at_b, "sumsel")[32 * (m // 32) + HD, m] = 1
    i, j = np.divmod(np.arange(NE * NE), NE)
    cut(cb, at_b, "rank")[:] = np.concatenate([j < i, j > i])[None, :]
    cut(cb, at_b, "idft")[0:KROWS] = idft.reshape(KT, KROWS, TOK).transpose(1, 0, 2).reshape(KROWS, -1)
    cut(cb, at_b, "mix")[:] = mixer.reshape(HALVES, P, TOK).transpose(1, 0, 2).reshape(P, -1)
    return {"const_a": ca.astype(np.float32), "const_b": cb.astype(np.float32)}


def kernel(**inputs):
    import concourse.bacc as bacc
    from concourse.bass_utils import run_bass_kernel_spmd

    nc = bacc.Bacc("TRN2", target_bir_lowering=False, num_devices=1)
    arrays, handles = {}, {}
    for name, value in {**inputs, **constants()}.items():
        v = np.ascontiguousarray(value)
        arrays[f"in_{name}"] = v
        handles[name] = nc.dram_tensor(f"in_{name}", v.shape, mybir.dt.from_np(v.dtype), kind="ExternalInput").ap()
    out = nc.dram_tensor("out_x", (B, HH, WW, C), F32, kind="ExternalOutput").ap()
    hybrid_kernel(nc, handles, out)
    return run_bass_kernel_spmd(nc, [arrays], core_ids=[0]).results[0]["out_x"]
```

```python
from contextlib import ExitStack

import numpy as np

import concourse.bass as bass
from concourse import mybir

F32 = mybir.dt.float32
BF16 = mybir.dt.bfloat16
ALU = mybir.AluOpType
ACT = mybir.ActivationFunctionType
AX = mybir.AxisListType

B, HH, WW, C = 8, 16, 16, 96
P = 128
TOK = HH * WW
HALVES = TOK // P
TILES = B * HALVES
IMGS = 2
CT = IMGS * HALVES
CN = IMGS * TOK
CHUNKS = B // IMGS
HID = 4 * C
HT = HID // P
WF = WW // 2 + 1
POS = HH * WF
NB, BS = 8, C // 8
GB = NB // 2
GR = GB * BS
BINS = 2 * BS
PPB = 512 // BINS
SBANKS = -(-POS // PPB)
KT = 3
KP = POS // KT
KROWS = 2 * KP
OH = BS // 2
INNER = 2 * C
IN2 = INNER - P
PW = WW + 1
IMG = PW * (HH + 1)
LEAD = PW + 1
TAPS = [(dy, dx) for dy in (-1, 0, 1) for dx in (-1, 0, 1)]
PE_TAPS = 4
UNITS = ["m0", "m1", "s0", "m2", "m3", "s1"]
NH, HD = 6, 16
HEAD_GROUPS = ((0, 1, 2, 3), (4, 5))
ITEMS = [(im, h) for heads in HEAD_GROUPS for im in range(IMGS) for h in heads]
NI = len(ITEMS)
NEG = -1e30
QG = 5
G1, G2 = HID // QG, C // QG
QB, QEPS = 128.0, 1e-5
QIMGS = QG * (B // QG)
NE = 4
LN_EPS = 1e-5
L0A, L0B, L1A, L1M, L1B, A2, F2, A3, MO = range(9)
X_OF = {L1A: 0, L1B: 1, A2: 2, F2: 3, A3: 4, MO: 5}

CONST_A = {"ident": 128, "hmask": NH, "nmask": 4, "delta": GB * B, "dft": HALVES * 2 * POS}
CONST_B = {"mask": 128, "rank": 32, "idft": KT * TOK, "mix": HALVES * TOK}


def spots(widths):
    at, out = 0, {}
    for name, w in widths.items():
        out[name] = (at, at + w)
        at += w
    return out, at


def chunks_of(l):
    if l == F2:
        return [(c, min(CT, HALVES * QIMGS - CT * c)) for c in range(CHUNKS) if CT * c < HALVES * QIMGS]
    return [(c, CT) for c in range(CHUNKS)]


LN_SEQ = [(l, c) for l in (L0A, L0B, L1A) for c in range(CHUNKS)]
LN_SEQ += [(l, c) for pair in ((0, 1), (2, 3)) for l in (L1M, L1B) for c in pair]
LN_SEQ += [(l, c) for l in (A2, F2) for c, _ in chunks_of(l)]
LN_SEQ += [(A3, CHUNKS - 1)] + [(A3, c) for c in range(CHUNKS - 1)] + [(MO, c) for c in range(CHUNKS)]
LN_NO = {k: n + 1 for n, k in enumerate(LN_SEQ)}
T_SEQ = [k for k in LN_SEQ if k[0] not in (L0A, L1M)]


def attention_steps(a, nxt):
    hooks = {2: [("turn_own", CHUNKS - 1)]} if a == 0 else {}
    for c in range(CHUNKS):
        if c:
            hooks.setdefault(NI * c - 6, []).append(("qkv", c))
        hooks.setdefault(NI * c + 15, []).append(("evac_o", c))
        hooks.setdefault(NI * c + 16, []).append(("turn_o", c))
        hooks.setdefault(NI * c + 17, []).append(("turn_n", c))
        hooks.setdefault(NI * c + 18, []).append(("proj", c))
        if (nxt, c) in T_SEQ:
            hooks.setdefault(NI * c + 20, []).append(("turn", c))
    return [(s, hooks.get(s, [])) for s in range(NI * CHUNKS + 9)]


def plan_banks():
    seq = []

    def use(bank, *key):
        seq.append((key, bank))

    def turn(l, c):
        use(c % 2, "turn", l, c)

    def mlp(m, l, nxt):
        for s in range(CHUNKS + 1):
            if s < CHUNKS:
                for k in range(HT):
                    use(2 + k, "up", m, s, k)
            if s == 0:
                turn(l, CHUNKS - 1)
            if s >= 1:
                use(5 + s % 2, "down", l, s - 1)
            if s >= 2:
                turn(nxt, s - 2)

    for b in range(B):
        use(b, "dft", b)
    for k in range(SBANKS):
        use(k, "spec", k)
    for k in range(KT):
        for j in range(2):
            use((7, 0, 1, 2, 3, 4)[2 * k + j], "spec_t", k, j)
    for k in range(HALVES * 2):
        use((5, 6, 7, 0)[k], "inv", k)
    use(1, "signprep", 0)
    use(2, "signprep", 1)
    for c in range(CHUNKS - 1):
        turn(L0B, c)
    use(3, "signprep", 2)
    use(4, "signprep", 3)
    mlp(0, L0B, L1A)
    def win(c):
        use(2 + c % 2, "win", c, 0)
        use(4 + c % 2, "win", c, 1)

    def taps(u):
        for im in range(IMGS):
            use(6 + im, "taps", u, im)

    for w in conv_order():
        if w[0] == "win":
            win(w[1])
        elif w[0] == "taps":
            taps(w[1])
        elif w[0] == "loc":
            use(1, "loc", w[1])
        elif w[0] == "mix":
            for ho in range(HALVES):
                use(2 + ho, "mix", w[1], ho)
        elif w[0] == "turn_m":
            use(4, "turn_m", w[1], 0)
            use(5, "turn_m", w[1], 1)
        elif w[0] == "wout":
            use(0, "down", L1A, w[1])
        elif w[0] == "turn_own":
            use(1, "turn", L1A, w[1])
        elif w[0] == "turn":
            use(0, "turn", L1B, w[1])
    mlp(1, L1B, A2)

    def attention(a, l, nxt):
        def qkv(c):
            for k in range(2):
                use(7, "qk", a, c, k)
            use(7, "v", a, c)
        qkv(0)
        for s, hooks in attention_steps(a, nxt):
            if s < NI * CHUNKS:
                use(s % 3, "s", a, s)
            if 0 <= s - 2 < NI * CHUNKS:
                use(3 + s % 2, "pt", a, s - 2)
            i = s - 3
            if 0 <= i < NI * CHUNKS:
                if i % NI == 0:
                    use(5, "o", a, i // NI, 0)
                if i % NI == IMGS * len(HEAD_GROUPS[0]):
                    use(6, "o", a, i // NI, 1)
            for what, c in hooks:
                if what == "qkv":
                    qkv(c)
                if what == "turn_own":
                    use(7, "turn", l, c)
                if what == "turn_o":
                    for im in range(IMGS):
                        use(7, "turn_o", a, c, im)
                if what == "turn_n":
                    use(7, "turn_n", a, c)
                if what == "proj":
                    use(7, "down", l, c)
                if what == "turn":
                    use(7, "turn", nxt, c)

    attention(0, A2, F2)
    for c, _ in chunks_of(F2):
        for k in range(HT):
            use(k + 3 * (c % 2), "qup", c, k)
    for k in range(2):
        use(6 + k, "gamma", 0, k)
    for c, _ in chunks_of(F2):
        use(c, "down", F2, c)
    for k in range(2):
        use(6 + k, "gamma", 1, k)
    for c in range(CHUNKS):
        use(6 + c % 2, "turn", A3, c)
    attention(1, A3, MO)
    for s in range(NE * CHUNKS + 1):
        if s < NE * CHUNKS:
            for k in range(HT):
                use(k, "eup", s, k)
        if s == 1:
            use(6, "gate")
        if s >= 1:
            use(3 + s % 3, "edown", s - 1)
    out, count = {}, [0] * 8
    for key, bank in seq:
        assert key not in out, key
        out[key] = (bank, count[bank])
        count[bank] += 1
    return out


def conv_order():
    return [("win", 0), ("turn_own", 3), ("win", 1), ("taps", "m0"), ("taps", "m1"), ("loc", "m0"), ("win", 2), ("taps", "s0"),
            ("loc", "m1"), ("win", 3), ("taps", "m2"), ("loc", "s0"), ("mix", 0), ("taps", "m3"), ("mix", 1),
            ("turn_m", 0), ("taps", "s1"), ("wout", 0), ("turn_m", 1), ("loc", "m2"), ("wout", 1),
            ("loc", "m3"), ("turn", 0), ("loc", "s1"), ("mix", 2), ("turn", 1), ("mix", 3),
            ("turn_m", 2), ("wout", 2), ("turn_m", 3), ("wout", 3), ("turn", 2)]


def hybrid_kernel(nc, a, out):
    uses = plan_banks()
    ctx = ExitStack()
    with ctx:
        def sb(name, shape, dt=F32):
            return ctx.enter_context(nc.sbuf_tensor(name, shape, dt))

        def sem(name):
            return ctx.enter_context(nc.semaphore(name))

        bank = [ctx.enter_context(nc.psum_tensor(f"bank{i}", [P, 512], F32)) for i in range(8)]

        at_a, wa = spots(CONST_A)
        at_b, wb = spots(CONST_B)
        const_a, const_b = sb("const_a", [P, wa]), sb("const_b", [P, wb])
        ca = lambda n: const_a[:, at_a[n][0]:at_a[n][1]]
        cb = lambda n: const_b[:, at_b[n][0]:at_b[n][1]]
        ident = ca("ident")
        nmask, delta = ca("nmask"), ca("delta")
        dft = ca("dft").rearrange("p (h n) -> p h n", h=HALVES)
        hmask = ca("hmask")
        idft = cb("idft").rearrange("p (k t) -> p k t", k=KT)
        mix = cb("mix").rearrange("p (h t) -> p h t", h=HALVES)
        ident_b, mask_b = sb("ident_b", [P, P], BF16), sb("mask_b", [P, P], BF16)
        ones = sb("ones", [P, P])

        n1g, n1b, n1b16 = sb("n1g", [P, 1]), sb("n1b", [P, 1]), sb("n1b16", [P, 1])
        affine = {l: (sb(f"g{l}", [C, 1]), sb(f"b{l}", [C, 1])) for l in (L0B, L1A, L1B)}
        mlp_w1 = [sb(f"mlp_w1_{m}", [C, HID]) for m in range(2)]
        mlp_b1 = [sb(f"mlp_b1_{m}", [P, HT]) for m in range(2)]
        mlp_w2 = [sb(f"mlp_w2_{m}", [P, HT, C]) for m in range(2)]
        bias_row = {l: sb(f"bias_row{l}", [P, C]) for l in (L0B, L1A, L1B, F2, A3)}
        w_in = sb("w_in", [C, INNER])
        b_in = [sb("b_in0", [P, 1]), sb("b_in1", [IN2, 1])]
        kcol = [sb("kcol0", [P, 9]), sb("kcol1", [P, 9])]
        on_g, on_b = sb("on_g", [C, 2]), sb("on_b", [C, 2])
        w_out = sb("w_out", [C, 2, C])
        tap_diag = sb("tap_diag", [P, 2, PE_TAPS, P])
        w_qkv = [sb(f"w_qkv{i}", [C, 3 * C]) for i in range(2)]
        w_proj = [sb(f"w_proj{i}", [C, C]) for i in range(2)]
        qw1, qw2 = sb("qw1", [P, HT, C]), sb("qw2", [C, HID])
        qb1 = sb("qb1", [P, HT])
        qw1_t, qw2_t = sb("qw1_t", [C, HID]), sb("qw2_t", [P, HT, C])
        sign1, sign2 = sb("sign1", [C, HID]), sb("sign2", [P, HT, C])
        qsum, qmean = sb("qsum", [P, 2, QG]), sb("qmean", [P, 2, QG])
        gate_w, gate_b = sb("gate_w", [C, NE]), sb("gate_b", [P, NE])
        e_w1, e_w2 = sb("e_w1", [C, NE, HID]), sb("e_w2", [P, NE, HT, C])
        e_b1, e_b2 = sb("e_b1", [P, NE, HT]), sb("e_b2", [P, NE, C])

        X = sb("X", [P, TILES, C])
        stats, moments = sb("stats", [P, 9, TILES, 6]), sb("moments", [P, 9, TILES, 2])
        rstd, exponent = sb("rstd", [P, 9, TILES]), sb("exponent", [P, CT])
        normed = [sb(f"normed{i}", [P, TILES, C]) for i in range(2)]
        normed_t = [sb(f"normed_t{i}", [C, B * TOK]) for i in range(2)]
        hidden = sb("hidden", [P, 2, HT, CN])
        normed_s = hidden[:, :, :, :].rearrange("p a k n -> p (a k n)")[:, 0:TILES * P].rearrange(
            "p (t c) -> p t c", c=P)
        arena = sb("arena", [P, 24600])

        class Arena:
            def __init__(self):
                self.at = 0

            def __call__(self, shape, rows=P):
                n = int(np.prod(shape))
                assert self.at + n <= 24600, self.at + n
                v = arena[0:rows, self.at:self.at + n]
                self.at += n
                if len(shape) == 1:
                    return v
                names = "abcdef"[:len(shape)]
                return v.rearrange(f"p ({' '.join(names)}) -> p {' '.join(names)}",
                                   **{x: s for x, s in zip(names, shape)})

        ar = Arena()
        spec_w = [ar([POS, BINS]) for _ in range(2)]
        spec_x = [ar([POS, GB, B]) for _ in range(2)]
        spec_f = ar([B, 2, POS])
        spec_o = ar([BS, POS, 2], 2 * 32)
        spec_ot = ar([KT, BS, 2 * 32], KROWS)
        xs = normed[0][:, :, :]
        ar = Arena()
        pad = [ar([LEAD + B * IMG + 1]), ar([LEAD + B // 2 * IMG + 1])]
        conv = [ar([B, TOK]), ar([B // 2, TOK])]
        loc = ar([HALVES, B, INNER])
        mixed = ar([TILES, INNER])
        mixed_t = [ar([B * TOK], C), ar([B * TOK], C)]
        conv_end = ar.at
        ar = Arena()
        q_raw, q_heads = ar([2, CN], C), ar([2, NH, CN], C)
        k_t = ar([B * TOK], C)
        probs, probs_t = ar([3, 384]), ar([3, 384])
        o_raw = ar([2, 2, CN])
        o_norm, o_t = ar([2, CT, C]), ar([2, CN], C)
        o_rec = ar([2, CT, NH])
        assert ar.at <= 20500
        ar.at = max(ar.at, conv_end)
        v_sb = ar([TILES, NH, 32])
        ar = Arena()
        NQ = QIMGS * TOK
        qy1, qh = ar([HT, NQ]), ar([HT, NQ])
        qy2 = ar([HALVES * QIMGS, C])
        nmax = sb("nmax", [P, 3, 2])
        qmax, qmax1, qrec, qdiag, qscale = (sb("qmax", [P, 2, QG]), sb("qmax1", [QG, 2]), sb("qrec", [QG, 2]),
                                            sb("qdiag", [QG, 2, QG]), sb("qscale", [P, 2, QG]))
        ar = Arena()
        score, gate1 = ar([TILES, NE]), ar([TILES])
        cmp_a, cmp_b = ar([TILES, NE * NE]), ar([TILES, NE * NE])
        bias_sum, bias_term = ar([TILES, C]), ar([TILES, C])
        gates = sb("gates", [P, TILES, NE])

        bank_filled = [sem(f"bank{i}_filled") for i in range(8)]
        bank_drained = [sem(f"bank{i}_drained") for i in range(8)]
        x_loaded = [sem(f"x_loaded{c}") for c in range(CHUNKS)]
        const_a_loaded, const_b_loaded = sem("const_a_loaded"), sem("const_b_loaded")
        spec_w_loaded, n1_loaded = sem("spec_w_loaded"), sem("n1_loaded")
        l0_loaded, l1_loaded, l2_loaded, l3_loaded = (sem(f"l{i}_loaded") for i in range(4))
        q_loaded, stored = sem("q_loaded"), sem("stored")
        stats_ready, moments_ready = sem("stats_ready"), sem("moments_ready")
        eps_added = sem("eps_added")
        rstd_ready, normed_ready = sem("rstd_ready"), sem("normed_ready")
        spec_zero, n1_zero, gap_zero = sem("spec_zero"), sem("n1_zero"), sem("gap_zero")
        spec_x_rows, spec_w_rows = sem("spec_x_rows"), sem("spec_w_rows")
        dc_ready, spec_x_dve, spec_x_act = sem("dc_ready"), sem("spec_x_dve"), sem("spec_x_act")
        x_plus_xs, bias_added = sem("x_plus_xs"), sem("bias_added")
        ones_ready, bf_ready = sem("ones_ready"), sem("bf_ready")
        sign_copied, sign_centred, sign_ready = sem("sign_copied"), sem("sign_centred"), sem("sign_ready")
        diag_ready, pad_zero, conv_step = sem("diag_ready"), sem("pad_zero"), sem("conv_step")
        v_zero, v_pad_ready = sem("v_zero"), sem("v_pad_ready")
        q_heads_ready, o_rec_ready = sem("q_heads_ready"), sem("o_rec_ready")
        bias_sum_step, bias_sum_added = sem("bias_sum_step"), sem("bias_sum_added")
        nmax_ready = sem("nmax_ready")
        qmax_ready, qchain, qclip, qh_ready, qclip2 = (sem("qmax_ready"), sem("qchain"), sem("qclip"),
                                                       sem("qh_ready"), sem("qclip2"))
        gate_step, gate_exp_ready = sem("gate_step"), sem("gate_exp_ready")

        def pe_bank(pe, *key):
            k, n = uses[key]
            if n:
                pe.wait_ge(bank_drained[k], n)
            return bank[k], bank_filled[k]

        def read_bank(eng, *key):
            k, n = uses[key]
            eng.wait_ge(bank_filled[k], n + 1)
            return bank[k], bank_drained[k]

        def landed(eng, *key):
            k, n = uses[key]
            eng.wait_ge(bank_drained[k], n + 1)

        tok = lambda t, n=P: slice(P * t, P * t + n)
        ctok = lambda c, n=CN: slice(CN * c, CN * c + n)
        SPEC_ALL = [(g, ri, n) for g in range(2) for ri in range(2) for n in range(GB)]
        SPEC_DVE, SPEC_ACT = SPEC_ALL[:11], SPEC_ALL[11:]
        BIASED = (L0B, L1A, L1B, A3)
        BIAS_SEQ = [(L0B, c) for c in range(CHUNKS)] + [k for k in LN_SEQ if k[0] in BIASED[1:]]
        GATE_STEPS = 15
        bias_no = lambda l, c: BIAS_SEQ.index((l, c)) + 1
        CONV_STEPS = IMGS * (len(TAPS) - PE_TAPS - 1)
        HALF = POS // 2

        def unit_chunks(u):
            return (int(u[1]),) if u[0] == "m" else (2 * int(u[1]), 2 * int(u[1]) + 1)

        def window(k, image, dy, dx):
            at = LEAD + IMG * image + dy * PW + dx
            return pad[k][:, at:at + HH * PW].rearrange("p (y x) -> p y x", x=PW)[:, :, 0:WW]

        def spec_copy(g, ri, n, ph):
            rows = slice(64 * g, 64 * g + GR)
            pos = slice(HALF * ph, HALF * ph + HALF)
            return (spec_x[g][64 * ri:64 * ri + GR, pos, n, :],
                    spec_f[rows, :, ri, pos].rearrange("p b q -> p q b"), nmask[rows, n:n + 1])

        def relu_spec(n):
            q = min(PPB, POS - PPB * n)
            return (spec_o[0:64, :, PPB * n:PPB * n + q, :].rearrange("p o q r -> p q o r"),
                    bank[n][0:64, 0:q * BINS].rearrange("p (q o r) -> p q o r", q=q, o=BS))

        def inv_out(h, j):
            return xs.rearrange("p (b h) (n o) -> p h o n b", h=HALVES, o=BS)[:, h, OH * j:OH * j + OH]

        SPEC_W_DMAS, L0_DMAS, L1_DMAS, L2_DMAS, Q_DMAS, L3_DMAS = 4, 6, 18, 5, 4, 12
        col = lambda v: v.rearrange("(p o) -> p o", o=1)
        row = lambda v: v.rearrange("(o c) -> o c", o=1).broadcast_to([P, C])

        ctx.enter_context(nc.allow_non_contiguous_dma(reason="biases and scales, a channel a partition"))
        block = ctx.enter_context(nc.Block())

        @block.sync
        def _(sp):
            x_d = a["x"].rearrange("b h w c -> (b h w) c").rearrange("(t p) c -> p t c", p=P)
            o_d = out.rearrange("b h w c -> (b h w) c").rearrange("(t p) c -> p t c", p=P)
            for c in range(CHUNKS):
                sp.dma_start(X[:, CT * c:CT * c + CT, :], x_d[:, CT * c:CT * c + CT, :]).then_inc(x_loaded[c], 16)
                if c == 0:
                    sp.dma_start(const_a[:, :], a["const_a"]).then_inc(const_a_loaded, 16)
                    sp.wait_ge(n1_zero, 2)
                    for v, t in ((a["L0_conv_norm1_w"], n1g), (a["L0_conv_norm1_b"], n1b)):
                        for g in range(2):
                            sp.dma_start(t[64 * g:64 * g + GR, :], col(v[GR * g:GR * g + GR])).then_inc(n1_loaded, 16)
            w_d = a["L0_conv_w1"].rearrange("h w n i o r -> (n i) (h w) (o r)")
            b_d = a["L0_conv_b1"].rearrange("h w n o r -> n (h w) (o r)")
            sp.wait_ge(spec_zero, 2)
            for g in range(2):
                sp.dma_start(spec_w[g][0:GR], w_d[GR * g:GR * g + GR]).then_inc(spec_w_loaded, 16)
                sp.dma_start(spec_w[g][GR:GR + GB], b_d[GB * g:GB * g + GB]).then_inc(spec_w_loaded, 16)
            sp.dma_start(qw1[:, :, :], a["L2_ffn_W1"].rearrange("(k p) c -> p k c", p=P)).then_inc(q_loaded, 16)
            sp.dma_start(qw2[:, :], a["L2_ffn_W2"]).then_inc(q_loaded, 16)
            sp.dma_start(qb1[:, :], a["L2_ffn_b1"].rearrange("(k p) -> p k", p=P)).then_inc(q_loaded, 16)
            sp.dma_start(bias_row[F2][:, :], row(a["L2_ffn_b2"])).then_inc(q_loaded, 16)
            sp.dma_start(const_b[:, :], a["const_b"]).then_inc(const_b_loaded, 16)
            sp.dma_start(mlp_w1[0][:, :], a["L0_conv_mlp_w1"]).then_inc(l0_loaded, 16)
            sp.dma_start(mlp_b1[0][:, :], a["L0_conv_mlp_b1"].rearrange("(k p) -> p k", p=P)).then_inc(l0_loaded, 16)
            sp.dma_start(mlp_w2[0][:, :, :], a["L0_conv_mlp_w2"].rearrange("(k p) c -> p k c", p=P)).then_inc(l0_loaded, 16)
            sp.dma_start(bias_row[L0B][:, :], row(a["L0_conv_mlp_b2"])).then_inc(l0_loaded, 16)
            sp.dma_start(affine[L0B][0][:, :], col(a["L0_conv_norm2_w"])).then_inc(l0_loaded, 16)
            sp.dma_start(affine[L0B][1][:, :], col(a["L0_conv_norm2_b"])).then_inc(l0_loaded, 16)
            l1 = [(affine[L1A][0][:, :], col(a["L1_conv_n1_g"])), (affine[L1A][1][:, :], col(a["L1_conv_n1_b"])),
                  (affine[L1B][0][:, :], col(a["L1_conv_n2_g"])), (affine[L1B][1][:, :], col(a["L1_conv_n2_b"])),
                  (w_in[:, :], a["L1_conv_w_in"]),
                  (b_in[0][:, :], col(a["L1_conv_b_in"][0:P])), (b_in[1][:, :], col(a["L1_conv_b_in"][P:INNER])),
                  (on_g[:, :], a["L1_conv_on_g"].rearrange("(k p) -> p k", p=C)),
                  (on_b[:, :], a["L1_conv_on_b"].rearrange("(k p) -> p k", p=C)),
                  (w_out[:, :, :], a["L1_conv_w_out"].rearrange("(k p) c -> p k c", p=C)),
                  (bias_row[L1A][:, :], row(a["L1_conv_b_out"])),
                  (mlp_w1[1][:, :], a["L1_conv_w1"]),
                  (mlp_b1[1][:, :], a["L1_conv_b1"].rearrange("(k p) -> p k", p=P)),
                  (mlp_w2[1][:, :, :], a["L1_conv_w2"].rearrange("(k p) c -> p k c", p=P)),
                  (bias_row[L1B][:, :], row(a["L1_conv_b2"]))]
            k_d = a["L1_conv_k_conv"].rearrange("y x o c -> c (y x o)")
            l1 += [(kcol[0][:, :], k_d[0:P]), (kcol[1][0:IN2, :], k_d[P:INNER]), (kcol[1][IN2:P, :], k_d[P:INNER])]
            for dst, src in l1:
                sp.dma_start(dst, src).then_inc(l1_loaded, 16)
            for i, name in enumerate(("L2_attn_w_attn", "L3_attn_W_qkv")):
                sp.dma_start(w_qkv[i][:, :], a[name]).then_inc(l2_loaded, 16)
            for i, name in enumerate(("L2_attn_w_proj", "L3_attn_W_proj")):
                sp.dma_start(w_proj[i][:, :], a[name]).then_inc(l2_loaded, 16)
            sp.dma_start(bias_row[A3][:, :], row(a["L3_attn_b_proj"])).then_inc(l2_loaded, 16)
            sp.dma_start(gate_w[:, :], a["L3_ffn_gate_w"]).then_inc(l3_loaded, 16)
            sp.dma_start(gate_b[:, :], a["L3_ffn_gate_b"].rearrange("(o e) -> o e", o=1).broadcast_to([P, NE])
                         ).then_inc(l3_loaded, 16)
            for e in range(NE):
                sp.dma_start(e_w1[:, e, :], a["L3_ffn_w1"][e]).then_inc(l3_loaded, 16)
                sp.dma_start(e_w2[:, e], a["L3_ffn_w2"][e].rearrange("(k p) c -> p k c", p=P)).then_inc(l3_loaded, 16)
            sp.dma_start(e_b1[:, :, :], a["L3_ffn_b1"].rearrange("e (k p) -> p e k", p=P)).then_inc(l3_loaded, 16)
            sp.dma_start(e_b2[:, :, :].rearrange("p e c -> p (e c)"),
                         a["L3_ffn_b2"].rearrange("(o e) c -> o (e c)", o=1).broadcast_to([P, NE * C])).then_inc(l3_loaded, 16)
            for c in range(CHUNKS):
                landed(sp, "edown", NE * c + NE - 1)
                sp.dma_start(o_d[:, CT * c:CT * c + CT, :], X[:, CT * c:CT * c + CT, :]).then_inc(stored, 16)
            sp.wait_ge(stored, 16 * CHUNKS)

        @block.tensor
        def _(pe):
            def turn(l, c, src, width=CT):
                pe.wait_ge(normed_ready, LN_NO[l, c])
                ps, filled = pe_bank(pe, "turn", l, c)
                for t in range(width):
                    mm = nc.tensor.transpose(ps[0:C, tok(t)], src[:, CT * c + t, :], ident)
                mm.then_inc(filled, 1)

            def down(l, c, src, w, width=CT):
                ps, filled = pe_bank(pe, "down", l, c)
                for t in range(width):
                    for k in range(len(src)):
                        mm = nc.tensor.matmul(ps[:, C * t:C * t + C], src[k][:, tok(t)], w[k],
                                              start=(k == 0), stop=(k == len(src) - 1))
                mm.then_inc(filled, 1)

            def mlp(m, l, nxt):
                for s in range(CHUNKS + 1):
                    if s < CHUNKS:
                        landed(pe, "turn", l, s)
                        for k in range(HT):
                            ps, filled = pe_bank(pe, "up", m, s, k)
                            nc.tensor.matmul(ps[:, :], mlp_w1[m][:, tok(k)], normed_t[l % 2][:, ctok(s)],
                                             start=True, stop=True).then_inc(filled, 1)
                    if s == 0:
                        turn(l, CHUNKS - 1, normed[l % 2])
                    if s >= 1:
                        for k in range(HT):
                            landed(pe, "up", m, s - 1, k)
                        down(l, s - 1, [hidden[:, (s - 1) % 2, k, :] for k in range(HT)],
                             [mlp_w2[m][:, k, :] for k in range(HT)])
                    if s >= 2:
                        turn(nxt, s - 2, normed[nxt % 2])

            pe.wait_ge(const_a_loaded, 16)
            pe.wait_ge(gap_zero, 1)
            for b in range(B):
                pe.wait_ge(normed_ready, LN_NO[L0A, b // IMGS])
                ps, filled = pe_bank(pe, "dft", b)
                for h in range(HALVES):
                    mm = nc.tensor.matmul(ps[0:64 + GR, 0:2 * POS], normed_s[:, HALVES * b + h, 0:64 + GR],
                                          dft[:, h, :], start=(h == 0), stop=(h == HALVES - 1))
                mm.then_inc(filled, 1)
            pe.wait_ge(spec_w_loaded, 16 * SPEC_W_DMAS)
            pe.wait_ge(spec_w_rows, 4)
            for p in range(POS):
                if p % (POS // 2) == 0:
                    pe.wait_ge(spec_x_dve, len(SPEC_DVE) * (1 + p // (POS // 2)))
                    pe.wait_ge(spec_x_act, len(SPEC_ACT) * (1 + p // (POS // 2)))
                if p % PPB == 0:
                    ps, filled = pe_bank(pe, "spec", p // PPB)
                for g in range(2):
                    mm = nc.tensor.matmul(ps[32 * g:32 * g + 32, BINS * (p % PPB):BINS * (p % PPB) + BINS],
                                          spec_x[g][0:64 + GR, p, :, :].rearrange("p n b -> p (n b)"),
                                          spec_w[g][0:64 + GR, p, :], start=True, stop=True)
                if p % PPB == PPB - 1 or p == POS - 1:
                    mm.then_inc(filled, 1)
            for k in range(KT):
                for n in range((KP * (k + 1) - 1) // PPB + 1):
                    landed(pe, "spec", n)
                for j in range(2):
                    ps, filled = pe_bank(pe, "spec_t", k, j)
                    for o in range(OH):
                        oo = OH * j + o
                        mm = nc.tensor.transpose(ps[0:KROWS, 64 * o:64 * o + 64],
                                                 spec_o[:, oo, KP * k:KP * k + KP, :].rearrange("p q r -> p (q r)"),
                                                 ident[0:64, 0:64])
                    mm.then_inc(filled, 1)
            pe.wait_ge(const_b_loaded, 16)
            for h in range(HALVES):
                for j in range(2):
                    ps, filled = pe_bank(pe, "inv", 2 * h + j)
                    for k in range(KT):
                        landed(pe, "spec_t", k, j)
                        mm = nc.tensor.matmul(ps[:, 0:64 * OH], idft[0:KROWS, k, tok(h)],
                                              spec_ot[:, k, OH * j:OH * j + OH, :].rearrange("p o m -> p (o m)"),
                                              start=(k == 0), stop=(k == KT - 1))
                    mm.then_inc(filled, 1)
            pe.wait_ge(q_loaded, 16 * Q_DMAS)
            ps, filled = pe_bank(pe, "signprep", 0)
            for k in range(HT):
                mm = nc.tensor.transpose(ps[0:C, tok(k)], qw1[:, k, :], ident)
            mm.then_inc(filled, 1)
            ps, filled = pe_bank(pe, "signprep", 1)
            for k in range(HT):
                mm = nc.tensor.transpose(ps[:, C * k:C * k + C], qw2[:, tok(k)], ident[0:C, 0:C])
            mm.then_inc(filled, 1)
            for c in range(CHUNKS - 1):
                turn(L0B, c, normed[L0B % 2])
            pe.wait_ge(ones_ready, 1)
            landed(pe, "signprep", 0)
            landed(pe, "signprep", 1)
            ps, filled = pe_bank(pe, "signprep", 2)
            nc.tensor.matmul(ps[:, 0:QG], ones[0:C, :], qsum[0:C, 0, :], start=True, stop=True).then_inc(filled, 1)
            ps, filled = pe_bank(pe, "signprep", 3)
            nc.tensor.matmul(ps[:, 0:QG], ones[:, :], qsum[:, 1, :], start=True, stop=True).then_inc(filled, 1)
            pe.wait_ge(l0_loaded, 16 * L0_DMAS)
            mlp(0, L0B, L1A)

            pe.wait_ge(l1_loaded, 16 * L1_DMAS)
            for what, x in conv_order():
                if what == "win":
                    landed(pe, "turn", L1A, x)
                    for k, (lo, n) in enumerate(((0, P), (P, IN2))):
                        ps, filled = pe_bank(pe, "win", x, k)
                        nc.tensor.matmul(ps[0:n, :], w_in[:, lo:lo + n], normed_t[L1A % 2][:, ctok(x)],
                                         start=True, stop=True).then_inc(filled, 1)
                elif what == "taps":
                    k, first = int(x[0] == "s"), IMGS * int(x[1])
                    pe.wait_ge(diag_ready, 2 * PE_TAPS)
                    pe.wait_ge(pad_zero, 2)
                    for c in unit_chunks(x):
                        landed(pe, "win", c, k)
                    for im in range(IMGS):
                        ps, filled = pe_bank(pe, "taps", x, im)
                        for n in range(PE_TAPS):
                            dy, dx = TAPS[n]
                            mm = nc.tensor.matmul(ps[:, 0:TOK], tap_diag[:, k, n, :], window(k, first + im, dy, dx),
                                                  start=(n == 0), stop=(n == PE_TAPS - 1))
                        mm.then_inc(filled, 1)
                elif what == "loc":
                    k, first = int(x[0] == "s"), IMGS * int(x[1])
                    pe.wait_ge(conv_step, CONV_STEPS * (UNITS.index(x) + 1))
                    ps, filled = pe_bank(pe, "loc", x)
                    for im in range(IMGS):
                        for h in range(HALVES):
                            mm = nc.tensor.transpose(ps[:, tok(HALVES * im + h)], conv[k][:, first + im, tok(h)],
                                                     ident)
                    mm.then_inc(filled, 1)
                elif what == "mix":
                    landed(pe, "loc", f"m{x}")
                    landed(pe, "loc", f"s{x // 2}")
                    for ho in range(HALVES):
                        ps, filled = pe_bank(pe, "mix", x, ho)
                        for hi in range(HALVES):
                            mm = nc.tensor.matmul(
                                ps[:, 0:IMGS * INNER], mix[:, hi, tok(ho)],
                                loc[:, hi, IMGS * x:IMGS * x + IMGS, :].rearrange("p b c -> p (b c)"),
                                start=(hi == 0), stop=(hi == HALVES - 1))
                        mm.then_inc(filled, 1)
                elif what == "turn_m":
                    pe.wait_ge(normed_ready, LN_NO[L1M, x])
                    for k in range(2):
                        ps, filled = pe_bank(pe, "turn_m", x, k)
                        for t in range(CT):
                            mm = nc.tensor.transpose(ps[0:C, tok(t)], mixed[:, CT * x + t, C * k:C * k + C], ident)
                        mm.then_inc(filled, 1)
                elif what == "wout":
                    landed(pe, "turn_m", x, 0)
                    landed(pe, "turn_m", x, 1)
                    down(L1A, x, [mixed_t[k][:, ctok(x)] for k in range(2)], [w_out[:, k, :] for k in range(2)])
                elif what == "turn_own":
                    turn(L1A, x, normed[L1A % 2])
                elif what == "turn":
                    turn(L1B, x, normed[L1B % 2])
            mlp(1, L1B, A2)

            def attention(a, l, nxt):
                def qkv(c):
                    landed(pe, "turn", l, c)
                    for k in range(2):
                        ps, filled = pe_bank(pe, "qk", a, c, k)
                        nc.tensor.matmul(ps[0:C, :], w_qkv[a][:, C * k:C * k + C], normed_t[l % 2][:, ctok(c)],
                                         start=True, stop=True).then_inc(filled, 1)
                    ps, filled = pe_bank(pe, "v", a, c)
                    for t in range(CT):
                        mm = nc.tensor.matmul(ps[:, C * t:C * t + C], normed_t[l % 2][:, tok(CT * c + t)],
                                              w_qkv[a][:, 2 * C:3 * C], start=True, stop=True)
                    mm.then_inc(filled, 1)

                pe.wait_ge(l2_loaded, 16 * L2_DMAS)
                qkv(0)
                for s, hooks in attention_steps(a, nxt):
                    if s < NI * CHUNKS:
                        c, (im, h) = s // NI, ITEMS[s % NI]
                        if s % NI == 0:
                            landed(pe, "qk", a, c, 1)
                            pe.wait_ge(q_heads_ready, NH * (CHUNKS * a + c) + NH)
                        t0 = CN * c + TOK * im
                        ps, filled = pe_bank(pe, "s", a, s)
                        for n, (q0, k0) in enumerate(((0, 0), (P, 0), (P, P))):
                            diagonal = q0 == k0
                            if diagonal:
                                nc.tensor.matmul(ps[:, tok(n)], ident_b[:, :], mask_b[:, :], start=True, stop=False)
                            mm = nc.tensor.matmul(ps[:, tok(n)],
                                                  q_heads[:, c % 2, h, TOK * im + q0:TOK * im + q0 + P],
                                                  k_t[:, t0 + k0:t0 + k0 + P], start=not diagonal, stop=True)
                        mm.then_inc(filled, 1)
                    i = s - 2
                    if 0 <= i < NI * CHUNKS:
                        landed(pe, "s", a, i)
                        ps, filled = pe_bank(pe, "pt", a, i)
                        for k in range(3):
                            mm = nc.tensor.transpose(ps[:, tok(k)], probs[:, i % 3, tok(k)], ident)
                        mm.then_inc(filled, 1)
                    i = s - 3
                    if 0 <= i < NI * CHUNKS:
                        c, (im, h) = i // NI, ITEMS[i % NI]
                        g, r = int(h >= 4), 32 * (h % 4)
                        if i % NI in (0, IMGS * len(HEAD_GROUPS[0])):
                            o_bank = pe_bank(pe, "o", a, c, g)
                        if i % NI == 0:
                            landed(pe, "v", a, c)
                        ps, filled = o_bank
                        landed(pe, "pt", a, i)
                        t0 = CT * c + HALVES * im
                        nc.tensor.matmul(ps[r:r + 32, TOK * im:TOK * im + TOK], v_sb[:, t0, h, :],
                                         probs_t[:, i % 3, 0:TOK], start=True, stop=False)
                        mm = nc.tensor.matmul(ps[r:r + 32, TOK * im + P:TOK * im + TOK], v_sb[:, t0 + 1, h, :],
                                              probs_t[:, i % 3, TOK:384], start=False, stop=True)
                        if i % NI in (IMGS * len(HEAD_GROUPS[0]) - 1, NI - 1):
                            mm.then_inc(filled, 1)
                    for what, c in hooks:
                        if what == "qkv":
                            qkv(c)
                        if what == "turn_own":
                            turn(l, c, normed[l % 2])
                        if what == "turn_o":
                            landed(pe, "o", a, c, 0)
                            landed(pe, "o", a, c, 1)
                            for im in range(IMGS):
                                ps, filled = pe_bank(pe, "turn_o", a, c, im)
                                for t in range(HALVES):
                                    for g, heads in enumerate(HEAD_GROUPS):
                                        rows, lo = 32 * len(heads), 32 * (NH * t + heads[0])
                                        mm = nc.tensor.transpose(ps[:, lo:lo + rows],
                                                                 o_raw[0:rows, c % 2, g, tok(HALVES * im + t)],
                                                                 ident[0:rows, 0:rows])
                                mm.then_inc(filled, 1)
                        if what == "turn_n":
                            for im in range(IMGS):
                                landed(pe, "turn_o", a, c, im)
                            ps, filled = pe_bank(pe, "turn_n", a, c)
                            for t in range(CT):
                                mm = nc.tensor.transpose(ps[0:C, tok(t)], o_norm[:, c % 2, t, :], ident)
                            mm.then_inc(filled, 1)
                        if what == "proj":
                            landed(pe, "turn_n", a, c)
                            down(l, c, [o_t[:, c % 2, :]], [w_proj[a][:, :]])
                        if what == "turn":
                            turn(nxt, c, normed[nxt % 2], dict(chunks_of(nxt))[c])

            attention(0, A2, F2)

            pe.wait_ge(sign_ready, 4)
            for c, w in chunks_of(F2):
                landed(pe, "turn", F2, c)
                for k in range(HT):
                    ps, filled = pe_bank(pe, "qup", c, k)
                    nc.tensor.matmul(ps[:, 0:P * w], sign1[:, tok(k)], normed_t[F2 % 2][:, ctok(c, P * w)],
                                     start=True, stop=True).then_inc(filled, 1)

            def gamma(n):
                pe.wait_ge(qmax_ready, QG * (n + 1))
                ps, filled = pe_bank(pe, "gamma", n, 0)
                nc.tensor.transpose(ps[0:QG, 0:P], qmax[:, n, :], ident).then_inc(filled, 1)
                pe.wait_ge(qchain, 3 * n + 3)
                ps, filled = pe_bank(pe, "gamma", n, 1)
                nc.tensor.matmul(ps[:, 0:QG], ones[0:QG, :], qdiag[:, n, :], start=True, stop=True).then_inc(filled, 1)

            gamma(0)
            for c, w in chunks_of(F2):
                pe.wait_ge(qh_ready, min(IMGS * c + IMGS, QG))
                down(F2, c, [qh[:, k, ctok(c, P * w)] for k in range(HT)], [sign2[:, k, :] for k in range(HT)], w)
            gamma(1)
            for c in range(CHUNKS):
                turn(A3, c, normed[A3 % 2])

            attention(1, A3, MO)

            pe.wait_ge(l3_loaded, 16 * L3_DMAS)
            for s in range(NE * CHUNKS + 1):
                if s < NE * CHUNKS:
                    c, e = s // NE, s % NE
                    landed(pe, "turn", MO, c)
                    for k in range(HT):
                        ps, filled = pe_bank(pe, "eup", s, k)
                        nc.tensor.matmul(ps[:, :], e_w1[:, e, tok(k)], normed_t[MO % 2][:, ctok(c)],
                                         start=True, stop=True).then_inc(filled, 1)
                if s == 1:
                    for c in range(CHUNKS):
                        landed(pe, "turn", MO, c)
                    ps, filled = pe_bank(pe, "gate")
                    for t in range(TILES):
                        mm = nc.tensor.matmul(ps[:, NE * t:NE * t + NE], normed_t[MO % 2][:, tok(t)], gate_w[:, :],
                                              start=True, stop=True)
                    mm.then_inc(filled, 1)
                if s >= 1:
                    i = s - 1
                    ps, filled = pe_bank(pe, "edown", i)
                    for k in range(HT):
                        landed(pe, "eup", i, k)
                    for t in range(CT):
                        for k in range(HT):
                            mm = nc.tensor.matmul(ps[:, C * t:C * t + C], hidden[:, i % 2, k, tok(t)],
                                                  e_w2[:, i % NE, k, :], start=(k == 0), stop=(k == HT - 1))
                    mm.then_inc(filled, 1)

        @block.scalar
        def _(act):
            def turned(l, c, width=CT):
                ps, drained = read_bank(act, "turn", l, c)
                dst = normed_t[l % 2][:, ctok(c, P * width)]
                if l in affine:
                    g, b = affine[l]
                    nc.scalar.activation(dst, ps[0:C, 0:P * width], ACT.Identity, bias=b[:, :],
                                         scale=g[:, :]).then_inc(drained, 1)
                else:
                    nc.scalar.activation(dst, ps[0:C, 0:P * width], ACT.Copy).then_inc(drained, 1)

            def mlp(m, l, nxt):
                for s in range(CHUNKS + 1):
                    if s < CHUNKS:
                        for k in range(HT):
                            ps, drained = read_bank(act, "up", m, s, k)
                            nc.scalar.activation(hidden[:, s % 2, k, :], ps[:, :], ACT.Gelu,
                                                 bias=mlp_b1[m][:, k:k + 1]).then_inc(drained, 1)
                    if s == 0:
                        turned(l, CHUNKS - 1)
                    if s >= 2:
                        turned(nxt, s - 2)

            act.wait_ge(const_a_loaded, 16)
            nc.scalar.activation(spec_x[0][32:64].rearrange("p q n b -> p q (n b)"),
                                 delta[32:64, :].unsqueeze(1).broadcast_to([32, POS, GB * B]),
                                 ACT.Copy).then_inc(spec_x_rows, 1)
            act.wait_ge(n1_loaded, 16 * 4)
            for b in range(B):
                ps, drained = read_bank(act, "dft", b)
                nc.scalar.activation(spec_f[0:64 + GR, b].rearrange("p r q -> p (r q)"), ps[0:64 + GR, 0:2 * POS],
                                     ACT.Identity, scale=n1g[0:64 + GR, :]).then_inc(drained, 1)
            act.wait_ge(spec_w_loaded, 16 * SPEC_W_DMAS)
            for g in range(2):
                nc.scalar.activation(spec_w[g][64:64 + GR, :, 0:BINS:2], spec_w[g][0:GR, :, 1:BINS:2], ACT.Copy,
                                     scale=-1.0).then_inc(spec_w_rows, 1)
                nc.scalar.activation(spec_w[g][64:64 + GR, :, 1:BINS:2], spec_w[g][0:GR, :, 0:BINS:2],
                                     ACT.Copy).then_inc(spec_w_rows, 1)
            act.wait_ge(dc_ready, 2)
            act.wait_ge(spec_x_rows, 2)
            for ph in range(2):
                for g, ri, n in SPEC_ACT:
                    dst, src, mask = spec_copy(g, ri, n, ph)
                    nc.scalar.activation(dst, src, ACT.Copy, scale=mask).then_inc(spec_x_act, 1)
            for n in range(0, SBANKS, 2):
                ps, drained = read_bank(act, "spec", n)
                dst, src = relu_spec(n)
                nc.scalar.activation(dst, src, ACT.Relu).then_inc(drained, 1)
            for k in range(KT):
                ps, drained = read_bank(act, "spec_t", k, 0)
                nc.scalar.activation(spec_ot[:, k, 0:OH, :].rearrange("p o m -> p (o m)"),
                                     ps[0:KROWS, 0:64 * OH], ACT.Copy).then_inc(drained, 1)
            for h in range(HALVES):
                ps, drained = read_bank(act, "inv", 2 * h)
                nc.scalar.activation(inv_out(h, 0), ps[:, 0:64 * OH].rearrange("p (o n b) -> p o n b", o=OH, b=B),
                                     ACT.Copy).then_inc(drained, 1)
            act.wait_ge(l0_loaded, 16 * L0_DMAS)
            for c in range(CHUNKS - 1):
                turned(L0B, c)
            act.wait_ge(sign_centred, 2)
            nc.scalar.activation(sign1[:, 0:QG * G1], qw1_t[:, 0:QG * G1], ACT.Sign).then_inc(sign_ready, 1)
            nc.scalar.activation(sign2[:, :, 0:QG * G2], qw2_t[:, :, 0:QG * G2], ACT.Sign).then_inc(sign_ready, 1)
            act.wait_ge(l1_loaded, 16 * L1_DMAS)
            mlp(0, L0B, L1A)

            act.wait_ge(pad_zero, 2)
            for what, x in conv_order():
                if what == "win":
                    lo = LEAD + IMG * IMGS * x
                    ps, drained = read_bank(act, "win", x, 0)
                    dst = pad[0][:, lo:lo + IMGS * IMG].rearrange("p (b y x) -> p b y x", b=IMGS, x=PW)
                    nc.scalar.activation(dst[:, :, 0:HH, 0:WW],
                                         ps[:, :].rearrange("p (b y x) -> p b y x", b=IMGS, x=WW),
                                         ACT.Identity, bias=b_in[0][:, :]).then_inc(drained, 1)
                    r, lo = 64 * (x % 2), LEAD + IMG * IMGS * (x // 2)
                    ps, drained = read_bank(act, "win", x, 1)
                    dst = pad[1][r:r + IN2, lo:lo + IMGS * IMG].rearrange("p (b y x) -> p b y x", b=IMGS, x=PW)
                    nc.scalar.activation(dst[:, :, 0:HH, 0:WW],
                                         ps[0:IN2, :].rearrange("p (b y x) -> p b y x", b=IMGS, x=WW),
                                         ACT.Identity, bias=b_in[1][:, :]).then_inc(drained, 1)
                elif what == "loc":
                    ps, drained = read_bank(act, "loc", x)
                    n = int(x[1])
                    for im in range(IMGS):
                        if x[0] == "m":
                            src = ps[:, tok(HALVES * im, HALVES * P)].rearrange("p (h c) -> p h c", h=HALVES)
                            last = nc.scalar.activation(loc[:, :, IMGS * n + im, 0:P], src, ACT.Copy)
                        else:
                            src = ps[:, tok(HALVES * im, HALVES * P)].rearrange("p (h k c) -> p h k c",
                                                                               h=HALVES, k=2)
                            b = 2 * IMGS * n + im
                            last = nc.scalar.activation(loc[:, :, b:b + IMGS + 1:IMGS, P:INNER], src, ACT.Copy)
                    last.then_inc(drained, 1)
                elif what == "turn_m":
                    for k in range(2):
                        ps, drained = read_bank(act, "turn_m", x, k)
                        nc.scalar.activation(mixed_t[k][:, ctok(x)], ps[0:C, :], ACT.Identity,
                                             bias=on_b[:, k:k + 1], scale=on_g[:, k:k + 1]).then_inc(drained, 1)
                elif what == "turn_own":
                    turned(L1A, x)
                elif what == "turn":
                    turned(L1B, x)
            mlp(1, L1B, A2)

            def attention(a, l, nxt):
                def qkv(c):
                    ps, drained = read_bank(act, "qk", a, c, 0)
                    nc.scalar.activation(q_raw[:, c % 2, :], ps[0:C, :], ACT.Copy).then_inc(drained, 1)
                    ps, drained = read_bank(act, "qk", a, c, 1)
                    nc.scalar.activation(k_t[:, ctok(c)], ps[0:C, :], ACT.Copy).then_inc(drained, 1)

                qkv(0)
                for s, hooks in attention_steps(a, nxt):
                    i = s - 2
                    if 0 <= i < NI * CHUNKS and i % 2:
                        ps, drained = read_bank(act, "pt", a, i)
                        nc.scalar.activation(probs_t[:, i % 3, :], ps[:, 0:384], ACT.Copy).then_inc(drained, 1)
                    if s < NI * CHUNKS:
                        ps, drained = read_bank(act, "s", a, s)
                        act.wait_ge(nmax_ready, NI * CHUNKS * a + s + 1)
                        nc.scalar.activation(probs[:, s % 3, 0:P], ps[:, 0:P], ACT.Exp, bias=nmax[:, s % 3, 0:1])
                        nc.scalar.activation(probs[:, s % 3, P:384], ps[:, P:384], ACT.Exp,
                                             bias=nmax[:, s % 3, 1:2]).then_inc(drained, 1)
                    for what, c in hooks:
                        if what == "qkv":
                            qkv(c)
                        if what == "turn_own":
                            turned(l, c)
                        if what == "evac_o":
                            for g, heads in enumerate(HEAD_GROUPS):
                                ps, drained = read_bank(act, "o", a, c, g)
                                nc.scalar.activation(o_raw[0:32 * len(heads), c % 2, g, :],
                                                     ps[0:32 * len(heads), :], ACT.Copy).then_inc(drained, 1)
                        if what == "turn_n":
                            ps, drained = read_bank(act, "turn_n", a, c)
                            nc.scalar.activation(o_t[:, c % 2, :], ps[0:C, :], ACT.Copy).then_inc(drained, 1)
                        if what == "turn":
                            turned(nxt, c, dict(chunks_of(nxt))[c])

            attention(0, A2, F2)

            for c, w in chunks_of(F2):
                for k in range(HT):
                    ps, drained = read_bank(act, "qup", c, k)
                    nc.scalar.activation(qy1[:, k, ctok(c, P * w)], ps[:, 0:P * w], ACT.Identity,
                                         bias=qb1[:, k:k + 1]).then_inc(drained, 1)
            for b in range(QIMGS):
                act.wait_ge(qclip, 2 * b + 2)
                nc.scalar.activation(qh[:, :, TOK * b:TOK * b + TOK], qy1[:, :, TOK * b:TOK * b + TOK],
                                     ACT.Gelu).then_inc(qh_ready, 1)
            for c in range(CHUNKS):
                turned(A3, c)
            attention(1, A3, MO)

            act.wait_ge(l3_loaded, 16 * L3_DMAS)
            for i in range(NE * CHUNKS):
                for k in range(HT):
                    ps, drained = read_bank(act, "eup", i, k)
                    nc.scalar.activation(hidden[:, i % 2, k, :], ps[:, :], ACT.Gelu,
                                         bias=e_b1[:, i % NE, k:k + 1]).then_inc(drained, 1)
                if i == 0:
                    act.wait_ge(gate_step, 2)
                    nc.scalar.activation(score[:, :, :], score[:, :, :], ACT.Exp).then_inc(gate_exp_ready, 1)

        @block.vector
        def _(dve):
            def norm(l, c, src, width=CT):
                no = LN_NO[l, c]
                t0 = CT * c
                for t in range(width):
                    ins = nc.vector.bn_stats(stats[:, l, t0 + t, :], src(t))
                ins.then_inc(stats_ready, 1)
                dve.wait_ge(stats_ready, no)
                for t in range(width):
                    ins = nc.vector.bn_aggr(moments[:, l, t0 + t, :], stats[:, l, t0 + t, :])
                ins.then_inc(moments_ready, 1)
                dve.wait_ge(rstd_ready, no)
                for t in range(width):
                    if l == L0A:
                        dst = normed_s[:, t0 + t, :].rearrange("p (g c) -> p g c", g=2)[:, :, 0:GR]
                        v = src(t).rearrange("p (g c) -> p g c", g=2)
                    else:
                        dst = mixed[:, t0 + t, :] if l == L1M else normed[l % 2][:, t0 + t, :]
                        v = src(t)
                    ins = nc.vector.tensor_scalar(dst, v, moments[:, l, t0 + t, 0:1], rstd[:, l, t0 + t:t0 + t + 1],
                                                  ALU.subtract, ALU.mult)
                return ins.then_inc(normed_ready, 1)

            def x_tile(c):
                return lambda t: X[:, CT * c + t, :]

            def update(l, c):
                ps, drained = read_bank(dve, "down", l, c)
                if l in BIASED:
                    dve.wait_ge(bias_added, bias_no(l, c))
                v = X[:, CT * c:CT * c + CT, :]
                nc.vector.tensor_tensor(v, ps[:, 0:C * CT].rearrange("p (t c) -> p t c", c=C), v,
                                        ALU.add).then_inc(drained, 1)
                landed(dve, "down", l, c)

            def mlp(m, l, nxt):
                for c in range(CHUNKS):
                    update(l, c)
                    norm(nxt, c, x_tile(c))

            nc.vector.memset(spec_w[0][32:64].rearrange("p q m -> p (q m)"), 0.0).then_inc(spec_zero, 1)
            for c in range(CHUNKS):
                dve.wait_ge(x_loaded[c], 16)
                norm(L0A, c, x_tile(c))
            dve.wait_ge(const_a_loaded, 16)
            nc.vector.tensor_copy(spec_x[1][32:64].rearrange("p q n b -> p q (n b)"),
                                  delta[32:64, :].unsqueeze(1).broadcast_to([32, POS, GB * B])
                                  ).then_inc(spec_x_rows, 1)
            dve.wait_ge(n1_loaded, 16 * 4)
            nc.vector.tensor_scalar(n1b16[0:64 + GR, :], n1b[0:64 + GR, :], float(TOK) ** 0.5, None,
                                    ALU.mult).then_inc(dc_ready, 1)
            for b in range(B):
                landed(dve, "dft", b)
            dve.wait_ge(dc_ready, 1)
            dc = spec_f[0:64 + GR, :, 0, 0]
            nc.vector.tensor_scalar(dc, dc, n1b16[0:64 + GR, :], None, ALU.add).then_inc(dc_ready, 1)
            dve.wait_ge(dc_ready, 2)
            dve.wait_ge(spec_x_rows, 2)
            for ph in range(2):
                for g, ri, n in SPEC_DVE:
                    dst, src, mask = spec_copy(g, ri, n, ph)
                    nc.vector.tensor_scalar(dst, src, mask, None, ALU.mult).then_inc(spec_x_dve, 1)
            for n in range(1, SBANKS, 2):
                ps, drained = read_bank(dve, "spec", n)
                dst, src = relu_spec(n)
                nc.vector.tensor_scalar(dst, src, 0.0, None, ALU.max).then_inc(drained, 1)
            for k in range(KT):
                ps, drained = read_bank(dve, "spec_t", k, 1)
                nc.vector.tensor_copy(spec_ot[:, k, OH:BS, :].rearrange("p o m -> p (o m)"),
                                      ps[0:KROWS, 0:64 * OH]).then_inc(drained, 1)
            for h in range(HALVES):
                ps, drained = read_bank(dve, "inv", 2 * h + 1)
                nc.vector.tensor_copy(inv_out(h, 1),
                                      ps[:, 0:64 * OH].rearrange("p (o n b) -> p o n b", o=OH, b=B)
                                      ).then_inc(drained, 1)
            for k in range(2 * HALVES):
                landed(dve, "inv", k)
            for c in range(CHUNKS):
                norm(L0B, c, lambda t, c=c: xs[:, CT * c + t, :])
            ps, drained = read_bank(dve, "signprep", 0)
            nc.vector.tensor_copy(qw1_t[:, :], ps[0:C, 0:HID]).then_inc(sign_copied, 1)
            nc.vector.tensor_reduce(qsum[0:C, 0, :], ps[0:C, 0:QG * G1].rearrange("p (g m) -> p g m", g=QG),
                                    AX.X, ALU.add).then_inc(drained, 1)
            ps, drained = read_bank(dve, "signprep", 1)
            nc.vector.tensor_copy(qw2_t[:, :, :].rearrange("p k c -> p (k c)"), ps[:, 0:HT * C]
                                  ).then_inc(sign_copied, 1)
            nc.vector.tensor_reduce(
                qsum[:, 1, :],
                ps[:, 0:HT * C].rearrange("p (k c) -> p k c", k=HT)[:, :, 0:QG * G2].rearrange(
                    "p k (g m) -> p g k m", g=QG), AX.XY, ALU.add).then_inc(drained, 1)
            for n, size in enumerate((G1 * C, G2 * HID)):
                ps, drained = read_bank(dve, "signprep", 2 + n)
                nc.vector.tensor_scalar(qmean[:, n, :], ps[:, 0:QG], 1.0 / size, None, ALU.mult).then_inc(drained, 1)
            dve.wait_ge(sign_copied, 2)
            landed(dve, "signprep", 2)
            landed(dve, "signprep", 3)
            v = qw1_t[:, 0:QG * G1].rearrange("p (g m) -> p g m", g=QG)
            nc.vector.tensor_tensor(v, v, qmean[0:C, 0, :].unsqueeze(2).broadcast_to([C, QG, G1]),
                                    ALU.subtract).then_inc(sign_centred, 1)
            for k in range(HT):
                v = qw2_t[:, k, 0:QG * G2].rearrange("p (g m) -> p g m", g=QG)
                ins = nc.vector.tensor_tensor(v, v, qmean[:, 1, :].unsqueeze(2).broadcast_to([P, QG, G2]),
                                              ALU.subtract)
            ins.then_inc(sign_centred, 1)
            dve.wait_ge(l0_loaded, 16 * L0_DMAS)
            mlp(0, L0B, L1A)

            dve.wait_ge(l1_loaded, 16 * L1_DMAS)

            def conv_unit(u):
                k, first = int(u[0] == "s"), IMGS * int(u[1])
                base = CONV_STEPS * UNITS.index(u)
                for n in range(PE_TAPS, len(TAPS)):
                    dy, dx = TAPS[n]
                    for im in range(IMGS):
                        dst = conv[k][:, first + im, :].rearrange("p (y x) -> p y x", x=WW)
                        src = window(k, first + im, dy, dx)
                        if n == PE_TAPS:
                            ps, drained = read_bank(dve, "taps", u, im)
                            nc.vector.scalar_tensor_tensor(dst, src, kcol[k][:, n:n + 1], ps[:, 0:TOK].rearrange("p (y x) -> p y x", x=WW),
                                                           ALU.mult, ALU.add).then_inc(drained, 1)
                            continue
                        if n == PE_TAPS + 1:
                            landed(dve, "taps", u, im)
                        else:
                            dve.wait_ge(conv_step, base + IMGS * (n - PE_TAPS - 2) + im + 1)
                        nc.vector.scalar_tensor_tensor(dst, src, kcol[k][:, n:n + 1], dst,
                                                       ALU.mult, ALU.add).then_inc(conv_step, 1)

            def norm_mixed(c):
                banks = [read_bank(dve, "mix", c, ho) for ho in range(HALVES)]
                norm(L1M, c, lambda t: banks[t % HALVES][0][:, INNER * (t // HALVES):INNER * (t // HALVES) + INNER])
                for _, drained in banks:
                    dve.wait_ge(normed_ready, LN_NO[L1M, c])
                    dve.sem_inc(drained, 1)

            for u in ("m0", "m1", "s0", "m2"):
                conv_unit(u)
            norm_mixed(0)
            conv_unit("m3")
            norm_mixed(1)
            conv_unit("s1")
            for c in (0, 1):
                update(L1A, c)
                norm(L1B, c, x_tile(c))
            norm_mixed(2)
            norm_mixed(3)
            for c in (2, 3):
                update(L1A, c)
                norm(L1B, c, x_tile(c))
            mlp(1, L1B, A2)

            def attention(a, l, nxt):
                def qkv(c):
                    landed(dve, "qk", a, c, 0)
                    for h in range(NH):
                        nc.vector.tensor_scalar(q_heads[:, c % 2, h, :], q_raw[:, c % 2, :], hmask[0:C, h:h + 1],
                                                None, ALU.mult).then_inc(q_heads_ready, 1)
                    ps, drained = read_bank(dve, "v", a, c)
                    dst = v_sb[:, CT * c:CT * c + CT].rearrange("p t h d -> p (t h) d")[:, :, 0:HD]
                    nc.vector.tensor_copy(dst, ps[:, 0:CT * C].rearrange("p (n d) -> p n d", d=HD)
                                          ).then_inc(drained, 1)

                qkv(0)
                for s, hooks in attention_steps(a, nxt):
                    if s < NI * CHUNKS:
                        k, n = uses["s", a, s]
                        dve.wait_ge(bank_filled[k], n + 1)
                        nc.vector.tensor_reduce(nmax[:, s % 3, 0:1], bank[k][:, 0:P], AX.X, ALU.max, negate=True)
                        nc.vector.tensor_reduce(nmax[:, s % 3, 1:2], bank[k][:, P:384], AX.X, ALU.max,
                                                negate=True).then_inc(nmax_ready, 1)
                    i = s - 2
                    if 0 <= i < NI * CHUNKS and i % 2 == 0:
                        ps, drained = read_bank(dve, "pt", a, i)
                        nc.vector.tensor_copy(probs_t[:, i % 3, :], ps[:, 0:384]).then_inc(drained, 1)
                    for what, c in hooks:
                        if what == "qkv":
                            qkv(c)
                        if what == "turn_o":
                            for im in range(IMGS):
                                ps, drained = read_bank(dve, "turn_o", a, c, im)
                                v = ps[:, 0:HALVES * NH * 32].rearrange("p (n d) -> p n d", d=32)
                                t = slice(HALVES * im, HALVES * im + HALVES)
                                rec = o_rec[:, c % 2, t, :].rearrange("p t h -> p (t h)")
                                nc.vector.reciprocal(rec, v[:, :, HD]).then_inc(o_rec_ready, 1)
                                dve.wait_ge(o_rec_ready, IMGS * (CHUNKS * a + c) + im + 1)
                                nc.vector.tensor_tensor(
                                    o_norm[:, c % 2, t, :].rearrange("p t (h d) -> p (t h) d", d=HD), v[:, :, 0:HD],
                                    rec.unsqueeze(2).broadcast_to([P, HALVES * NH, HD]), ALU.mult
                                    ).then_inc(drained, 1)
                        if what == "proj":
                            update(l, c)
                            if (nxt, c) in LN_NO:
                                norm(nxt, c, x_tile(c), dict(chunks_of(nxt))[c])

            dve.wait_ge(v_pad_ready, 1)
            attention(0, A2, F2)

            CLIP = QB - QEPS

            def scale_of(n):
                ps, drained = read_bank(dve, "gamma", n, 0)
                nc.vector.tensor_reduce(qmax1[:, n:n + 1], ps[0:QG, 0:P], AX.X, ALU.max).then_inc(drained, 1)
                landed(dve, "gamma", n, 0)
                nc.vector.tensor_scalar(qmax1[:, n:n + 1], qmax1[:, n:n + 1], QEPS, None,
                                        ALU.add).then_inc(qchain, 1)
                dve.wait_ge(qchain, 3 * n + 1)
                nc.vector.reciprocal(qrec[:, n:n + 1], qmax1[:, n:n + 1]).then_inc(qchain, 1)
                dve.wait_ge(qchain, 3 * n + 2)
                nc.vector.tensor_scalar(qdiag[:, n, :], ident[0:QG, 0:QG], qrec[:, n:n + 1], QB,
                                        ALU.mult, ALU.mult).then_inc(qchain, 1)
                ps, drained = read_bank(dve, "gamma", n, 1)
                nc.vector.tensor_copy(qscale[:, n, :], ps[:, 0:QG]).then_inc(drained, 1)
                landed(dve, "gamma", n, 1)

            for c, w in chunks_of(F2):
                for k in range(HT):
                    landed(dve, "qup", c, k)
                for b in range(IMGS * c, IMGS * c + w // HALVES):
                    nc.vector.tensor_reduce(qmax[:, 0, b:b + 1], qy1[:, :, TOK * b:TOK * b + TOK], AX.XY, ALU.max,
                                            apply_absolute_value=True).then_inc(qmax_ready, 1)
            scale_of(0)
            for b in range(QIMGS):
                v = qy1[:, :, TOK * b:TOK * b + TOK]
                nc.vector.tensor_scalar(v, v, qscale[:, 0, b:b + 1], CLIP, ALU.mult, ALU.min).then_inc(qclip, 1)
                dve.wait_ge(qclip, 2 * b + 1)
                nc.vector.tensor_scalar(v, v, -CLIP, None, ALU.max).then_inc(qclip, 1)
            for c, w in chunks_of(F2):
                ps, drained = read_bank(dve, "down", F2, c)
                nc.vector.tensor_tensor(qy2[:, CT * c:CT * c + w, :], ps[:, 0:C * w].rearrange("p (t c) -> p t c", c=C),
                                        bias_row[F2][:, :].unsqueeze(1).broadcast_to([P, w, C]),
                                        ALU.add).then_inc(drained, 1)
                landed(dve, "down", F2, c)
                for b in range(IMGS * c, IMGS * c + w // HALVES):
                    nc.vector.tensor_reduce(qmax[:, 1, b:b + 1], qy2[:, HALVES * b:HALVES * b + HALVES, :], AX.XY,
                                            ALU.max, apply_absolute_value=True).then_inc(qmax_ready, 1)
            scale_of(1)
            norm(A3, CHUNKS - 1, x_tile(CHUNKS - 1))
            for b in range(QIMGS):
                v = qy2[:, HALVES * b:HALVES * b + HALVES, :]
                x = X[:, HALVES * b:HALVES * b + HALVES, :]
                nc.vector.tensor_scalar(v, v, qscale[:, 1, b:b + 1], CLIP, ALU.mult, ALU.min).then_inc(qclip2, 1)
                dve.wait_ge(qclip2, 3 * b + 1)
                nc.vector.tensor_scalar(v, v, -CLIP, None, ALU.max).then_inc(qclip2, 1)
                dve.wait_ge(qclip2, 3 * b + 2)
                nc.vector.tensor_tensor(x, x, v, ALU.add).then_inc(qclip2, 1)
            for c in range(CHUNKS - 1):
                dve.wait_ge(qclip2, 3 * min(IMGS * c + IMGS, QIMGS))
                norm(A3, c, x_tile(c))

            attention(1, A3, MO)

            step = [0]

            def then(ins):
                step[0] += 1
                ins.then_inc(gate_step, 1)
                dve.wait_ge(gate_step, step[0])

            spread = lambda v: v[:, :].unsqueeze(2).broadcast_to([P, TILES, NE])
            pairs = lambda v: v[:, :, :].rearrange("p t (i j) -> p t i j", i=NE)
            rank = lambda k: cb("rank")[:, NE * NE * k:NE * NE * (k + 1)].unsqueeze(1).broadcast_to(
                [P, TILES, NE * NE])
            dve.wait_ge(l3_loaded, 16 * L3_DMAS)
            ps, drained = read_bank(dve, "gate")
            nc.vector.tensor_tensor(score[:, :, :], ps[:, 0:NE * TILES].rearrange("p (t e) -> p t e", e=NE),
                                    gate_b[:, :].unsqueeze(1).broadcast_to([P, TILES, NE]),
                                    ALU.add).then_inc(drained, 1)
            landed(dve, "gate")
            then(nc.vector.tensor_reduce(gate1[:, :], score[:, :, :], AX.X, ALU.max))
            then(nc.vector.tensor_tensor(score[:, :, :], score[:, :, :], spread(gate1), ALU.subtract))
            dve.wait_ge(gate_exp_ready, 1)
            then(nc.vector.tensor_reduce(gate1[:, :], score[:, :, :], AX.X, ALU.add))
            then(nc.vector.reciprocal(gate1[:, :], gate1[:, :]))
            then(nc.vector.tensor_tensor(score[:, :, :], score[:, :, :], spread(gate1), ALU.mult))
            of_j = score[:, :, :].unsqueeze(2).broadcast_to([P, TILES, NE, NE])
            of_i = score[:, :, :].unsqueeze(3).broadcast_to([P, TILES, NE, NE])
            nc.vector.tensor_tensor(pairs(cmp_a), of_j, of_i, ALU.is_ge)
            then(nc.vector.tensor_tensor(pairs(cmp_b), of_j, of_i, ALU.is_gt))
            nc.vector.tensor_tensor(cmp_a[:, :, :], cmp_a[:, :, :], rank(0), ALU.mult)
            then(nc.vector.tensor_tensor(cmp_b[:, :, :], cmp_b[:, :, :], rank(1), ALU.mult))
            then(nc.vector.tensor_tensor(cmp_a[:, :, :], cmp_a[:, :, :], cmp_b[:, :, :], ALU.add))
            then(nc.vector.tensor_reduce(gates[:, :, :], pairs(cmp_a), AX.X, ALU.add))
            then(nc.vector.tensor_scalar(gates[:, :, :], gates[:, :, :], 1.5, None, ALU.is_lt))
            then(nc.vector.tensor_tensor(gates[:, :, :], gates[:, :, :], score[:, :, :], ALU.mult))
            then(nc.vector.tensor_reduce(gate1[:, :], gates[:, :, :], AX.X, ALU.add))
            then(nc.vector.tensor_scalar(gate1[:, :], gate1[:, :], 1e-9, None, ALU.add))
            then(nc.vector.reciprocal(gate1[:, :], gate1[:, :]))
            then(nc.vector.tensor_tensor(gates[:, :, :], gates[:, :, :], spread(gate1), ALU.mult))
            for i in range(NE * CHUNKS):
                c, e = i // NE, i % NE
                x = X[:, CT * c:CT * c + CT, :]
                if e == NE - 1:
                    landed(dve, "edown", i - 1)
                    dve.wait_ge(bias_sum_step, 2 * NE - 1)
                    nc.vector.tensor_tensor(x, x, bias_sum[:, CT * c:CT * c + CT, :], ALU.add
                                            ).then_inc(bias_sum_added, 1)
                    dve.wait_ge(bias_sum_added, c + 1)
                ps, drained = read_bank(dve, "edown", i)
                if 0 < e < NE - 1:
                    landed(dve, "edown", i - 1)
                for t in range(CT):
                    n = CT * c + t
                    ins = nc.vector.scalar_tensor_tensor(X[:, n, :], ps[:, C * t:C * t + C], gates[:, n, e:e + 1],
                                                         X[:, n, :], ALU.mult, ALU.add)
                ins.then_inc(drained, 1)

        @block.gpsimd
        def _(pool):
            def add_bias(l, c):
                x = X[:, CT * c:CT * c + CT, :]
                nc.gpsimd.tensor_tensor(x, x, bias_row[l][:, :].unsqueeze(1).broadcast_to([P, CT, C]),
                                        ALU.add).then_inc(bias_added, 1)

            def rstds(*norms):
                for l, c in [k for k in LN_SEQ if k[0] in norms]:
                    w = dict(chunks_of(l))[c]
                    pool.wait_ge(moments_ready, LN_NO[l, c])
                    t = slice(CT * c, CT * c + w)
                    nc.gpsimd.tensor_scalar(moments[:, l, t, 1], moments[:, l, t, 1], LN_EPS, None,
                                            ALU.add).then_inc(eps_added, 1)
                    pool.wait_ge(eps_added, LN_NO[l, c])
                    nc.gpsimd.tensor_tensor(rstd[:, l, t], moments[:, l, t, 1], exponent[:, 0:w],
                                            ALU.pow).then_inc(rstd_ready, 1)
                    if l in BIASED and l != L0B:
                        pool.wait_ge(normed_ready, LN_NO[l, c])
                        add_bias(l, c)

            nc.gpsimd.memset(exponent[:, :], -0.5)
            nc.gpsimd.memset(n1g[:, :], 0.0).then_inc(n1_zero, 1)
            nc.gpsimd.memset(n1b[:, :], 0.0).then_inc(n1_zero, 1)
            nc.gpsimd.memset(normed_s[:, :, GR:64], 0.0).then_inc(gap_zero, 1)
            pool.wait_ge(gap_zero, 1)
            nc.gpsimd.memset(spec_w[1][32:64].rearrange("p q m -> p (q m)"), 0.0).then_inc(spec_zero, 1)
            pool.wait_ge(spec_zero, 2)
            rstds(L0A)
            nc.gpsimd.memset(ones[:, :], 1.0).then_inc(ones_ready, 1)
            nc.gpsimd.memset(sign1[:, QG * G1:HID], 0.0).then_inc(sign_ready, 1)
            nc.gpsimd.memset(sign2[:, :, QG * G2:C], 0.0).then_inc(sign_ready, 1)
            pool.wait_ge(const_b_loaded, 16)
            nc.gpsimd.tensor_copy(ident_b[:, :], ident).then_inc(bf_ready, 1)
            nc.gpsimd.tensor_copy(mask_b[:, :], cb("mask")).then_inc(bf_ready, 1)
            rstds(L0B)
            for k in range(2 * HALVES):
                landed(pool, "inv", k)
            for c in range(CHUNKS):
                x = X[:, CT * c:CT * c + CT, :]
                nc.gpsimd.tensor_tensor(x, x, xs[:, CT * c:CT * c + CT, :], ALU.add).then_inc(x_plus_xs, 1)
            pool.wait_ge(l0_loaded, 16 * L0_DMAS)
            for c in range(CHUNKS):
                pool.wait_ge(x_plus_xs, c + 1)
                add_bias(L0B, c)
            for v in pad:
                nc.gpsimd.memset(v, 0.0).then_inc(pad_zero, 1)
            pool.wait_ge(l1_loaded, 16 * L1_DMAS)
            for k in range(2):
                for n in range(PE_TAPS):
                    nc.gpsimd.tensor_scalar(tap_diag[:, k, n, :], ident, kcol[k][:, n:n + 1], None,
                                            ALU.mult).then_inc(diag_ready, 1)
            rstds(L1A)
            pool.wait_ge(l2_loaded, 16 * L2_DMAS)
            nc.gpsimd.memset(v_sb, 0.0).then_inc(v_zero, 1)
            pool.wait_ge(v_zero, 1)
            nc.gpsimd.memset(v_sb[:, :, :, HD:HD + 1], 1.0).then_inc(v_pad_ready, 1)
            rstds(L1M, L1B, A2, F2, A3, MO)
            pool.wait_ge(l3_loaded, 16 * L3_DMAS)
            pool.wait_ge(gate_step, GATE_STEPS)
            for e in range(NE):
                dst = bias_term if e else bias_sum
                nc.gpsimd.tensor_tensor(dst, e_b2[:, e, :].unsqueeze(1).broadcast_to([P, TILES, C]),
                                        gates[:, :, e:e + 1].broadcast_to([P, TILES, C]),
                                        ALU.mult).then_inc(bias_sum_step, 1)
                if e:
                    pool.wait_ge(bias_sum_step, 2 * e)
                    nc.gpsimd.tensor_tensor(bias_sum, bias_sum, bias_term, ALU.add).then_inc(bias_sum_step, 1)
                    pool.wait_ge(bias_sum_step, 2 * e + 1)


def constants():
    f = np.float64
    at_a, wa = spots(CONST_A)
    at_b, wb = spots(CONST_B)
    ca, cb = np.zeros((P, wa), f), np.zeros((P, wb), f)
    y, x = np.divmod(np.arange(TOK), WW)
    kh, kw = np.divmod(np.arange(POS), WF)
    angle = 2 * np.pi * (np.outer(y, kh) / HH + np.outer(x, kw) / WW)
    norm = TOK ** -0.5
    dft = np.concatenate([np.cos(angle), -np.sin(angle)], 1) * norm
    twice = np.where((kw == 0) | (kw == WW // 2), 1.0, 2.0)
    idft = np.stack([np.cos(angle) * twice * norm, -np.sin(angle) * twice * norm], 2).reshape(TOK, 2 * POS).T
    near = lambda d: 0.25 * 0.4 * 0.6 ** np.abs(d) * np.where(d == 0, 2.0, 1.0)
    dy, dx = y[:, None] - y[None, :], x[:, None] - x[None, :]
    mixer = np.eye(TOK) + near(dx) * (dy == 0) + near(dy) * (dx == 0)
    cut = lambda m, at, n: m[:, at[n][0]:at[n][1]]
    cut(ca, at_a, "ident")[:] = np.eye(P)
    for g in range(2):
        for n in range(GB):
            cut(ca, at_a, "nmask")[64 * g + BS * n:64 * g + BS * n + BS, n] = 1
    for n in range(GB):
        cut(ca, at_a, "delta")[GR + n, B * n:B * n + B] = 1
    cut(ca, at_a, "dft")[:] = dft.reshape(HALVES, P, 2 * POS).transpose(1, 0, 2).reshape(P, -1)
    above = np.where(np.arange(P)[None, :] > np.arange(P)[:, None], NEG, 0.0)
    cut(cb, at_b, "mask")[:] = above
    for h in range(NH):
        cut(ca, at_a, "hmask")[HD * h:HD * h + HD, h] = HD ** -0.5
    i, j = np.divmod(np.arange(NE * NE), NE)
    cut(cb, at_b, "rank")[:] = np.concatenate([j < i, j > i])[None, :]
    cut(cb, at_b, "idft")[0:KROWS] = idft.reshape(KT, KROWS, TOK).transpose(1, 0, 2).reshape(KROWS, -1)
    cut(cb, at_b, "mix")[:] = mixer.reshape(HALVES, P, TOK).transpose(1, 0, 2).reshape(P, -1)
    return {"const_a": ca.astype(np.float32), "const_b": cb.astype(np.float32)}


def kernel(**inputs):
    import concourse.bacc as bacc
    from concourse.bass_utils import run_bass_kernel_spmd

    nc = bacc.Bacc("TRN2", target_bir_lowering=False, num_devices=1)
    arrays, handles = {}, {}
    for name, value in {**inputs, **constants()}.items():
        v = np.ascontiguousarray(value)
        arrays[f"in_{name}"] = v
        handles[name] = nc.dram_tensor(f"in_{name}", v.shape, mybir.dt.from_np(v.dtype), kind="ExternalInput").ap()
    out = nc.dram_tensor("out_x", (B, HH, WW, C), F32, kind="ExternalOutput").ap()
    hybrid_kernel(nc, handles, out)
    return run_bass_kernel_spmd(nc, [arrays], core_ids=[0]).results[0]["out_x"]
```

```python
from contextlib import ExitStack

import numpy as np

import concourse.bass as bass
from concourse import mybir

F32 = mybir.dt.float32
F32R = mybir.dt.float32r
I32 = mybir.dt.int32
BF16 = mybir.dt.bfloat16
ALU = mybir.AluOpType
ACT = mybir.ActivationFunctionType
AX = mybir.AxisListType

B, HH, WW, C = 8, 16, 16, 96
P = 128
TOK = HH * WW
HALVES = TOK // P
TILES = B * HALVES
IMGS = 2
CT = IMGS * HALVES
CN = IMGS * TOK
CHUNKS = B // IMGS
HID = 4 * C
HT = HID // P
WF = WW // 2 + 1
POS = HH * WF
NB, BS = 8, C // 8
GB = NB // 2
GR = GB * BS
BINS = 2 * BS
PPB = 512 // BINS
SBANKS = -(-POS // PPB)
KT = 3
KP = POS // KT
KROWS = 2 * KP
OH = BS // 2
INNER = 2 * C
IN2 = INNER - P
PW = WW + 1
IMG = PW * (HH + 1)
LEAD = PW + 1
TAPS = [(dy, dx) for dy in (-1, 0, 1) for dx in (-1, 0, 1)]
PE_TAPS = 4
NH, HD = 6, 16
HEAD_GROUPS = ((0, 1, 2, 3), (4, 5))
ITEMS = [(im, h) for heads in HEAD_GROUPS for im in range(IMGS) for h in heads]
NI = len(ITEMS)
NEG = -1e30
QG = 5
G1, G2 = HID // QG, C // QG
QB, QEPS = 128.0, 1e-5
QIMGS = QG * (B // QG)
NE = 4
LN_EPS = 1e-5
L0A, L0B, L1A, L1M, L1B, A2, F2, A3, MO = range(9)

MLP_NORM = (L0B, L1B)

CONST_A = {"ident": 128, "hmask": NH, "nmask": 4, "dft": HALVES * 2 * POS}
CONST_B = {"mask": 128, "rank": 32, "idft": KT * TOK, "mix": HALVES * TOK}


def spots(widths):
    at, out = 0, {}
    for name, w in widths.items():
        out[name] = (at, at + w)
        at += w
    return out, at


def chunks_of(l):
    if l == F2:
        return [(c, min(CT, HALVES * QIMGS - CT * c)) for c in range(CHUNKS) if CT * c < HALVES * QIMGS]
    return [(c, CT) for c in range(CHUNKS)]


CONV_DVE = [("update", L0B, 0), ("moments", L1A, 0), ("scale", L1A, 0), ("centre",),
            ("update", L0B, 1), ("moments", L1A, 1), ("scale", L1A, 1), ("update", L0B, 2),
            ("moments", L1A, 2), ("scale", L1A, 2), ("update", L0B, 3), ("moments", L1A, 3),
            ("scale", L1A, 3), ("taps", "m0", 4), ("taps", "m0", 5), ("taps", "m0", 6),
            ("taps", "m0", 7), ("taps", "m0", 8), ("taps", "m1", 4), ("taps", "m1", 5),
            ("taps", "m1", 6), ("taps", "m1", 7), ("taps", "m1", 8), ("taps", "s0", 4),
            ("taps", "s0", 5), ("taps", "s0", 6), ("taps", "s0", 7), ("taps", "s0", 8),
            ("taps", "m2", 4), ("taps", "m2", 5), ("taps", "m2", 6), ("taps", "m2", 7),
            ("taps", "m2", 8), ("moments", L1M, 0), ("taps", "m3", 4), ("taps", "m3", 5),
            ("scale", L1M, 0), ("taps", "m3", 6), ("taps", "m3", 7), ("taps", "m3", 8),
            ("moments", L1M, 1), ("taps", "s1", 4), ("taps", "s1", 5), ("scale", L1M, 1),
            ("taps", "s1", 6), ("taps", "s1", 7), ("taps", "s1", 8), ("update", L1A, 0),
            ("moments", L1B, 0), ("update", L1A, 1), ("moments", L1B, 1), ("scale", L1B, 0),
            ("moments", L1M, 2), ("scale", L1B, 1), ("moments", L1M, 3), ("scale", L1M, 2),
            ("scale", L1M, 3), ("update", L1A, 2), ("moments", L1B, 2), ("update", L1A, 3),
            ("moments", L1B, 3), ("scale", L1B, 2), ("scale", L1B, 3), ("update", L1B, 0),
            ("moments", A2, 0), ("scale", A2, 0), ("update", L1B, 1), ("moments", A2, 1),
            ("scale", A2, 1), ("update", L1B, 2), ("moments", A2, 2), ("scale", A2, 2),
            ("update", L1B, 3), ("moments", A2, 3), ("scale", A2, 3)]
CONV_PE = [("up", 0, 0), ("turn", L0B, 1), ("signprep",), ("up", 0, 1), ("turn", L0B, 2),
           ("down", 0, 0), ("sign_means",), ("up", 0, 2), ("turn", L0B, 3), ("down", 0, 1),
           ("turn", L1A, 0), ("up", 0, 3), ("down", 0, 2), ("turn", L1A, 1), ("down", 0, 3),
           ("turn", L1A, 2), ("signs",), ("win", 0), ("win", 1), ("taps", "m0"), ("turn", L1A, 3),
           ("taps", "m1"), ("win", 2), ("taps", "s0"), ("loc", "m1"), ("loc", "m0"), ("win", 3),
           ("taps", "m2"), ("loc", "s0"), ("mix", 0), ("taps", "m3"), ("mix", 1), ("turn_m", 0),
           ("taps", "s1"), ("wout", 0), ("turn_m", 1), ("loc", "m2"), ("wout", 1), ("loc", "m3"),
           ("loc", "s1"), ("mix", 2), ("turn", L1B, 1), ("turn", L1B, 0), ("mix", 3), ("turn_m", 2),
           ("turn_m", 3), ("wout", 2), ("wout", 3), ("turn", L1B, 2), ("up", 1, 0), ("turn", L1B, 3),
           ("up", 1, 1), ("down", 1, 0), ("up", 1, 2), ("down", 1, 1), ("turn", A2, 0), ("up", 1, 3),
           ("down", 1, 2), ("turn", A2, 1), ("down", 1, 3), ("turn", A2, 2)]

WARM = {"start": 12, "spec": 66, "inverse": 12, ("turn", L1B, 0): 6, ("turn_m", 2): 10, ("turn_m", 3): 10,
        ("turn", L1B, 2): 10, "scores": 10}

LN_SEQ = [(l, c) for l in (L0A, L0B) for c in range(CHUNKS)]
LN_SEQ += [x[1:] for x in CONV_DVE if x[0] == "moments"]


SLOTS = [(0, 0), (0, 3), (0, 1), (0, 2), (1, 3), (1, 0), (1, 1), (1, 2)]
STEPS = NI * len(SLOTS)
MOE_CHUNKS = [c for a, c in SLOTS if a == 1]


O = {"own": 1, "q": -6, "k": -4, "v": -5, ("evac_o", 0): 12, ("evac_o", 1): 15, ("turn_o", 0): 16,
     ("turn_o", 1): 17, "turn_n": 19, "proj": 20, "norm": 20, "scale": 1, "turn": 2, "gate_scores": 4,
     "gate_best": 7, "ffn": 4, ("qmax", 0): 6, ("gamma_max", 0): 6, ("gamma_spread", 0): 8,
     ("clip", 0): 8, "qgelu": 8, "qdown": 11, ("qmax", 1): 0, ("gamma_max", 1): 3,
     ("gamma_spread", 1): 3, ("clip", 1): 3, "norm2": 4, "split_w": 51, "split_x": -3, "eup": 1,
     "edown": 4}


SIDE_WORK = ["k", "turn_n", "turn_o", "gamma_max"]
SIDE_BANK = {what: 2 for what in SIDE_WORK}


def stream():
    hooks = {}

    def at(step, *what):
        hooks.setdefault(step, []).append(what)

    at(O["own"], "turn", A2, CHUNKS - 1)
    for j, (a, c) in enumerate(SLOTS):
        base = NI * j
        nxt = MO if a else F2 if c in dict(chunks_of(F2)) else A3
        if j:
            for k, what in enumerate(("q", "k", "v")):
                at(base + O[what], what, j)
        for g in range(2):
            at(base + O["evac_o", g], "evac_o", j, g)
        for im in range(IMGS):
            at(base + O["turn_o", im], "turn_o", j, im)
        at(base + O["turn_n"], "turn_n", j)
        at(base + O["proj"], "proj", j)
        t = base + O["norm"]
        at(t, "norm", nxt, c)
        at(t + O["scale"], "scale", nxt, c)
        at(t + O["turn"], "turn", nxt, c)
        if nxt == MO:
            at(t + O["gate_scores"], "gate_scores", c)
            at(t + O["gate_best"], "gate_best", c)
        if nxt == F2:
            t += O["ffn"]
            for k in range(HT):
                at(t + 2 * k, "qup", c, k)
            at(t + O["qmax", 0], "qmax", 0, c)
            at(t + O["gamma_max", 0], "gamma_max", 0, c)
            at(t + O["gamma_spread", 0], "gamma_spread", 0, c)
            at(t + O["clip", 0], "clip", 0, c)
            at(t + O["qgelu"], "qgelu", c)
            t += O["qdown"]
            at(t, "qdown", c)
            at(t + O["qmax", 1], "qmax", 1, c)
            at(t + O["gamma_max", 1], "gamma_max", 1, c)
            at(t + O["gamma_spread", 1], "gamma_spread", 1, c)
            at(t + O["clip", 1], "clip", 1, c)
            t += O["norm2"]
            at(t, "norm", A3, c)
            at(t + O["scale"], "scale", A3, c)
            at(t + O["turn"], "turn", A3, c)
    for e in range(NE):
        at(O["split_w"] + e, "split_w", e)
    for i in range(NE * CHUNKS):
        if i % NE == 0:
            at(STEPS + O["eup"] + 2 * i + O["split_x"], "split_x", i // NE)
        at(STEPS + O["eup"] + 2 * i, "eup", i)
        at(STEPS + O["edown"] + 2 * i, "edown", i)
    return [(s, hooks.get(s, [])) for s in range(max(hooks) + 1)]


LN_SEQ += [h[1:] for _, hooks in stream() for h in hooks if h[0] == "norm"]
GAMMA_SEQ = [h[1:] for _, hooks in stream() for h in hooks if h[0] == "gamma_max"]
LN_NO = {k: n + 1 for n, k in enumerate(LN_SEQ)}


def plan_banks():
    seq = []

    def use(bank, *key):
        seq.append((key, bank))

    def turn(l, c):
        use(c % 2, "turn", l, c)

    for b in range(B):
        use(b, "dft", b)
    for k in range(SBANKS):
        use(k, "spec", k)
    for k in range(KT):
        for j in range(2):
            use((7, 0, 1, 2, 3, 4)[2 * k + j], "spec_t", k, j)
    for k in range(HALVES * 2):
        use((5, 6, 7, 0)[k], "inv", k)
    turn(L0B, 0)
    def win(c):
        use(2 + c % 2, "win", c, 0)
        use(4 + c % 2, "win", c, 1)

    def taps(u):
        for im in range(IMGS):
            use(6 + im, "taps", u, im)

    for w in CONV_PE:
        if w[0] == "win":
            win(w[1])
        elif w[0] == "taps":
            taps(w[1])
        elif w[0] == "loc":
            use(1, "loc", w[1])
        elif w[0] == "mix":
            for ho in range(HALVES):
                use((6 if w[1] == 3 else 2) + ho, "mix", w[1], ho)
        elif w[0] == "turn_m":
            use(4, "turn_m", w[1], 0)
            use(5, "turn_m", w[1], 1)
        elif w[0] == "wout":
            use(0, "down", L1A, w[1])
        elif w[0] == "turn":
            use(0 if w[1] == L1B and w[2] < CHUNKS - 1 else w[2] % 2, *w)
        elif w[0] == "up":
            for k in range(HT):
                use(2 + k, *w, k)
        elif w[0] == "down":
            use(5 + w[2] % 2, "down", MLP_NORM[w[1]], w[2])
        elif w[0] == "signprep":
            use(7, "signprep", 0)
            use(5, "signprep", 1)
        elif w[0] == "sign_means":
            use(7, "sign_means")

    for what in ("q", "k", "v"):
        use(SIDE_BANK.get(what, 7), what, 0)
    for s, hooks in stream():
        if s < STEPS:
            use(s % 2, "s", s)
        if 0 <= s - 2 < STEPS:
            use(3 + s % 2, "pt", s - 2)
        i = s - 3
        if 0 <= i < STEPS:
            if i % NI == 0:
                use(5, "o", i // NI, 0)
            if i % NI == IMGS * len(HEAD_GROUPS[0]):
                use(6, "o", i // NI, 1)
        for what, *x in hooks:
            if what in ("q", "k", "v", "turn", "turn_o", "turn_n", "qup", "gamma_max", "gamma_spread", "gate_scores"):
                use(SIDE_BANK.get(what, 7), what, *x)
            if what == "proj":
                use(SIDE_BANK.get(what, 7), "down", *x)
            if what == "qdown":
                use(SIDE_BANK.get(what, 7), what, *x)
            if what == "eup":
                for k in range(HT):
                    use(k, what, *x, k)
            if what == "edown":
                use(3 + x[0] % 3, what, *x)
    out, count = {}, [0] * 8
    for key, bank in seq:
        assert key not in out, key
        out[key] = (bank, count[bank])
        count[bank] += 1
    return out


def hybrid_kernel(nc, a, out):
    uses = plan_banks()
    ctx = ExitStack()
    with ctx:
        def sb(name, shape, dt=F32):
            return ctx.enter_context(nc.sbuf_tensor(name, shape, dt))

        def sem(name):
            return ctx.enter_context(nc.semaphore(name))

        bank = [ctx.enter_context(nc.psum_tensor(f"bank{i}", [P, 512], F32)) for i in range(8)]

        at_a, wa = spots(CONST_A)
        at_b, wb = spots(CONST_B)
        const_a, const_b = sb("const_a", [P, wa]), sb("const_b", [P, wb])
        ca = lambda n: const_a[:, at_a[n][0]:at_a[n][1]]
        cb = lambda n: const_b[:, at_b[n][0]:at_b[n][1]]
        ident = ca("ident")
        nmask = ca("nmask")
        dft = ca("dft").rearrange("p (h n) -> p h n", h=HALVES)
        hmask = ca("hmask")
        idft = cb("idft").rearrange("p (k t) -> p k t", k=KT)
        mix = cb("mix").rearrange("p (h t) -> p h t", h=HALVES)
        ident_b, mask_b = sb("ident_b", [P, P], BF16), sb("mask_b", [P, P], BF16)
        ones = sb("ones", [P, P])
        idle_w = sb("idle_w", [P, 256], BF16)

        n1g, n1b, n1b16 = sb("n1g", [P, 1]), sb("n1b", [P, 1]), sb("n1b16", [P, 1])
        affine = {l: (sb(f"g{l}", [C, 1]), sb(f"b{l}", [C, 1])) for l in (L0B, L1A, L1B)}
        mlp_w1 = [sb(f"mlp_w1_{m}", [C, HID]) for m in range(2)]
        mlp_b1 = [sb(f"mlp_b1_{m}", [P, HT]) for m in range(2)]
        mlp_w2 = [sb(f"mlp_w2_{m}", [P, HT, C]) for m in range(2)]
        bias_row = {l: sb(f"bias_row{l}", [P, C]) for l in (L0B, L1A, L1B, F2, A3)}
        w_in = sb("w_in", [C, INNER])
        b_in = [sb("b_in0", [P, 1]), sb("b_in1", [IN2, 1])]
        kcol = [sb("kcol0", [P, 9]), sb("kcol1", [P, 9])]
        on_g, on_b = sb("on_g", [C, 2]), sb("on_b", [C, 2])
        w_out = sb("w_out", [C, 2, C])
        w_qkv = [sb(f"w_qkv{i}", [C, 3 * C]) for i in range(2)]
        w_proj = [sb(f"w_proj{i}", [C, C]) for i in range(2)]
        qw1, qw2 = sb("qw1", [P, HT, C]), sb("qw2", [C, HID])
        qb1 = sb("qb1", [P, HT])
        sign1, sign2 = sb("sign1", [C, HID]), sb("sign2", [P, HT, C])
        qsum, qmean = sb("qsum", [P, 2, QG]), sb("qmean", [P, 2, QG])
        gate_w, gate_b = sb("gate_w", [C, NE]), sb("gate_b", [P, NE])
        e_w1, e_w2 = sb("e_w1", [C, NE, HID]), sb("e_w2", [P, NE, HT, C])
        e_b1, e_b2 = sb("e_b1", [P, NE, HT]), sb("e_b2", [P, NE, C])

        X = sb("X", [P, TILES, C])
        stats, moments = sb("stats", [P, 9, TILES, 6]), sb("moments", [P, 9, TILES, 2])
        rstd, exponent = sb("rstd", [P, 9, TILES]), sb("exponent", [P, CT])
        normed = [sb(f"normed{i}", [P, TILES, C]) for i in range(2)]
        normed_t = [sb(f"normed_t{i}", [C, B * TOK]) for i in range(2)]
        hidden = sb("hidden", [P, 2, HT, CN])
        normed_s = hidden[:, :, :, :].rearrange("p a k n -> p (a k n)")[:, 0:TILES * P].rearrange(
            "p (t c) -> p t c", c=P)
        arena = sb("arena", [P, 24192])

        class Arena:
            def __init__(self):
                self.at = 0

            def __call__(self, shape, rows=P):
                n = int(np.prod(shape))
                assert self.at + n <= 24192, self.at + n
                v = arena[0:rows, self.at:self.at + n]
                self.at += n
                if len(shape) == 1:
                    return v
                names = "abcdef"[:len(shape)]
                return v.rearrange(f"p ({' '.join(names)}) -> p {' '.join(names)}",
                                   **{x: s for x, s in zip(names, shape)})

        ar = Arena()
        spec_w = [ar([POS, BINS]) for _ in range(2)]
        spec_x = [ar([POS, GB, B]) for _ in range(2)]
        spec_f = ar([B, 2, POS])
        spec_o = ar([BS, POS, 2], 2 * 32)
        spec_ot = ar([KT, BS, 2 * 32], KROWS)
        xs = normed[0][:, :, :]
        ar = Arena()
        pad = [ar([LEAD + B * IMG + 1]), ar([LEAD + B // 2 * IMG + 1])]
        conv = [ar([B, TOK]), ar([B // 2, TOK])]
        loc = ar([HALVES, B, INNER])
        mixed = ar([TILES, INNER])
        mixed_t = [ar([B * TOK], C), ar([B * TOK], C)]
        tap_diag = ar([2, PE_TAPS, P])
        conv_end = ar.at
        ar = Arena()
        q_raw, q_heads = ar([2, CN], C), ar([2, NH, CN], C)
        k_t = ar([B * TOK], C)
        probs, probs_t = ar([3, 384]), ar([3, 384])
        o_raw = ar([2, 2, CN])
        o_norm, o_t = ar([2, CT, C]), ar([2, CN], C)
        o_rec = ar([2, CT, NH])
        qy2 = ar([HALVES * QIMGS, C])
        score, gate1 = ar([TILES, NE]), ar([TILES])
        cmp_a, cmp_b = ar([TILES, NE * NE]), ar([TILES, NE * NE])
        bias_sum, bias_term = ar([TILES, C]), ar([TILES, C])
        ar.at = max(ar.at, conv_end)
        v_sb = ar([TILES, NH, 32])
        qw1_t, qw2_t = ar([HID], C), ar([HT, C])
        qy1, qh = hidden[:, 0], hidden[:, 1]
        nmax = sb("nmax", [P, 3, 2])
        qmax, qmax1, qrec, qdiag, qscale = (sb("qmax", [P, 2, QG]), sb("qmax1", [IMGS, len(GAMMA_SEQ)]),
                                            sb("qrec", [IMGS, len(GAMMA_SEQ)]),
                                            sb("qdiag", [IMGS, len(GAMMA_SEQ), IMGS]),
                                            sb("qscale", [P, 2, QG]))
        gates = sb("gates", [P, TILES, NE])

        x_hi, x_lo = sb("x_hi", [C, 2, CN], F32R), sb("x_lo", [C, 2, CN], F32R)
        w_hi, w_lo = sb("w_hi", [C, NE, HID], F32R), sb("w_lo", [C, NE, HID], F32R)
        top_bits = sb("top_bits", [C, CN], I32)

        bank_filled = [sem(f"bank{i}_filled") for i in range(8)]
        bank_drained = [sem(f"bank{i}_drained") for i in range(8)]
        x_loaded = [sem(f"x_loaded{c}") for c in range(CHUNKS)]
        const_a_loaded, const_b_loaded = sem("const_a_loaded"), sem("const_b_loaded")
        block_w_loaded = [sem(f"block_w{g}_loaded") for g in range(2)]
        spec_w_loaded, n1_loaded = sem("spec_w_loaded"), sem("n1_loaded")
        l0_loaded, l1_loaded, l2_loaded, l3_loaded = (sem(f"l{i}_loaded") for i in range(4))
        q_loaded, stored = sem("q_loaded"), sem("stored")
        stats_ready, moments_ready = sem("stats_ready"), sem("moments_ready")
        eps_added = sem("eps_added")
        rstd_ready, normed_ready = sem("rstd_ready"), sem("normed_ready")
        n1_zero, gap_zero = sem("n1_zero"), sem("gap_zero")
        spec_x_rows, spec_w_rows = sem("spec_x_rows"), sem("spec_w_rows")
        dc_ready, spec_x_dve, spec_x_act = sem("dc_ready"), sem("spec_x_dve"), sem("spec_x_act")
        x_plus_xs, bias_added = sem("x_plus_xs"), sem("bias_added")
        idle_ready = sem("idle_ready")
        ones_ready, bf_ready = sem("ones_ready"), sem("bf_ready")
        sign_copied, sign_centred, sign_ready = sem("sign_copied"), sem("sign_centred"), sem("sign_ready")
        diag_ready, pad_zero, conv_step = sem("diag_ready"), sem("pad_zero"), sem("conv_step")
        v_zero, v_pad_ready = sem("v_zero"), sem("v_pad_ready")
        q_heads_ready, o_rec_ready = sem("q_heads_ready"), sem("o_rec_ready")
        bias_sum_step, bias_sum_added = sem("bias_sum_step"), sem("bias_sum_added")
        nmax_ready = sem("nmax_ready")
        qmax_ready, qchain, qclip, qh_ready, qclip2 = (sem("qmax_ready"), sem("qchain"), sem("qclip"),
                                                       sem("qh_ready"), sem("qclip2"))
        x_split, w_split = sem("x_split"), sem("w_split")
        gate_step, gate_exp_ready = sem("gate_step"), sem("gate_exp_ready")

        def pe_bank(pe, *key):
            k, n = uses[key]
            if n:
                pe.wait_ge(bank_drained[k], n)
            return bank[k], bank_filled[k]

        def read_bank(eng, *key):
            k, n = uses[key]
            eng.wait_ge(bank_filled[k], n + 1)
            return bank[k], bank_drained[k]

        def landed(eng, *key):
            k, n = uses[key]
            eng.wait_ge(bank_drained[k], n + 1)

        tok = lambda t, n=P: slice(P * t, P * t + n)
        ctok = lambda c, n=CN: slice(CN * c, CN * c + n)
        SPEC_ALL = [(g, ri, n) for g in range(2) for ri in range(2) for n in range(GB)]
        SPEC_DVE, SPEC_ACT = SPEC_ALL[:12], SPEC_ALL[12:]
        BIASED = (L0B, L1A, L1B, A3)
        BIAS_SEQ = [(L0B, c) for c in range(CHUNKS)] + [k for k in LN_SEQ if k[0] in BIASED[1:]]
        GATE_STEPS = 15
        BIAS_STEPS = 2 * NE - 1
        slot_norm = lambda j: A3 if SLOTS[j][0] else A2

        def images(c):
            return range(IMGS * c, min(IMGS * c + IMGS, QIMGS))

        def gamma_no(n, c):
            k = GAMMA_SEQ.index((n, c))
            return k, sum(len(images(x)) for _, x in GAMMA_SEQ[:k + 1])
        bias_no = lambda l, c: BIAS_SEQ.index((l, c)) + 1
        CONV_STEPS = [x[1:] for x in CONV_DVE if x[0] == "taps" and x[2] > PE_TAPS]

        def tap_no(u, n, im=IMGS - 1):
            return IMGS * CONV_STEPS.index((u, n)) + im + 1

        def unit_chunks(u):
            return (int(u[1]),) if u[0] == "m" else (2 * int(u[1]), 2 * int(u[1]) + 1)

        def window(k, image, dy, dx):
            at = LEAD + IMG * image + dy * PW + dx
            return pad[k][:, at:at + HH * PW].rearrange("p (y x) -> p y x", x=PW)[:, :, 0:WW]

        def spec_copy(g, ri, n, bh):
            rows = slice(64 * g, 64 * g + GR)
            b = slice(B // 2 * bh, B // 2 * bh + B // 2)
            return (spec_x[g][64 * ri:64 * ri + GR, :, n, b],
                    spec_f[rows, b, ri, :].rearrange("p b q -> p q b"), nmask[rows, n:n + 1])

        def relu_spec(n):
            q = min(PPB, POS - PPB * n)
            return (spec_o[0:64, :, PPB * n:PPB * n + q, :].rearrange("p o q r -> p q o r"),
                    bank[n][0:64, 0:q * BINS].rearrange("p (q o r) -> p q o r", q=q, o=BS))

        def inv_out(h, j):
            return xs.rearrange("p (b h) (n o) -> p h o n b", h=HALVES, o=BS)[:, h, OH * j:OH * j + OH]

        SPEC_W_DMAS, L0_DMAS, L1_DMAS, L2_DMAS, Q_DMAS, L3_DMAS = 4, 6, 18, 5, 4, 12
        col = lambda v: v.rearrange("(p o) -> p o", o=1)
        row = lambda v: v.rearrange("(o c) -> o c", o=1).broadcast_to([P, C])

        ctx.enter_context(nc.allow_non_contiguous_dma(reason="biases and scales, a channel a partition"))
        block = ctx.enter_context(nc.Block())

        @block.sync
        def _(sp):
            x_d = a["x"].rearrange("b h w c -> (b h w) c").rearrange("(t p) c -> p t c", p=P)
            o_d = out.rearrange("b h w c -> (b h w) c").rearrange("(t p) c -> p t c", p=P)
            w_d = a["L0_conv_w1"].rearrange("h w n i o r -> (n i) (h w) (o r)")
            b_d = a["L0_conv_b1"].rearrange("h w n o r -> n (h w) (o r)")
            for c in range(CHUNKS):
                sp.dma_start(X[:, CT * c:CT * c + CT, :], x_d[:, CT * c:CT * c + CT, :]).then_inc(x_loaded[c], 16)
                if c == 0:
                    sp.dma_start(const_a[:, :], a["const_a"]).then_inc(const_a_loaded, 16)
            sp.wait_ge(n1_zero, 2)
            for v, t in ((a["L0_conv_norm1_w"], n1g), (a["L0_conv_norm1_b"], n1b)):
                for g in range(2):
                    sp.dma_start(t[64 * g:64 * g + GR, :], col(v[GR * g:GR * g + GR])).then_inc(n1_loaded, 16)
            for g in (1, 0):
                sp.dma_start(spec_w[g][0:GR], w_d[GR * g:GR * g + GR]).then_inc(block_w_loaded[g], 16)
            for g in range(2):
                sp.dma_start(spec_x[g][GR:64].rearrange("p q n b -> p (q n b)"), a["const_rows"]
                             ).then_inc(spec_x_rows, 16)
                sp.dma_start(spec_w[g][GR:GR + GB], b_d[GB * g:GB * g + GB]).then_inc(spec_w_loaded, 16)
                sp.dma_start(spec_w[g][GR + GB:64].rearrange("p q m -> p (q m)"),
                             a["const_rows"][GB:, 0:POS * BINS]).then_inc(spec_w_loaded, 16)
            sp.dma_start(qw1[:, :, :], a["L2_ffn_W1"].rearrange("(k p) c -> p k c", p=P)).then_inc(q_loaded, 16)
            sp.dma_start(qw2[:, :], a["L2_ffn_W2"]).then_inc(q_loaded, 16)
            sp.dma_start(qb1[:, :], a["L2_ffn_b1"].rearrange("(k p) -> p k", p=P)).then_inc(q_loaded, 16)
            sp.dma_start(bias_row[F2][:, :], row(a["L2_ffn_b2"])).then_inc(q_loaded, 16)
            sp.dma_start(const_b[:, :], a["const_b"]).then_inc(const_b_loaded, 16)
            sp.dma_start(mlp_w1[0][:, :], a["L0_conv_mlp_w1"]).then_inc(l0_loaded, 16)
            sp.dma_start(mlp_b1[0][:, :], a["L0_conv_mlp_b1"].rearrange("(k p) -> p k", p=P)).then_inc(l0_loaded, 16)
            sp.dma_start(mlp_w2[0][:, :, :], a["L0_conv_mlp_w2"].rearrange("(k p) c -> p k c", p=P)).then_inc(l0_loaded, 16)
            sp.dma_start(bias_row[L0B][:, :], row(a["L0_conv_mlp_b2"])).then_inc(l0_loaded, 16)
            sp.dma_start(affine[L0B][0][:, :], col(a["L0_conv_norm2_w"])).then_inc(l0_loaded, 16)
            sp.dma_start(affine[L0B][1][:, :], col(a["L0_conv_norm2_b"])).then_inc(l0_loaded, 16)
            l1 = [(affine[L1A][0][:, :], col(a["L1_conv_n1_g"])), (affine[L1A][1][:, :], col(a["L1_conv_n1_b"])),
                  (affine[L1B][0][:, :], col(a["L1_conv_n2_g"])), (affine[L1B][1][:, :], col(a["L1_conv_n2_b"])),
                  (w_in[:, :], a["L1_conv_w_in"]),
                  (b_in[0][:, :], col(a["L1_conv_b_in"][0:P])), (b_in[1][:, :], col(a["L1_conv_b_in"][P:INNER])),
                  (on_g[:, :], a["L1_conv_on_g"].rearrange("(k p) -> p k", p=C)),
                  (on_b[:, :], a["L1_conv_on_b"].rearrange("(k p) -> p k", p=C)),
                  (w_out[:, :, :], a["L1_conv_w_out"].rearrange("(k p) c -> p k c", p=C)),
                  (bias_row[L1A][:, :], row(a["L1_conv_b_out"])),
                  (mlp_w1[1][:, :], a["L1_conv_w1"]),
                  (mlp_b1[1][:, :], a["L1_conv_b1"].rearrange("(k p) -> p k", p=P)),
                  (mlp_w2[1][:, :, :], a["L1_conv_w2"].rearrange("(k p) c -> p k c", p=P)),
                  (bias_row[L1B][:, :], row(a["L1_conv_b2"]))]
            k_d = a["L1_conv_k_conv"].rearrange("y x o c -> c (y x o)")
            l1 += [(kcol[0][:, :], k_d[0:P]), (kcol[1][0:IN2, :], k_d[P:INNER]), (kcol[1][IN2:P, :], k_d[P:INNER])]
            for dst, src in l1:
                sp.dma_start(dst, src).then_inc(l1_loaded, 16)
            for i, name in enumerate(("L2_attn_w_attn", "L3_attn_W_qkv")):
                sp.dma_start(w_qkv[i][:, :], a[name]).then_inc(l2_loaded, 16)
            for i, name in enumerate(("L2_attn_w_proj", "L3_attn_W_proj")):
                sp.dma_start(w_proj[i][:, :], a[name]).then_inc(l2_loaded, 16)
            sp.dma_start(bias_row[A3][:, :], row(a["L3_attn_b_proj"])).then_inc(l2_loaded, 16)
            sp.dma_start(gate_w[:, :], a["L3_ffn_gate_w"]).then_inc(l3_loaded, 16)
            sp.dma_start(gate_b[:, :], a["L3_ffn_gate_b"].rearrange("(o e) -> o e", o=1).broadcast_to([P, NE])
                         ).then_inc(l3_loaded, 16)
            for e in range(NE):
                sp.dma_start(e_w1[:, e, :], a["L3_ffn_w1"][e]).then_inc(l3_loaded, 16)
                sp.dma_start(e_w2[:, e], a["L3_ffn_w2"][e].rearrange("(k p) c -> p k c", p=P)).then_inc(l3_loaded, 16)
            sp.dma_start(e_b1[:, :, :], a["L3_ffn_b1"].rearrange("e (k p) -> p e k", p=P)).then_inc(l3_loaded, 16)
            sp.dma_start(e_b2[:, :, :].rearrange("p e c -> p (e c)"),
                         a["L3_ffn_b2"].rearrange("(o e) c -> o (e c)", o=1).broadcast_to([P, NE * C])).then_inc(l3_loaded, 16)
            for c in MOE_CHUNKS:
                landed(sp, "edown", NE * MOE_CHUNKS.index(c) + NE - 1)
                sp.dma_start(o_d[:, CT * c:CT * c + CT, :], X[:, CT * c:CT * c + CT, :]).then_inc(stored, 16)
            sp.wait_ge(stored, 16 * CHUNKS)

        @block.tensor
        def _(pe):
            def turn(l, c, src, width=CT):
                pe.wait_ge(normed_ready, LN_NO[l, c])
                ps, filled = pe_bank(pe, "turn", l, c)
                for t in range(width):
                    mm = nc.tensor.transpose(ps[0:C, tok(t)], src[:, CT * c + t, :], ident)
                mm.then_inc(filled, 1)

            def keep_warm(n, *key):
                ps, _ = pe_bank(pe, *key)
                for _ in range(n):
                    nc.tensor.matmul(ps[:, 0:256], idle_w[:, 0:P], idle_w[:, :], start=True, stop=True)

            def down(l, c, src, w, width=CT):
                ps, filled = pe_bank(pe, "down", l, c)
                for t in range(width):
                    for k in range(len(src)):
                        mm = nc.tensor.matmul(ps[:, C * t:C * t + C], src[k][:, tok(t)], w[k],
                                              start=(k == 0), stop=(k == len(src) - 1))
                mm.then_inc(filled, 1)

            def signprep():
                pe.wait_ge(q_loaded, 16 * Q_DMAS)
                ps, filled = pe_bank(pe, "signprep", 0)
                for k in range(HT):
                    mm = nc.tensor.transpose(ps[0:C, tok(k)], qw1[:, k, :], ident)
                mm.then_inc(filled, 1)
                ps, filled = pe_bank(pe, "signprep", 1)
                for k in range(HT):
                    mm = nc.tensor.transpose(ps[:, C * k:C * k + C], qw2[:, tok(k)], ident[0:C, 0:C])
                mm.then_inc(filled, 1)

            def sign_means():
                pe.wait_ge(ones_ready, 1)
                landed(pe, "signprep", 0)
                landed(pe, "signprep", 1)
                ps, filled = pe_bank(pe, "sign_means")
                nc.tensor.matmul(ps[:, 0:QG], ones[0:C, :], qsum[0:C, 0, :], start=True, stop=True)
                nc.tensor.matmul(ps[:, QG:2 * QG], ones[:, :], qsum[:, 1, :], start=True, stop=True
                                 ).then_inc(filled, 1)

            def up(m, c):
                landed(pe, "turn", MLP_NORM[m], c)
                for k in range(HT):
                    ps, filled = pe_bank(pe, "up", m, c, k)
                    nc.tensor.matmul(ps[:, :], mlp_w1[m][:, tok(k)], normed_t[MLP_NORM[m] % 2][:, ctok(c)],
                                     start=True, stop=True).then_inc(filled, 1)

            pe.wait_ge(idle_ready, 1)
            keep_warm(WARM["start"], "dft", 0)
            pe.wait_ge(const_a_loaded, 16)
            pe.wait_ge(gap_zero, 1)
            for b in range(B):
                pe.wait_ge(normed_ready, LN_NO[L0A, b // IMGS])
                ps, filled = pe_bank(pe, "dft", b)
                for h in range(HALVES):
                    mm = nc.tensor.matmul(ps[0:64 + GR, 0:2 * POS], normed_s[:, HALVES * b + h, 0:64 + GR],
                                          dft[:, h, :], start=(h == 0), stop=(h == HALVES - 1))
                mm.then_inc(filled, 1)
            keep_warm(WARM["spec"], "spec", 0)
            pe.wait_ge(spec_w_loaded, 16 * SPEC_W_DMAS)
            pe.wait_ge(spec_w_rows, 4)
            pe.wait_ge(spec_x_rows, 16 * 2)
            pe.wait_ge(spec_x_dve, 2 * len(SPEC_DVE))
            pe.wait_ge(spec_x_act, 2 * len(SPEC_ACT))
            for p in range(POS):
                if p % PPB == 0:
                    ps, filled = pe_bank(pe, "spec", p // PPB)
                for g in range(2):
                    mm = nc.tensor.matmul(ps[32 * g:32 * g + 32, BINS * (p % PPB):BINS * (p % PPB) + BINS],
                                          spec_x[g][0:64 + GR, p, :, :].rearrange("p n b -> p (n b)"),
                                          spec_w[g][0:64 + GR, p, :], start=True, stop=True)
                if p % PPB == PPB - 1 or p == POS - 1:
                    mm.then_inc(filled, 1)
            for k in range(KT):
                for n in range((KP * (k + 1) - 1) // PPB + 1):
                    landed(pe, "spec", n)
                for j in range(2):
                    ps, filled = pe_bank(pe, "spec_t", k, j)
                    for o in range(OH):
                        oo = OH * j + o
                        mm = nc.tensor.transpose(ps[0:KROWS, 64 * o:64 * o + 64],
                                                 spec_o[:, oo, KP * k:KP * k + KP, :].rearrange("p q r -> p (q r)"),
                                                 ident[0:64, 0:64])
                    mm.then_inc(filled, 1)
            pe.wait_ge(const_b_loaded, 16)
            for h in range(HALVES):
                for j in range(2):
                    ps, filled = pe_bank(pe, "inv", 2 * h + j)
                    for k in range(KT):
                        landed(pe, "spec_t", k, j)
                        mm = nc.tensor.matmul(ps[:, 0:64 * OH], idft[0:KROWS, k, tok(h)],
                                              spec_ot[:, k, OH * j:OH * j + OH, :].rearrange("p o m -> p (o m)"),
                                              start=(k == 0), stop=(k == KT - 1))
                    mm.then_inc(filled, 1)
            keep_warm(WARM["inverse"], "turn", L0B, 0)
            turn(L0B, 0, normed[L0B % 2])
            pe.wait_ge(l0_loaded, 16 * L0_DMAS)
            for what, *args in CONV_PE:
                x = args[0] if args else None
                if (what, *args) in WARM:
                    keep_warm(WARM[(what, *args)], what, *args, *((0,) if what == "turn_m" else ()))
                if what == "up":
                    up(*args)
                elif what == "down":
                    m, c = args
                    for k in range(HT):
                        landed(pe, "up", m, c, k)
                    down(MLP_NORM[m], c, [hidden[:, c % 2, k, :] for k in range(HT)],
                         [mlp_w2[m][:, k, :] for k in range(HT)])
                elif what == "signprep":
                    signprep()
                elif what == "sign_means":
                    sign_means()
                elif what == "turn":
                    turn(*args, normed[x % 2])
                elif what == "win":
                    if x == 0:
                        pe.wait_ge(l1_loaded, 16 * L1_DMAS)
                    landed(pe, "turn", L1A, x)
                    for k, (lo, n) in enumerate(((0, P), (P, IN2))):
                        ps, filled = pe_bank(pe, "win", x, k)
                        nc.tensor.matmul(ps[0:n, :], w_in[:, lo:lo + n], normed_t[L1A % 2][:, ctok(x)],
                                         start=True, stop=True).then_inc(filled, 1)
                elif what == "taps":
                    k, first = int(x[0] == "s"), IMGS * int(x[1])
                    pe.wait_ge(diag_ready, 2 * PE_TAPS)
                    pe.wait_ge(pad_zero, 2)
                    for c in unit_chunks(x):
                        landed(pe, "win", c, k)
                    for im in range(IMGS):
                        ps, filled = pe_bank(pe, "taps", x, im)
                        for n in range(PE_TAPS):
                            dy, dx = TAPS[n]
                            mm = nc.tensor.matmul(ps[:, 0:TOK], tap_diag[:, k, n, :], window(k, first + im, dy, dx),
                                                  start=(n == 0), stop=(n == PE_TAPS - 1))
                        mm.then_inc(filled, 1)
                elif what == "loc":
                    k, first = int(x[0] == "s"), IMGS * int(x[1])
                    pe.wait_ge(conv_step, tap_no(x, len(TAPS) - 1))
                    ps, filled = pe_bank(pe, "loc", x)
                    for im in range(IMGS):
                        for h in range(HALVES):
                            mm = nc.tensor.transpose(ps[:, tok(HALVES * im + h)], conv[k][:, first + im, tok(h)],
                                                     ident)
                    mm.then_inc(filled, 1)
                elif what == "mix":
                    landed(pe, "loc", f"m{x}")
                    landed(pe, "loc", f"s{x // 2}")
                    for ho in range(HALVES):
                        ps, filled = pe_bank(pe, "mix", x, ho)
                        for hi in range(HALVES):
                            mm = nc.tensor.matmul(
                                ps[:, 0:IMGS * INNER], mix[:, hi, tok(ho)],
                                loc[:, hi, IMGS * x:IMGS * x + IMGS, :].rearrange("p b c -> p (b c)"),
                                start=(hi == 0), stop=(hi == HALVES - 1))
                        mm.then_inc(filled, 1)
                elif what == "turn_m":
                    pe.wait_ge(normed_ready, LN_NO[L1M, x])
                    for k in range(2):
                        ps, filled = pe_bank(pe, "turn_m", x, k)
                        for t in range(CT):
                            mm = nc.tensor.transpose(ps[0:C, tok(t)], mixed[:, CT * x + t, C * k:C * k + C], ident)
                        mm.then_inc(filled, 1)
                elif what == "wout":
                    landed(pe, "turn_m", x, 0)
                    landed(pe, "turn_m", x, 1)
                    down(L1A, x, [mixed_t[k][:, ctok(x)] for k in range(2)], [w_out[:, k, :] for k in range(2)])

            def qkv(what, j):
                a, c = SLOTS[j]
                l = slot_norm(j)
                if what == "q":
                    landed(pe, "turn", l, c)
                ps, filled = pe_bank(pe, what, j)
                if what == "v":
                    for t in range(CT):
                        mm = nc.tensor.matmul(ps[:, C * t:C * t + C], normed_t[l % 2][:, tok(CT * c + t)],
                                              w_qkv[a][:, 2 * C:3 * C], start=True, stop=True)
                else:
                    k = int(what == "k")
                    mm = nc.tensor.matmul(ps[0:C, :], w_qkv[a][:, C * k:C * k + C], normed_t[l % 2][:, ctok(c)],
                                          start=True, stop=True)
                mm.then_inc(filled, 1)

            pe.wait_ge(l2_loaded, 16 * L2_DMAS)
            for what in ("q", "k", "v"):
                qkv(what, 0)
            for s, hooks in stream():
                if s < STEPS:
                    j, (im, h) = s // NI, ITEMS[s % NI]
                    if s == 0:
                        keep_warm(WARM["scores"], "s", 0)
                    if s % NI == 0:
                        landed(pe, "k", j)
                        pe.wait_ge(q_heads_ready, NH * (j + 1))
                    t0 = CN * SLOTS[j][1] + TOK * im
                    ps, filled = pe_bank(pe, "s", s)
                    for n, (q0, k0) in enumerate(((0, 0), (P, 0), (P, P))):
                        diagonal = q0 == k0
                        if diagonal:
                            nc.tensor.matmul(ps[:, tok(n)], ident_b[:, :], mask_b[:, :], start=True, stop=False)
                        mm = nc.tensor.matmul(ps[:, tok(n)], q_heads[:, j % 2, h, TOK * im + q0:TOK * im + q0 + P],
                                              k_t[:, t0 + k0:t0 + k0 + P], start=not diagonal, stop=True)
                    mm.then_inc(filled, 1)
                i = s - 2
                if 0 <= i < STEPS:
                    landed(pe, "s", i)
                    ps, filled = pe_bank(pe, "pt", i)
                    for k in range(3):
                        mm = nc.tensor.transpose(ps[:, tok(k)], probs[:, i % 3, tok(k)], ident)
                    mm.then_inc(filled, 1)
                i = s - 3
                if 0 <= i < STEPS:
                    j, (im, h) = i // NI, ITEMS[i % NI]
                    g, r = int(h >= 4), 32 * (h % 4)
                    if i % NI in (0, IMGS * len(HEAD_GROUPS[0])):
                        o_bank = pe_bank(pe, "o", j, g)
                    if i % NI == 0:
                        landed(pe, "v", j)
                    ps, filled = o_bank
                    landed(pe, "pt", i)
                    t0 = CT * SLOTS[j][1] + HALVES * im
                    nc.tensor.matmul(ps[r:r + 32, TOK * im:TOK * im + TOK], v_sb[:, t0, h, :],
                                     probs_t[:, i % 3, 0:TOK], start=True, stop=False)
                    mm = nc.tensor.matmul(ps[r:r + 32, TOK * im + P:TOK * im + TOK], v_sb[:, t0 + 1, h, :],
                                          probs_t[:, i % 3, TOK:384], start=False, stop=True)
                    if i % NI in (IMGS * len(HEAD_GROUPS[0]) - 1, NI - 1):
                        mm.then_inc(filled, 1)
                for what, *x in hooks:
                    if what in ("q", "k", "v"):
                        qkv(what, *x)
                    if what == "turn_o":
                        j, im = x
                        landed(pe, "o", j, 0)
                        landed(pe, "o", j, 1)
                        ps, filled = pe_bank(pe, what, j, im)
                        for t in range(HALVES):
                            for g, heads in enumerate(HEAD_GROUPS):
                                rows, lo = 32 * len(heads), 32 * (NH * t + heads[0])
                                mm = nc.tensor.transpose(ps[:, lo:lo + rows],
                                                         o_raw[0:rows, j % 2, g, tok(HALVES * im + t)],
                                                         ident[0:rows, 0:rows])
                        mm.then_inc(filled, 1)
                    if what == "turn_n":
                        j, = x
                        for im in range(IMGS):
                            landed(pe, "turn_o", j, im)
                        ps, filled = pe_bank(pe, what, j)
                        for t in range(CT):
                            mm = nc.tensor.transpose(ps[0:C, tok(t)], o_norm[:, j % 2, t, :], ident)
                        mm.then_inc(filled, 1)
                    if what == "proj":
                        j, = x
                        landed(pe, "turn_n", j)
                        ps, filled = pe_bank(pe, "down", j)
                        for t in range(CT):
                            mm = nc.tensor.matmul(ps[:, C * t:C * t + C], o_t[:, j % 2, tok(t)],
                                                  w_proj[SLOTS[j][0]][:, :], start=True, stop=True)
                        mm.then_inc(filled, 1)
                    if what == "turn":
                        l, c = x
                        turn(l, c, normed[l % 2], dict(chunks_of(l))[c])
                    if what == "qup":
                        c, k = x
                        if k == 0:
                            landed(pe, "turn", F2, c)
                        if (c, k) == (0, 0):
                            pe.wait_ge(sign_ready, 4)
                        n = TOK * len(images(c))
                        ps, filled = pe_bank(pe, what, c, k)
                        nc.tensor.matmul(ps[:, 0:n], sign1[:, tok(k)], normed_t[F2 % 2][:, ctok(c, n)],
                                         start=True, stop=True).then_inc(filled, 1)
                    if what == "gamma_max":
                        k, n_images = gamma_no(*x)
                        n, c = x
                        w = len(images(c))
                        pe.wait_ge(qmax_ready, n_images)
                        ps, filled = pe_bank(pe, what, *x)
                        nc.tensor.transpose(ps[0:w, 0:P], qmax[:, n, IMGS * c:IMGS * c + w], ident).then_inc(filled, 1)
                    if what == "gamma_spread":
                        k, _ = gamma_no(*x)
                        w = len(images(x[1]))
                        pe.wait_ge(qchain, 3 * k + 3)
                        ps, filled = pe_bank(pe, what, *x)
                        nc.tensor.matmul(ps[:, 0:w], ones[0:w, :], qdiag[0:w, k, 0:w], start=True, stop=True
                                         ).then_inc(filled, 1)
                    if what == "qdown":
                        c, = x
                        pe.wait_ge(qh_ready, images(c)[-1] + 1)
                        ps, filled = pe_bank(pe, what, c)
                        for t in range(HALVES * len(images(c))):
                            for k in range(HT):
                                mm = nc.tensor.matmul(ps[:, C * t:C * t + C], qh[:, k, tok(t)], sign2[:, k, :],
                                                      start=(k == 0), stop=(k == HT - 1))
                        mm.then_inc(filled, 1)
                    if what == "gate_scores":
                        c, = x
                        pe.wait_ge(l3_loaded, 16 * L3_DMAS)
                        landed(pe, "turn", MO, c)
                        ps, filled = pe_bank(pe, what, c)
                        for t in range(CT):
                            mm = nc.tensor.matmul(ps[:, NE * t:NE * t + NE], normed_t[MO % 2][:, tok(CT * c + t)],
                                                  gate_w[:, :], start=True, stop=True)
                        mm.then_inc(filled, 1)
                    if what == "eup":
                        i, = x
                        c, e = MOE_CHUNKS[i // NE], i % NE
                        m = i // NE
                        pe.wait_ge(w_split, 3 * NE)
                        pe.wait_ge(x_split, 3 * (m + 1))
                        for k in range(HT):
                            ps, filled = pe_bank(pe, what, i, k)
                            for n, (w, x) in enumerate(((w_hi, x_hi), (w_hi, x_lo), (w_lo, x_hi))):
                                mm = nc.tensor.matmul(ps[:, :], w[:, e, tok(k)], x[:, m % 2, :], start=(n == 0), stop=(n == 2))
                            mm.then_inc(filled, 1)
                    if what == "edown":
                        i, = x
                        ps, filled = pe_bank(pe, what, i)
                        for k in range(HT):
                            landed(pe, "eup", i, k)
                        for t in range(CT):
                            for k in range(HT):
                                mm = nc.tensor.matmul(ps[:, C * t:C * t + C], hidden[:, i % 2, k, tok(t)],
                                                      e_w2[:, i % NE, k, :], start=(k == 0), stop=(k == HT - 1))
                        mm.then_inc(filled, 1)

        @block.scalar
        def _(act):
            def turned(l, c, width=CT):
                ps, drained = read_bank(act, "turn", l, c)
                dst = normed_t[l % 2][:, ctok(c, P * width)]
                if l in affine:
                    g, b = affine[l]
                    nc.scalar.activation(dst, ps[0:C, 0:P * width], ACT.Identity, bias=b[:, :],
                                         scale=g[:, :]).then_inc(drained, 1)
                else:
                    nc.scalar.activation(dst, ps[0:C, 0:P * width], ACT.Copy).then_inc(drained, 1)

            act.wait_ge(const_a_loaded, 16)
            act.wait_ge(n1_loaded, 16 * 4)
            for bh in range(2):
                for b in range(B // 2 * bh, B // 2 * bh + B // 2):
                    ps, drained = read_bank(act, "dft", b)
                    nc.scalar.activation(spec_f[0:64 + GR, b].rearrange("p r q -> p (r q)"), ps[0:64 + GR, 0:2 * POS],
                                         ACT.Identity, scale=n1g[0:64 + GR, :]).then_inc(drained, 1)
                act.wait_ge(dc_ready, bh + 2)
                for g, ri, n in SPEC_ACT:
                    dst, src, mask = spec_copy(g, ri, n, bh)
                    nc.scalar.activation(dst, src, ACT.Copy, scale=mask).then_inc(spec_x_act, 1)
            act.wait_ge(block_w_loaded[0], 16)
            nc.scalar.activation(spec_w[0][64:64 + GR, :, 0:BINS:2], spec_w[0][0:GR, :, 1:BINS:2], ACT.Copy,
                                 scale=-1.0).then_inc(spec_w_rows, 1)
            nc.scalar.activation(spec_w[0][64:64 + GR, :, 1:BINS:2], spec_w[0][0:GR, :, 0:BINS:2],
                                 ACT.Copy).then_inc(spec_w_rows, 1)
            for n in range(0, SBANKS, 2):
                ps, drained = read_bank(act, "spec", n)
                dst, src = relu_spec(n)
                nc.scalar.activation(dst, src, ACT.Relu).then_inc(drained, 1)
            for k in range(KT):
                ps, drained = read_bank(act, "spec_t", k, 0)
                nc.scalar.activation(spec_ot[:, k, 0:OH, :].rearrange("p o m -> p (o m)"),
                                     ps[0:KROWS, 0:64 * OH], ACT.Copy).then_inc(drained, 1)
            for h in range(HALVES):
                ps, drained = read_bank(act, "inv", 2 * h)
                nc.scalar.activation(inv_out(h, 0), ps[:, 0:64 * OH].rearrange("p (o n b) -> p o n b", o=OH, b=B),
                                     ACT.Copy).then_inc(drained, 1)
            act.wait_ge(l0_loaded, 16 * L0_DMAS)
            turned(L0B, 0)

            for what, *args in CONV_PE:
                x = args[0] if args else None
                if what == "up":
                    m, c = args
                    for k in range(HT):
                        ps, drained = read_bank(act, "up", m, c, k)
                        nc.scalar.activation(hidden[:, c % 2, k, :], ps[:, :], ACT.Gelu,
                                             bias=mlp_b1[m][:, k:k + 1]).then_inc(drained, 1)
                elif what == "signs":
                    act.wait_ge(sign_centred, 2)
                    nc.scalar.activation(sign1[:, 0:QG * G1], qw1_t[:, 0:QG * G1], ACT.Sign).then_inc(sign_ready, 1)
                    nc.scalar.activation(sign2[:, :, 0:QG * G2], qw2_t[:, :, 0:QG * G2], ACT.Sign
                                         ).then_inc(sign_ready, 1)
                elif what == "turn":
                    if tuple(args) == (L1A, 0):
                        act.wait_ge(l1_loaded, 16 * L1_DMAS)
                    turned(*args)
                elif what == "win":
                    if x == 0:
                        act.wait_ge(pad_zero, 2)
                    lo = LEAD + IMG * IMGS * x
                    ps, drained = read_bank(act, "win", x, 0)
                    dst = pad[0][:, lo:lo + IMGS * IMG].rearrange("p (b y x) -> p b y x", b=IMGS, x=PW)
                    nc.scalar.activation(dst[:, :, 0:HH, 0:WW],
                                         ps[:, :].rearrange("p (b y x) -> p b y x", b=IMGS, x=WW),
                                         ACT.Identity, bias=b_in[0][:, :]).then_inc(drained, 1)
                    r, lo = 64 * (x % 2), LEAD + IMG * IMGS * (x // 2)
                    ps, drained = read_bank(act, "win", x, 1)
                    dst = pad[1][r:r + IN2, lo:lo + IMGS * IMG].rearrange("p (b y x) -> p b y x", b=IMGS, x=PW)
                    nc.scalar.activation(dst[:, :, 0:HH, 0:WW],
                                         ps[0:IN2, :].rearrange("p (b y x) -> p b y x", b=IMGS, x=WW),
                                         ACT.Identity, bias=b_in[1][:, :]).then_inc(drained, 1)
                elif what == "loc":
                    ps, drained = read_bank(act, "loc", x)
                    n = int(x[1])
                    for im in range(IMGS):
                        if x[0] == "m":
                            src = ps[:, tok(HALVES * im, HALVES * P)].rearrange("p (h c) -> p h c", h=HALVES)
                            last = nc.scalar.activation(loc[:, :, IMGS * n + im, 0:P], src, ACT.Copy)
                        else:
                            src = ps[:, tok(HALVES * im, HALVES * P)].rearrange("p (h k c) -> p h k c",
                                                                               h=HALVES, k=2)
                            b = 2 * IMGS * n + im
                            last = nc.scalar.activation(loc[:, :, b:b + IMGS + 1:IMGS, P:INNER], src, ACT.Copy)
                    last.then_inc(drained, 1)
                elif what == "turn_m":
                    for k in range(2):
                        ps, drained = read_bank(act, "turn_m", x, k)
                        nc.scalar.activation(mixed_t[k][:, ctok(x)], ps[0:C, :], ACT.Identity,
                                             bias=on_b[:, k:k + 1], scale=on_g[:, k:k + 1]).then_inc(drained, 1)

            def qkv(what, j):
                if what == "v":
                    return
                ps, drained = read_bank(act, what, j)
                dst = q_raw[:, j % 2, :] if what == "q" else k_t[:, ctok(SLOTS[j][1])]
                nc.scalar.activation(dst, ps[0:C, :], ACT.Copy).then_inc(drained, 1)

            for what in ("q", "k"):
                qkv(what, 0)
            for s, hooks in stream():
                i = s - 2
                if 0 <= i < STEPS and i % 2:
                    ps, drained = read_bank(act, "pt", i)
                    nc.scalar.activation(probs_t[:, i % 3, :], ps[:, 0:384], ACT.Copy).then_inc(drained, 1)
                if s < STEPS:
                    ps, drained = read_bank(act, "s", s)
                    act.wait_ge(nmax_ready, s + 1)
                    nc.scalar.activation(probs[:, s % 3, 0:P], ps[:, 0:P], ACT.Exp, bias=nmax[:, s % 3, 0:1])
                    nc.scalar.activation(probs[:, s % 3, P:384], ps[:, P:384], ACT.Exp,
                                         bias=nmax[:, s % 3, 1:2]).then_inc(drained, 1)
                for what, *x in hooks:
                    if what in ("q", "k", "v"):
                        qkv(what, *x)
                    if what == "evac_o":
                        j, g = x
                        ps, drained = read_bank(act, "o", j, g)
                        rows = 32 * len(HEAD_GROUPS[g])
                        nc.scalar.activation(o_raw[0:rows, j % 2, g, :], ps[0:rows, :], ACT.Copy).then_inc(drained, 1)
                    if what == "turn_n":
                        j, = x
                        ps, drained = read_bank(act, what, j)
                        nc.scalar.activation(o_t[:, j % 2, :], ps[0:C, :], ACT.Copy).then_inc(drained, 1)
                    if what == "turn":
                        l, c = x
                        turned(l, c, dict(chunks_of(l))[c])
                    if what == "qup":
                        c, k = x
                        n = TOK * len(images(c))
                        ps, drained = read_bank(act, what, c, k)
                        nc.scalar.activation(qy1[:, k, 0:n], ps[:, 0:n], ACT.Identity,
                                             bias=qb1[:, k:k + 1]).then_inc(drained, 1)
                    if what == "qgelu":
                        for im, b in enumerate(images(*x)):
                            act.wait_ge(qclip, 2 * b + 2)
                            nc.scalar.activation(qh[:, :, tok(HALVES * im, TOK)], qy1[:, :, tok(HALVES * im, TOK)],
                                                 ACT.Gelu).then_inc(qh_ready, 1)
                    if what == "gate_scores":
                        c, = x
                        act.wait_ge(gate_step, GATE_STEPS * MOE_CHUNKS.index(c) + 2)
                        v = score[:, CT * c:CT * c + CT, :]
                        nc.scalar.activation(v, v, ACT.Exp).then_inc(gate_exp_ready, 1)
                    if what == "eup":
                        i, = x
                        for k in range(HT):
                            ps, drained = read_bank(act, what, i, k)
                            nc.scalar.activation(hidden[:, i % 2, k, :], ps[:, :], ACT.Gelu,
                                                 bias=e_b1[:, i % NE, k:k + 1]).then_inc(drained, 1)

        @block.vector
        def _(dve):
            def moments_of(l, c, src, width=CT):
                no = LN_NO[l, c]
                t0 = CT * c
                for t in range(width):
                    ins = nc.vector.bn_stats(stats[:, l, t0 + t, :], src(t))
                ins.then_inc(stats_ready, 1)
                dve.wait_ge(stats_ready, no)
                for t in range(width):
                    ins = nc.vector.bn_aggr(moments[:, l, t0 + t, :], stats[:, l, t0 + t, :])
                ins.then_inc(moments_ready, 1)

            def scaled(l, c, src, width=CT):
                no = LN_NO[l, c]
                t0 = CT * c
                dve.wait_ge(rstd_ready, no)
                for t in range(width):
                    if l == L0A:
                        dst = normed_s[:, t0 + t, :].rearrange("p (g c) -> p g c", g=2)[:, :, 0:GR]
                        v = src(t).rearrange("p (g c) -> p g c", g=2)
                    else:
                        dst = mixed[:, t0 + t, :] if l == L1M else normed[l % 2][:, t0 + t, :]
                        v = src(t)
                    ins = nc.vector.tensor_scalar(dst, v, moments[:, l, t0 + t, 0:1], rstd[:, l, t0 + t:t0 + t + 1],
                                                  ALU.subtract, ALU.mult)
                ins.then_inc(normed_ready, 1)

            def norm(l, c, src):
                moments_of(l, c, src)
                scaled(l, c, src)

            def norms(l, chunks, src_of):
                for c in chunks:
                    moments_of(l, c, src_of(c))
                    if c > chunks[0]:
                        scaled(l, c - 1, src_of(c - 1))
                scaled(l, c, src_of(c))

            def x_tile(c):
                return lambda t: X[:, CT * c + t, :]

            def update(l, c):
                ps, drained = read_bank(dve, "down", l, c)
                if l in BIASED:
                    dve.wait_ge(bias_added, bias_no(l, c))
                v = X[:, CT * c:CT * c + CT, :]
                nc.vector.tensor_tensor(v, ps[:, 0:C * CT].rearrange("p (t c) -> p t c", c=C), v,
                                        ALU.add).then_inc(drained, 1)
                landed(dve, "down", l, c)

            def centre_signs():
                ps, drained = read_bank(dve, "sign_means")
                nc.vector.tensor_scalar(qmean[:, 0, :], ps[:, 0:QG], 1.0 / (G1 * C), None, ALU.mult)
                nc.vector.tensor_scalar(qmean[:, 1, :], ps[:, QG:2 * QG], 1.0 / (G2 * HID), None,
                                        ALU.mult).then_inc(drained, 1)
                dve.wait_ge(sign_copied, 2)
                landed(dve, "sign_means")
                v = qw1_t[:, 0:QG * G1].rearrange("p (g m) -> p g m", g=QG)
                nc.vector.tensor_tensor(v, v, qmean[0:C, 0, :].unsqueeze(2).broadcast_to([C, QG, G1]),
                                        ALU.subtract).then_inc(sign_centred, 1)
                for k in range(HT):
                    v = qw2_t[:, k, 0:QG * G2].rearrange("p (g m) -> p g m", g=QG)
                    ins = nc.vector.tensor_tensor(v, v, qmean[:, 1, :].unsqueeze(2).broadcast_to([P, QG, G2]),
                                                  ALU.subtract)
                ins.then_inc(sign_centred, 1)

            nc.vector.memset(idle_w[:, :], 0.0).then_inc(idle_ready, 1)
            for c in range(CHUNKS):
                dve.wait_ge(x_loaded[c], 16)
                moments_of(L0A, c, x_tile(c))
                if c:
                    scaled(L0A, c - 1, x_tile(c - 1))
            scaled(L0A, c, x_tile(c))
            dve.wait_ge(const_a_loaded, 16)
            dve.wait_ge(n1_loaded, 16 * 4)
            nc.vector.tensor_scalar(n1b16[0:64 + GR, :], n1b[0:64 + GR, :], float(TOK) ** 0.5, None,
                                    ALU.mult).then_inc(dc_ready, 1)
            dve.wait_ge(dc_ready, 1)
            for bh in range(2):
                halves = range(B // 2 * bh, B // 2 * bh + B // 2)
                for b in halves:
                    landed(dve, "dft", b)
                dc = spec_f[0:64 + GR, halves[0]:halves[-1] + 1, 0, 0]
                nc.vector.tensor_scalar(dc, dc, n1b16[0:64 + GR, :], None, ALU.add).then_inc(dc_ready, 1)
                dve.wait_ge(dc_ready, bh + 2)
                for g, ri, n in SPEC_DVE:
                    dst, src, mask = spec_copy(g, ri, n, bh)
                    nc.vector.tensor_scalar(dst, src, mask, None, ALU.mult).then_inc(spec_x_dve, 1)
            for n in range(1, SBANKS, 2):
                ps, drained = read_bank(dve, "spec", n)
                dst, src = relu_spec(n)
                nc.vector.tensor_scalar(dst, src, 0.0, None, ALU.max).then_inc(drained, 1)
            for k in range(KT):
                ps, drained = read_bank(dve, "spec_t", k, 1)
                nc.vector.tensor_copy(spec_ot[:, k, OH:BS, :].rearrange("p o m -> p (o m)"),
                                      ps[0:KROWS, 0:64 * OH]).then_inc(drained, 1)
            for h in range(HALVES):
                ps, drained = read_bank(dve, "inv", 2 * h + 1)
                nc.vector.tensor_copy(inv_out(h, 1),
                                      ps[:, 0:64 * OH].rearrange("p (o n b) -> p o n b", o=OH, b=B)
                                      ).then_inc(drained, 1)
            for k in range(2 * HALVES):
                landed(dve, "inv", k)
            norms(L0B, range(CHUNKS), lambda c: lambda t: xs[:, CT * c + t, :])
            ps, drained = read_bank(dve, "signprep", 0)
            nc.vector.tensor_copy(qw1_t[:, :], ps[0:C, 0:HID]).then_inc(sign_copied, 1)
            nc.vector.tensor_reduce(qsum[0:C, 0, :], ps[0:C, 0:QG * G1].rearrange("p (g m) -> p g m", g=QG),
                                    AX.X, ALU.add).then_inc(drained, 1)
            ps, drained = read_bank(dve, "signprep", 1)
            nc.vector.tensor_copy(qw2_t[:, :, :].rearrange("p k c -> p (k c)"), ps[:, 0:HT * C]
                                  ).then_inc(sign_copied, 1)
            nc.vector.tensor_reduce(
                qsum[:, 1, :],
                ps[:, 0:HT * C].rearrange("p (k c) -> p k c", k=HT)[:, :, 0:QG * G2].rearrange(
                    "p k (g m) -> p g k m", g=QG), AX.XY, ALU.add).then_inc(drained, 1)
            dve.wait_ge(l0_loaded, 16 * L0_DMAS)


            def conv_tap(u, n):
                k, first = int(u[0] == "s"), IMGS * int(u[1])
                dy, dx = TAPS[n]
                for im in range(IMGS):
                    dst = conv[k][:, first + im, :].rearrange("p (y x) -> p y x", x=WW)
                    src = window(k, first + im, dy, dx)
                    if n == PE_TAPS:
                        ps, drained = read_bank(dve, "taps", u, im)
                        nc.vector.scalar_tensor_tensor(dst, src, kcol[k][:, n:n + 1],
                                                       ps[:, 0:TOK].rearrange("p (y x) -> p y x", x=WW),
                                                       ALU.mult, ALU.add).then_inc(drained, 1)
                        continue
                    if n == PE_TAPS + 1:
                        landed(dve, "taps", u, im)
                    else:
                        dve.wait_ge(conv_step, tap_no(u, n - 1, im))
                    nc.vector.scalar_tensor_tensor(dst, src, kcol[k][:, n:n + 1], dst,
                                                   ALU.mult, ALU.add).then_inc(conv_step, 1)

            def mixed_tile(c):
                banks = [bank[uses["mix", c, ho][0]] for ho in range(HALVES)]
                return lambda t: banks[t % HALVES][:, INNER * (t // HALVES):INNER * (t // HALVES) + INNER]

            for what, *x in CONV_DVE:
                if what == "taps":
                    if x == ["m0", PE_TAPS]:
                        dve.wait_ge(l1_loaded, 16 * L1_DMAS)
                    conv_tap(*x)
                if what == "update":
                    update(*x)
                if what == "centre":
                    centre_signs()
                if what == "moments":
                    l, c = x
                    if l == L1M:
                        for ho in range(HALVES):
                            read_bank(dve, "mix", c, ho)
                    moments_of(l, c, mixed_tile(c) if l == L1M else x_tile(c))
                if what == "scale":
                    l, c = x
                    scaled(l, c, mixed_tile(c) if l == L1M else x_tile(c))
                    if l == L1M:
                        dve.wait_ge(normed_ready, LN_NO[L1M, c])
                        for ho in range(HALVES):
                            dve.sem_inc(bank_drained[uses["mix", c, ho][0]], 1)

            CLIP = QB - QEPS

            def qkv(what, j):
                if what == "q":
                    landed(dve, "q", j)
                    for h in range(NH):
                        nc.vector.tensor_scalar(q_heads[:, j % 2, h, :], q_raw[:, j % 2, :], hmask[0:C, h:h + 1],
                                                None, ALU.mult).then_inc(q_heads_ready, 1)
                if what == "v":
                    ps, drained = read_bank(dve, "v", j)
                    c = SLOTS[j][1]
                    dst = v_sb[:, CT * c:CT * c + CT].rearrange("p t h d -> p (t h) d")[:, :, 0:HD]
                    nc.vector.tensor_copy(dst, ps[:, 0:CT * C].rearrange("p (n d) -> p n d", d=HD)
                                          ).then_inc(drained, 1)

            gate_steps = [0]

            def then(ins):
                gate_steps[0] += 1
                ins.then_inc(gate_step, 1)
                dve.wait_ge(gate_step, gate_steps[0])

            def split(hi, lo, v, done, n):
                if n:
                    dve.wait_ge(done, 3 * n)
                elif done is x_split:
                    dve.wait_ge(w_split, 3 * NE)
                top = top_bits[:, 0:v.shape[-1]]
                nc.vector.tensor_scalar(top, v.bitcast(I32), -4096, None, ALU.bitwise_and).then_inc(done, 1)
                dve.wait_ge(done, 3 * n + 1)
                nc.vector.tensor_copy(hi, top.bitcast(F32)).then_inc(done, 1)
                nc.vector.tensor_tensor(lo, v, top.bitcast(F32), ALU.subtract).then_inc(done, 1)

            def gate_scores(c):
                sc, g1 = score[:, CT * c:CT * c + CT, :], gate1[:, CT * c:CT * c + CT]
                ps, drained = read_bank(dve, "gate_scores", c)
                nc.vector.tensor_tensor(sc, ps[:, 0:NE * CT].rearrange("p (t e) -> p t e", e=NE),
                                        gate_b[:, :].unsqueeze(1).broadcast_to([P, CT, NE]),
                                        ALU.add).then_inc(drained, 1)
                landed(dve, "gate_scores", c)
                then(nc.vector.tensor_reduce(g1, sc, AX.X, ALU.max))
                then(nc.vector.tensor_tensor(sc, sc, g1.unsqueeze(2).broadcast_to([P, CT, NE]), ALU.subtract))

            def gate_best(c):
                t = slice(CT * c, CT * c + CT)
                sc, g1, gt, ge, gr = score[:, t, :], gate1[:, t], gates[:, t, :], cmp_a[:, t, :], cmp_b[:, t, :]
                spread = g1.unsqueeze(2).broadcast_to([P, CT, NE])
                pairs = lambda v: v.rearrange("p t (i j) -> p t i j", i=NE)
                rank = lambda k: cb("rank")[:, NE * NE * k:NE * NE * (k + 1)].unsqueeze(1).broadcast_to(
                    [P, CT, NE * NE])
                dve.wait_ge(gate_exp_ready, MOE_CHUNKS.index(c) + 1)
                then(nc.vector.tensor_reduce(g1, sc, AX.X, ALU.add))
                then(nc.vector.reciprocal(g1, g1))
                then(nc.vector.tensor_tensor(sc, sc, spread, ALU.mult))
                of_j = sc.unsqueeze(2).broadcast_to([P, CT, NE, NE])
                of_i = sc.unsqueeze(3).broadcast_to([P, CT, NE, NE])
                nc.vector.tensor_tensor(pairs(ge), of_j, of_i, ALU.is_ge)
                then(nc.vector.tensor_tensor(pairs(gr), of_j, of_i, ALU.is_gt))
                nc.vector.tensor_tensor(ge, ge, rank(0), ALU.mult)
                then(nc.vector.tensor_tensor(gr, gr, rank(1), ALU.mult))
                then(nc.vector.tensor_tensor(ge, ge, gr, ALU.add))
                then(nc.vector.tensor_reduce(gt, pairs(ge), AX.X, ALU.add))
                then(nc.vector.tensor_scalar(gt, gt, 1.5, None, ALU.is_lt))
                then(nc.vector.tensor_tensor(gt, gt, sc, ALU.mult))
                then(nc.vector.tensor_reduce(g1, gt, AX.X, ALU.add))
                then(nc.vector.tensor_scalar(g1, g1, 1e-9, None, ALU.add))
                then(nc.vector.reciprocal(g1, g1))
                then(nc.vector.tensor_tensor(gt, gt, spread, ALU.mult))

            dve.wait_ge(v_pad_ready, 1)
            dve.wait_ge(l3_loaded, 16 * L3_DMAS)
            for what in ("q", "v"):
                qkv(what, 0)
            for s, hooks in stream():
                if s < STEPS:
                    k, n = uses["s", s]
                    dve.wait_ge(bank_filled[k], n + 1)
                    nc.vector.tensor_reduce(nmax[:, s % 3, 0:1], bank[k][:, 0:P], AX.X, ALU.max, negate=True)
                    nc.vector.tensor_reduce(nmax[:, s % 3, 1:2], bank[k][:, P:384], AX.X, ALU.max,
                                            negate=True).then_inc(nmax_ready, 1)
                i = s - 2
                if 0 <= i < STEPS and i % 2 == 0:
                    ps, drained = read_bank(dve, "pt", i)
                    nc.vector.tensor_copy(probs_t[:, i % 3, :], ps[:, 0:384]).then_inc(drained, 1)
                for what, *x in hooks:
                    if what in ("q", "k", "v"):
                        qkv(what, *x)
                    if what == "turn_o":
                        j, im = x
                        ps, drained = read_bank(dve, what, j, im)
                        v = ps[:, 0:HALVES * NH * 32].rearrange("p (n d) -> p n d", d=32)
                        t = slice(HALVES * im, HALVES * im + HALVES)
                        rec = o_rec[:, j % 2, t, :].rearrange("p t h -> p (t h)")
                        nc.vector.reciprocal(rec, v[:, :, HD]).then_inc(o_rec_ready, 1)
                        dve.wait_ge(o_rec_ready, IMGS * j + im + 1)
                        nc.vector.tensor_tensor(
                            o_norm[:, j % 2, t, :].rearrange("p t (h d) -> p (t h) d", d=HD), v[:, :, 0:HD],
                            rec.unsqueeze(2).broadcast_to([P, HALVES * NH, HD]), ALU.mult
                            ).then_inc(drained, 1)
                    if what == "proj":
                        j, = x
                        a, c = SLOTS[j]
                        ps, drained = read_bank(dve, "down", j)
                        if a == 1:
                            dve.wait_ge(bias_added, bias_no(A3, c))
                        v = X[:, CT * c:CT * c + CT, :]
                        nc.vector.tensor_tensor(v, ps[:, 0:C * CT].rearrange("p (t c) -> p t c", c=C), v,
                                                ALU.add).then_inc(drained, 1)
                        landed(dve, "down", j)
                    if what == "norm":
                        l, c = x
                        moments_of(l, c, x_tile(c), dict(chunks_of(l))[c])
                    if what == "scale":
                        l, c = x
                        scaled(l, c, x_tile(c), dict(chunks_of(l))[c])
                    if what == "qmax":
                        n, c = x
                        if n == 0:
                            for k in range(HT):
                                landed(dve, "qup", c, k)
                        else:
                            w = HALVES * len(images(c))
                            ps, drained = read_bank(dve, "qdown", c)
                            nc.vector.tensor_tensor(qy2[:, CT * c:CT * c + w, :],
                                                    ps[:, 0:C * w].rearrange("p (t c) -> p t c", c=C),
                                                    bias_row[F2][:, :].unsqueeze(1).broadcast_to([P, w, C]),
                                                    ALU.add).then_inc(drained, 1)
                            landed(dve, "qdown", c)
                        for im, b in enumerate(images(c)):
                            v = qy2[:, HALVES * b:HALVES * b + HALVES, :] if n else qy1[:, :, tok(HALVES * im, TOK)]
                            nc.vector.tensor_reduce(qmax[:, n, b:b + 1], v, AX.XY, ALU.max,
                                                    apply_absolute_value=True).then_inc(qmax_ready, 1)
                    if what == "gamma_max":
                        k, _ = gamma_no(*x)
                        w = len(images(x[1]))
                        ps, drained = read_bank(dve, what, *x)
                        nc.vector.tensor_reduce(qmax1[0:w, k:k + 1], ps[0:w, 0:P], AX.X, ALU.max).then_inc(drained, 1)
                        landed(dve, what, *x)
                        nc.vector.tensor_scalar(qmax1[0:w, k:k + 1], qmax1[0:w, k:k + 1], QEPS, None,
                                                ALU.add).then_inc(qchain, 1)
                        dve.wait_ge(qchain, 3 * k + 1)
                        nc.vector.reciprocal(qrec[0:w, k:k + 1], qmax1[0:w, k:k + 1]).then_inc(qchain, 1)
                        dve.wait_ge(qchain, 3 * k + 2)
                        nc.vector.tensor_scalar(qdiag[0:w, k, 0:w], ident[0:w, 0:w], qrec[0:w, k:k + 1], QB,
                                                ALU.mult, ALU.mult).then_inc(qchain, 1)
                    if what == "gamma_spread":
                        n, c = x
                        w = len(images(c))
                        ps, drained = read_bank(dve, what, n, c)
                        nc.vector.tensor_copy(qscale[:, n, IMGS * c:IMGS * c + w], ps[:, 0:w]).then_inc(drained, 1)
                        landed(dve, what, n, c)
                    if what == "clip":
                        n, c = x
                        for im, b in enumerate(images(c)):
                            scale = qscale[:, n, b:b + 1]
                            if n == 0:
                                v = qy1[:, :, tok(HALVES * im, TOK)]
                                nc.vector.tensor_scalar(v, v, scale, CLIP, ALU.mult, ALU.min).then_inc(qclip, 1)
                                dve.wait_ge(qclip, 2 * b + 1)
                                nc.vector.tensor_scalar(v, v, -CLIP, None, ALU.max).then_inc(qclip, 1)
                                continue
                            v, xt = (m[:, HALVES * b:HALVES * b + HALVES, :] for m in (qy2, X))
                            nc.vector.tensor_scalar(v, v, scale, CLIP, ALU.mult, ALU.min).then_inc(qclip2, 1)
                            dve.wait_ge(qclip2, 3 * b + 1)
                            nc.vector.tensor_scalar(v, v, -CLIP, None, ALU.max).then_inc(qclip2, 1)
                            dve.wait_ge(qclip2, 3 * b + 2)
                            nc.vector.tensor_tensor(xt, xt, v, ALU.add).then_inc(qclip2, 1)
                        if n:
                            dve.wait_ge(qclip2, 3 * images(c)[-1] + 3)
                    if what == "split_w":
                        e, = x
                        split(w_hi[:, e, :], w_lo[:, e, :], e_w1[:, e, :], w_split, e)
                    if what == "split_x":
                        m, = x
                        c = MOE_CHUNKS[m]
                        landed(dve, "turn", MO, c)
                        if m >= 2:
                            landed(dve, "eup", NE * (m - 1) - 1, HT - 1)
                        split(x_hi[:, m % 2, :], x_lo[:, m % 2, :], normed_t[MO % 2][:, ctok(c)], x_split, m)
                    if what == "gate_scores":
                        gate_scores(*x)
                    if what == "gate_best":
                        gate_best(*x)
                    if what == "edown":
                        i, = x
                        c, e = MOE_CHUNKS[i // NE], i % NE
                        xc = X[:, CT * c:CT * c + CT, :]
                        if e == NE - 1:
                            landed(dve, "edown", i - 1)
                            dve.wait_ge(bias_sum_step, BIAS_STEPS * (i // NE + 1))
                            nc.vector.tensor_tensor(xc, xc, bias_sum[:, CT * c:CT * c + CT, :], ALU.add
                                                    ).then_inc(bias_sum_added, 1)
                            dve.wait_ge(bias_sum_added, i // NE + 1)
                        ps, drained = read_bank(dve, what, i)
                        if 0 < e < NE - 1:
                            landed(dve, "edown", i - 1)
                        for t in range(CT):
                            n = CT * c + t
                            ins = nc.vector.scalar_tensor_tensor(X[:, n, :], ps[:, C * t:C * t + C],
                                                                 gates[:, n, e:e + 1], X[:, n, :],
                                                                 ALU.mult, ALU.add)
                        ins.then_inc(drained, 1)

        @block.gpsimd
        def _(pool):
            def add_bias(l, c):
                x = X[:, CT * c:CT * c + CT, :]
                nc.gpsimd.tensor_tensor(x, x, bias_row[l][:, :].unsqueeze(1).broadcast_to([P, CT, C]),
                                        ALU.add).then_inc(bias_added, 1)

            def rstd_of(l, c):
                w = dict(chunks_of(l))[c]
                pool.wait_ge(moments_ready, LN_NO[l, c])
                t = slice(CT * c, CT * c + w)
                nc.gpsimd.tensor_scalar(moments[:, l, t, 1], moments[:, l, t, 1], LN_EPS, None,
                                        ALU.add).then_inc(eps_added, 1)
                pool.wait_ge(eps_added, LN_NO[l, c])
                nc.gpsimd.tensor_tensor(rstd[:, l, t], moments[:, l, t, 1], exponent[:, 0:w],
                                        ALU.pow).then_inc(rstd_ready, 1)

            def bias_after(l, c):
                if l in BIASED and l != L0B:
                    pool.wait_ge(normed_ready, LN_NO[l, c])
                    add_bias(l, c)

            def value_columns():
                nc.gpsimd.memset(v_sb, 0.0).then_inc(v_zero, 1)
                pool.wait_ge(v_zero, 1)
                nc.gpsimd.memset(v_sb[:, :, :, HD:HD + 1], 1.0).then_inc(v_pad_ready, 1)

            def rstds(*norms):
                last = None
                for l, c in [k for k in LN_SEQ if k[0] in norms]:
                    rstd_of(l, c)
                    if last:
                        bias_after(*last)
                    last = l, c
                    if last == (L1A, CHUNKS - 1):
                        value_columns()
                bias_after(*last)

            nc.gpsimd.memset(exponent[:, :], -0.5)
            nc.gpsimd.memset(n1g[:, :], 0.0).then_inc(n1_zero, 1)
            nc.gpsimd.memset(n1b[:, :], 0.0).then_inc(n1_zero, 1)
            nc.gpsimd.memset(normed_s[:, :, GR:64], 0.0).then_inc(gap_zero, 1)
            rstds(L0A)
            pool.wait_ge(block_w_loaded[1], 16)
            pool.wait_ge(rstd_ready, CHUNKS)
            nc.gpsimd.tensor_scalar(spec_w[1][64:64 + GR, :, 0:BINS:2], spec_w[1][0:GR, :, 1:BINS:2], -1.0, None,
                                    ALU.mult).then_inc(spec_w_rows, 1)
            nc.gpsimd.tensor_copy(spec_w[1][64:64 + GR, :, 1:BINS:2], spec_w[1][0:GR, :, 0:BINS:2]
                                  ).then_inc(spec_w_rows, 1)
            pool.wait_ge(spec_w_rows, 4)
            nc.gpsimd.memset(ones[:, :], 1.0).then_inc(ones_ready, 1)
            nc.gpsimd.memset(sign1[:, QG * G1:HID], 0.0).then_inc(sign_ready, 1)
            nc.gpsimd.memset(sign2[:, :, QG * G2:C], 0.0).then_inc(sign_ready, 1)
            pool.wait_ge(const_b_loaded, 16)
            nc.gpsimd.tensor_copy(ident_b[:, :], ident).then_inc(bf_ready, 1)
            nc.gpsimd.tensor_copy(mask_b[:, :], cb("mask")).then_inc(bf_ready, 1)
            rstds(L0B)
            for k in range(2 * HALVES):
                landed(pool, "inv", k)
            pool.wait_ge(l0_loaded, 16 * L0_DMAS)
            for c in range(CHUNKS):
                x = X[:, CT * c:CT * c + CT, :]
                nc.gpsimd.tensor_tensor(x, x, xs[:, CT * c:CT * c + CT, :], ALU.add).then_inc(x_plus_xs, 1)
                pool.wait_ge(x_plus_xs, c + 1)
                add_bias(L0B, c)
            for v in pad:
                nc.gpsimd.memset(v, 0.0).then_inc(pad_zero, 1)
            pool.wait_ge(l1_loaded, 16 * L1_DMAS)
            for k in range(2):
                for n in range(PE_TAPS):
                    nc.gpsimd.tensor_scalar(tap_diag[:, k, n, :], ident, kcol[k][:, n:n + 1], None,
                                            ALU.mult).then_inc(diag_ready, 1)
            rstds(L1A, L1M, L1B, A2)
            pool.wait_ge(l3_loaded, 16 * L3_DMAS)
            for _, hooks in stream():
                for what, *x in hooks:
                    if what == "norm":
                        rstd_of(*x)
                    if what == "scale":
                        bias_after(*x)
                    if what == "gate_best":
                        c, = x
                        t, no = slice(CT * c, CT * c + CT), MOE_CHUNKS.index(c)
                        pool.wait_ge(gate_step, GATE_STEPS * (no + 1))
                        for e in range(NE):
                            dst = (bias_term if e else bias_sum)[:, t, :]
                            if e > 1:
                                pool.wait_ge(bias_sum_step, BIAS_STEPS * no + 2 * e - 1)
                            nc.gpsimd.tensor_tensor(dst, e_b2[:, e, :].unsqueeze(1).broadcast_to([P, CT, C]),
                                                    gates[:, t, e:e + 1].broadcast_to([P, CT, C]),
                                                    ALU.mult).then_inc(bias_sum_step, 1)
                            if e:
                                pool.wait_ge(bias_sum_step, BIAS_STEPS * no + 2 * e)
                                v = bias_sum[:, t, :]
                                nc.gpsimd.tensor_tensor(v, v, bias_term[:, t, :], ALU.add).then_inc(bias_sum_step, 1)


def constants():
    f = np.float64
    at_a, wa = spots(CONST_A)
    at_b, wb = spots(CONST_B)
    ca, cb = np.zeros((P, wa), f), np.zeros((P, wb), f)
    y, x = np.divmod(np.arange(TOK), WW)
    kh, kw = np.divmod(np.arange(POS), WF)
    angle = 2 * np.pi * (np.outer(y, kh) / HH + np.outer(x, kw) / WW)
    norm = TOK ** -0.5
    dft = np.concatenate([np.cos(angle), -np.sin(angle)], 1) * norm
    twice = np.where((kw == 0) | (kw == WW // 2), 1.0, 2.0)
    idft = np.stack([np.cos(angle) * twice * norm, -np.sin(angle) * twice * norm], 2).reshape(TOK, 2 * POS).T
    near = lambda d: 0.25 * 0.4 * 0.6 ** np.abs(d) * np.where(d == 0, 2.0, 1.0)
    dy, dx = y[:, None] - y[None, :], x[:, None] - x[None, :]
    mixer = np.eye(TOK) + near(dx) * (dy == 0) + near(dy) * (dx == 0)
    cut = lambda m, at, n: m[:, at[n][0]:at[n][1]]
    cut(ca, at_a, "ident")[:] = np.eye(P)
    for g in range(2):
        for n in range(GB):
            cut(ca, at_a, "nmask")[64 * g + BS * n:64 * g + BS * n + BS, n] = 1
    cut(ca, at_a, "dft")[:] = dft.reshape(HALVES, P, 2 * POS).transpose(1, 0, 2).reshape(P, -1)
    above = np.where(np.arange(P)[None, :] > np.arange(P)[:, None], NEG, 0.0)
    cut(cb, at_b, "mask")[:] = above
    for h in range(NH):
        cut(ca, at_a, "hmask")[HD * h:HD * h + HD, h] = HD ** -0.5
    i, j = np.divmod(np.arange(NE * NE), NE)
    cut(cb, at_b, "rank")[:] = np.concatenate([j < i, j > i])[None, :]
    cut(cb, at_b, "idft")[0:KROWS] = idft.reshape(KT, KROWS, TOK).transpose(1, 0, 2).reshape(KROWS, -1)
    cut(cb, at_b, "mix")[:] = mixer.reshape(HALVES, P, TOK).transpose(1, 0, 2).reshape(P, -1)
    rows = np.zeros((64 - GR, POS, GB, B), f)
    for n in range(GB):
        rows[n, :, n, :] = 1
    return {"const_a": ca.astype(np.float32), "const_b": cb.astype(np.float32),
            "const_rows": rows.reshape(64 - GR, -1).astype(np.float32)}


def kernel(**inputs):
    import concourse.bacc as bacc
    from concourse.bass_utils import run_bass_kernel_spmd

    nc = bacc.Bacc("TRN2", target_bir_lowering=False, num_devices=1)
    arrays, handles = {}, {}
    for name, value in {**inputs, **constants()}.items():
        v = np.ascontiguousarray(value)
        arrays[f"in_{name}"] = v
        handles[name] = nc.dram_tensor(f"in_{name}", v.shape, mybir.dt.from_np(v.dtype), kind="ExternalInput").ap()
    out = nc.dram_tensor("out_x", (B, HH, WW, C), F32, kind="ExternalOutput").ap()
    hybrid_kernel(nc, handles, out)
    return run_bass_kernel_spmd(nc, [arrays], core_ids=[0]).results[0]["out_x"]
```
